# Optimizing a Trainium2 kernel written in Bass

```python
import numpy as np
import jax
import jax.numpy as jnp

def _softmax(x, axis=-1):
    return jax.nn.softmax(x, axis=axis)

def _gelu(x):
    return jax.nn.gelu(x, approximate=True)

def _silu(x):
    return jax.nn.silu(x)

def _sigmoid(x):
    return jax.nn.sigmoid(x)

def _layernorm(x, axis=-1, eps=1e-05):
    m = jnp.mean(x, axis=axis, keepdims=True)
    v = jnp.var(x, axis=axis, keepdims=True)
    return (x - m) / jnp.sqrt(v + eps)

def _scatter_add(tgt, idx, src, axis=0):
    return tgt.at[idx].add(src)

def _segment_sum(src, seg, n):
    return jax.ops.segment_sum(src, seg, n)
kernel_name = 'mk_gps_d1_gnn_r32_e26d86'

def setup_inputs(seed: int=0):
    np.random.seed(seed)
    _w = jnp.asarray

    def _rec_inputs():
        import jax
        import jax.numpy as jnp
        _gk = jax.random.key(seed)
        x = -0.0003713 + 1 * jax.random.normal(jax.random.fold_in(_gk, 1), (3125, 256), jnp.float32)
        _s = jax.random.randint(jax.random.fold_in(_gk, 2), (25000,), 0, 3125, jnp.int32)
        _d = jax.random.randint(jax.random.fold_in(_gk, 3), (25000,), 0, 3125, jnp.int32)
        _loop = jnp.arange(3125, dtype=jnp.int32)
        src = jnp.concatenate([_s, _d, _loop])
        dst = jnp.concatenate([_d, _s, _loop])
        _o = jnp.argsort(dst, stable=True)
        src = src[_o]
        dst = dst[_o]
        return (x, src, dst)
    x, src, dst = _rec_inputs()

    def _L0_gnn_setup():
        import jax, jax.numpy as jnp
        import numpy as np
        N_NODES = 50000
        N_EDGES = 25000
        D_IN = 256
        D_HID = 256
        D_OUT = 256
        GAMMA = 0.0
        K_STEPS = 6

        def _spmm(h, src, dst, inv_deg):
            msg = h[src]
            agg = jax.ops.segment_sum(msg, dst, num_segments=h.shape[0])
            return agg * inv_deg[:, None]

        def _linear_diffusion(h, src, dst, gamma=GAMMA, k=K_STEPS):
            n = h.shape[0]
            deg = jax.ops.segment_sum(jnp.ones((src.shape[0],), h.dtype), dst, num_segments=n)
            inv_deg = 1.0 / jnp.clip(deg, 1.0)
            out = h
            term = h
            for i in range(1, k + 1):
                term = (_spmm(term, src, dst, inv_deg) + gamma * term) / float(i)
                out = out + term
            return out
        key = jax.random.key(seed)
        ks = jax.random.split(key, 8)
        h = jax.random.normal(ks[0], (N_NODES, D_IN), dtype=jnp.float32)
        src = jax.random.randint(ks[1], (N_EDGES,), 0, N_NODES, dtype=jnp.int64)
        dst = jax.random.randint(ks[2], (N_EDGES,), 0, N_NODES, dtype=jnp.int64)
        s_in = 1.0 / np.sqrt(D_IN)
        s_hid = 1.0 / np.sqrt(D_HID)
        W_in = jax.random.uniform(ks[3], (D_HID, D_IN), jnp.float32, -s_in, s_in)
        b_in = jax.random.uniform(ks[4], (D_HID,), jnp.float32, -s_in, s_in)
        W_out = jax.random.uniform(ks[5], (D_OUT, D_HID), jnp.float32, -s_hid, s_hid)
        b_out = jax.random.uniform(ks[6], (D_OUT,), jnp.float32, -s_hid, s_hid)
        return {'h': h, 'src': src, 'dst': dst, 'W_in': W_in, 'b_in': b_in, 'W_out': W_out, 'b_out': b_out}
    _L0_gnn_all = _L0_gnn_setup()
    _L0_gnn_in = {k: v for k, v in _L0_gnn_all.items() if k in ('W_in', 'b_in', 'W_out', 'b_out')}
    del _L0_gnn_all

    def _L0_mix_setup():
        import jax, jax.numpy as jnp
        import numpy as np
        MIDC = 256
        HEADS = 8
        HEADC = MIDC // HEADS
        EPS = 1e-05

        def _ln(x, gamma, beta):
            mu = jnp.mean(x, axis=-1, keepdims=True)
            var = jnp.var(x, axis=-1, keepdims=True)
            return (x - mu) * jax.lax.rsqrt(var + EPS) * gamma + beta
        key = jax.random.key(seed)
        ks = jax.random.split(key, 8)
        B, HW, C = (8, 128, MIDC)
        s = 1.0 / np.sqrt(C)
        return {'x': jax.random.normal(ks[0], (B, HW, C), jnp.float32), 'w_qkv': jax.random.normal(ks[1], (C, 3 * C), jnp.float32) * s, 'b_qkv': jnp.zeros((3 * C,), jnp.float32), 'kln_g': jnp.ones((HEADC,), jnp.float32), 'kln_b': jnp.zeros((HEADC,), jnp.float32), 'vln_g': jnp.ones((HEADC,), jnp.float32), 'vln_b': jnp.zeros((HEADC,), jnp.float32), 'w1': jax.random.normal(ks[2], (C, C), jnp.float32) * s, 'b1': jnp.zeros((C,), jnp.float32), 'w2': jax.random.normal(ks[3], (C, C), jnp.float32) * s, 'b2': jnp.zeros((C,), jnp.float32)}
    _L0_mix_all = _L0_mix_setup()
    _L0_mix_in = {k: v for k, v in _L0_mix_all.items() if k in ('w_qkv', 'b_qkv', 'kln_g', 'kln_b', 'vln_g', 'vln_b', 'w1', 'b1', 'w2', 'b2')}
    del _L0_mix_all

    def _L0_ffn_setup():
        import math
        import jax, jax.numpy as jnp
        import numpy as np
        CAPACITY_FACTOR = 1.25
        TOP_K = 2
        LN_EPS = 1e-05

        def _layer_norm(x, gamma, beta):
            mu = jnp.mean(x, axis=-1, keepdims=True)
            var = jnp.var(x, axis=-1, keepdims=True)
            return (x - mu) * jax.lax.rsqrt(var + LN_EPS) * gamma + beta
        key = jax.random.key(seed)
        ks = jax.random.split(key, 4)
        B, S, D, F, E = (8, 128, 256, 512, 8)
        x = jax.random.normal(ks[0], (B, S, D), dtype=jnp.float32)
        Wr = jax.random.normal(ks[1], (D, E), dtype=jnp.float32) / np.sqrt(D)
        br = jnp.zeros((E,), jnp.float32)
        W1 = jax.random.normal(ks[2], (E, D, F), dtype=jnp.float32) / np.sqrt(D)
        b1 = jnp.zeros((E, F), jnp.float32)
        W2 = jax.random.normal(ks[3], (E, F, D), dtype=jnp.float32) / np.sqrt(F)
        b2 = jnp.zeros((E, D), jnp.float32)
        gamma = jnp.ones((D,), jnp.float32)
        beta = jnp.zeros((D,), jnp.float32)
        return {'x': x, 'Wr': Wr, 'br': br, 'W1': W1, 'b1': b1, 'W2': W2, 'b2': b2, 'gamma': gamma, 'beta': beta}
    _L0_ffn_all = _L0_ffn_setup()
    _L0_ffn_in = {k: v for k, v in _L0_ffn_all.items() if k in ('Wr', 'br', 'W1', 'b1', 'W2', 'b2', 'gamma', 'beta')}
    del _L0_ffn_all
    return {'x': x, 'src': src, 'dst': dst, 'L0_gnn_W_in': _L0_gnn_in['W_in'], 'L0_gnn_b_in': _L0_gnn_in['b_in'], 'L0_gnn_W_out': _L0_gnn_in['W_out'], 'L0_gnn_b_out': _L0_gnn_in['b_out'], 'L0_mix_w_qkv': _L0_mix_in['w_qkv'], 'L0_mix_b_qkv': _L0_mix_in['b_qkv'], 'L0_mix_kln_g': _L0_mix_in['kln_g'], 'L0_mix_kln_b': _L0_mix_in['kln_b'], 'L0_mix_vln_g': _L0_mix_in['vln_g'], 'L0_mix_vln_b': _L0_mix_in['vln_b'], 'L0_mix_w1': _L0_mix_in['w1'], 'L0_mix_b1': _L0_mix_in['b1'], 'L0_mix_w2': _L0_mix_in['w2'], 'L0_mix_b2': _L0_mix_in['b2'], 'L0_ffn_Wr': _L0_ffn_in['Wr'], 'L0_ffn_br': _L0_ffn_in['br'], 'L0_ffn_W1': _L0_ffn_in['W1'], 'L0_ffn_b1': _L0_ffn_in['b1'], 'L0_ffn_W2': _L0_ffn_in['W2'], 'L0_ffn_b2': _L0_ffn_in['b2'], 'L0_ffn_gamma': _L0_ffn_in['gamma'], 'L0_ffn_beta': _L0_ffn_in['beta']}

def reference(x, src, dst, L0_gnn_W_in, L0_gnn_b_in, L0_gnn_W_out, L0_gnn_b_out, L0_mix_w_qkv, L0_mix_b_qkv, L0_mix_kln_g, L0_mix_kln_b, L0_mix_vln_g, L0_mix_vln_b, L0_mix_w1, L0_mix_b1, L0_mix_w2, L0_mix_b2, L0_ffn_Wr, L0_ffn_br, L0_ffn_W1, L0_ffn_b1, L0_ffn_W2, L0_ffn_b2, L0_ffn_gamma, L0_ffn_beta):
    import jax
    import jax.numpy as jnp

    def _L0_gnn_ref(h, src, dst, W_in, b_in, W_out, b_out):
        import jax, jax.numpy as jnp
        import numpy as np
        N_NODES = 50000
        N_EDGES = 25000
        D_IN = 256
        D_HID = 256
        D_OUT = 256
        GAMMA = 0.0
        K_STEPS = 6

        def _spmm(h, src, dst, inv_deg):
            msg = h[src]
            agg = jax.ops.segment_sum(msg, dst, num_segments=h.shape[0])
            return agg * inv_deg[:, None]

        def _linear_diffusion(h, src, dst, gamma=GAMMA, k=K_STEPS):
            n = h.shape[0]
            deg = jax.ops.segment_sum(jnp.ones((src.shape[0],), h.dtype), dst, num_segments=n)
            inv_deg = 1.0 / jnp.clip(deg, 1.0)
            out = h
            term = h
            for i in range(1, k + 1):
                term = (_spmm(term, src, dst, inv_deg) + gamma * term) / float(i)
                out = out + term
            return out
        x = h @ W_in.T + b_in
        x = jax.nn.silu(x)
        x = _linear_diffusion(x, src, dst)
        x = x @ W_out.T + b_out
        return x

    def _L0_mix_ref(x, w_qkv, b_qkv, kln_g, kln_b, vln_g, vln_b, w1, b1, w2, b2):
        import jax, jax.numpy as jnp
        import numpy as np
        MIDC = 256
        HEADS = 8
        HEADC = MIDC // HEADS
        EPS = 1e-05

        def _ln(x, gamma, beta):
            mu = jnp.mean(x, axis=-1, keepdims=True)
            var = jnp.var(x, axis=-1, keepdims=True)
            return (x - mu) * jax.lax.rsqrt(var + EPS) * gamma + beta
        B, HW, C = x.shape
        bias = x
        qkv = (x @ w_qkv + b_qkv).reshape(B, HW, HEADS, 3 * HEADC)
        qkv = qkv.transpose(0, 2, 1, 3)
        q, k, v = jnp.split(qkv, 3, axis=-1)
        k = _ln(k, kln_g, kln_b)
        v = _ln(v, vln_g, vln_b)
        kv = jnp.einsum('bhnd,bhne->bhde', k, v) / HW
        out = jnp.einsum('bhnd,bhde->bhne', q, kv)
        out = out.transpose(0, 2, 1, 3).reshape(B, HW, C)
        ret = out + bias
        h = jax.nn.gelu(ret @ w1 + b1, approximate=False)
        return h @ w2 + b2 + bias

    def _L0_ffn_ref(x, Wr, br, W1, b1, W2, b2, gamma, beta):
        import math
        import jax, jax.numpy as jnp
        import numpy as np
        CAPACITY_FACTOR = 1.25
        TOP_K = 2
        LN_EPS = 1e-05

        def _layer_norm(x, gamma, beta):
            mu = jnp.mean(x, axis=-1, keepdims=True)
            var = jnp.var(x, axis=-1, keepdims=True)
            return (x - mu) * jax.lax.rsqrt(var + LN_EPS) * gamma + beta
        B, S, D = x.shape
        E = Wr.shape[1]
        N = B * S
        K = TOP_K
        logits = jnp.mean(x, axis=1) @ Wr + br
        routing_weights = jax.nn.softmax(logits, axis=-1)
        capacity = float(math.ceil(N * CAPACITY_FACTOR / E))
        expected_loads = routing_weights.sum(axis=0) * (N / B)
        scale = jnp.where(expected_loads > capacity, capacity / expected_loads, 1.0)
        routing_weights = jax.nn.softmax(routing_weights * scale, axis=-1)
        rw_tok = jnp.broadcast_to(routing_weights[:, None, :], (B, S, E)).reshape(N, E)
        top_w, top_i = jax.lax.top_k(rw_tok, K)
        top_w = jax.nn.softmax(top_w, axis=-1)
        xf = x.reshape(N, D)
        h = jax.nn.gelu(jnp.einsum('nd,edf->enf', xf, W1) + b1[:, None, :], approximate=False)
        y = jnp.einsum('enf,efd->end', h, W2) + b2[:, None, :]
        w_dense = jnp.zeros((N, E), x.dtype).at[jnp.arange(N)[:, None], top_i].add(top_w)
        out = jnp.einsum('ne,end->nd', w_dense, y).reshape(B, S, D)
        out = _layer_norm(out + x, gamma, beta)
        return out
    xn = _layernorm(x, axis=-1)
    x = x + _L0_gnn_ref(xn, src, dst, L0_gnn_W_in, L0_gnn_b_in, L0_gnn_W_out, L0_gnn_b_out) + _L0_mix_ref(xn[None], L0_mix_w_qkv, L0_mix_b_qkv, L0_mix_kln_g, L0_mix_kln_b, L0_mix_vln_g, L0_mix_vln_b, L0_mix_w1, L0_mix_b1, L0_mix_w2, L0_mix_b2)[0]
    x = x + _L0_ffn_ref(_layernorm(x, axis=-1)[None], L0_ffn_Wr, L0_ffn_br, L0_ffn_W1, L0_ffn_b1, L0_ffn_W2, L0_ffn_b2, L0_ffn_gamma, L0_ffn_beta)[0]
    return x

_drawn_inputs = setup_inputs


def setup_inputs(seed=0):
    import zlib

    import numpy as np

    out = dict(_drawn_inputs(seed))
    spreads = {'L0_mix_b_qkv': (0.0, 0.1),
     'L0_mix_kln_g': (1.0, 0.6),
     'L0_mix_kln_b': (0.0, 0.448),
     'L0_mix_vln_g': (1.0, 0.585),
     'L0_mix_vln_b': (0.0, 0.397),
     'L0_mix_b1': (0.0, 0.267),
     'L0_mix_b2': (0.0, 0.1),
     'L0_ffn_br': (0.0, 0.8),
     'L0_ffn_b1': (0.0, 0.557),
     'L0_ffn_b2': (0.0, 0.361),
     'L0_ffn_gamma': (1.0, 0.2),
     'L0_ffn_beta': (0.0, 0.1)}
    factors = {'L0_gnn_b_in': 4.155, 'L0_gnn_b_out': 3.228}
    for name, (base, spread) in spreads.items():
        noise = np.random.default_rng([zlib.crc32(name.encode()), seed]).standard_normal(out[name].shape)
        drawn = base * np.exp(spread * noise) if base else spread * noise
        out[name] = jnp.asarray(drawn.astype(out[name].dtype))
    for name, factor in factors.items():
        out[name] = (out[name] * factor).astype(out[name].dtype)
    return out
```

```python
import numpy as np

import concourse.bass as bass
from concourse import mybir
from contextlib import ExitStack

F32, F16, I32 = mybir.dt.float32, mybir.dt.float16, mybir.dt.int32
U8, F8 = mybir.dt.uint8, mybir.dt.float8e4
ACT, ALU, AX = mybir.ActivationFunctionType, mybir.AluOpType, mybir.AxisListType

N, D, E = 3125, 256, 53125
P = 125
T = N // P
R = 5
ROUNDS = T // R
KC = D // 128
HEADS, HD = 8, 32
STEPS = 6
EPS = 1e-5
NX, FF = 8, 512
FM = FF // 128
CAP = float(-(-(N * 125) // (NX * 100)))

GD = 5
G = N // GD
GT = G // P
GPT = P // GD
W = 128
AL = 8
EC = 416
ECH = EC + W - AL
NS = EC // AL
PAD = 4095
LASTP = E - 127 * EC
FULLP = (E - ECH) // EC + 1
BATCHES = [3] * 7 + [4]
NB = len(BATCHES)
SR = 4
N_WEIGHTS = 16
MAGIC = 12582912.0
CHUNK = 4
CW = CHUNK * P

C_ID, C_MASK, C_IOTA, C_GRP, C_NODE, C_END = np.cumsum([0, 128, 128, 128, G, N]).tolist()


def constants():
    c = np.zeros((128, C_END), np.float32)
    c[:, C_ID:C_MASK] = np.eye(128)
    c[:, C_MASK:C_IOTA] = np.kron(np.eye(4), np.ones((32, 32)))
    c[:, C_IOTA:C_GRP] = np.arange(128)
    c[:, C_GRP:C_NODE] = np.arange(G)
    c[:, C_NODE:C_END] = np.arange(N)
    return c


class Links:

    def __init__(self, eng, sem, base=0):
        self.eng, self.sem, self.base, self.n = eng, sem, base, 0

    def __call__(self, ins):
        self.n += 1
        ins.then_inc(self.sem, 1)
        self.eng.wait_ge(self.sem, self.base + self.n)


def gps_kernel(nc, a, out):
    ctx = ExitStack()
    with ctx:
        def sb(name, shape, dt=F32):
            return ctx.enter_context(nc.sbuf_tensor(name, shape, dt))

        def dram(name, shape, dt=F32):
            return nc.dram_tensor(name, shape, dt, kind="Internal").ap()

        def sem(name):
            return ctx.enter_context(nc.semaphore(name))

        windows = dram("windows", (128 * NS, W))
        counts = dram("counts", (T, P, T * 128), U8)
        term_dram = dram("term_dram", (N, D))

        cst = sb("cst", [128, C_NODE])
        grp = cst[:, C_GRP:C_NODE]
        ident, mask = cst[:, C_ID:C_MASK], cst[:, C_MASK:C_IOTA]
        x1 = sb("x1", [P, T, D])
        acc = sb("acc", [P, T, D])
        xt_all = sb("xt_all", [128, KC, N])
        big = sb("big", [128, 2 * T * D])
        kc_all = big[0:P, :].rearrange("p (t f) -> p t f", t=T)
        u = [big[0:P, s * T * D:(s + 1) * T * D].bitcast(F16).rearrange("p (t f) -> p t f", t=T)
             for s in range(2)]
        w_in = sb("w_in", [128, KC, D])
        w_out = sb("w_out", [128, KC, D])
        wq_t = sb("wq_t", [128, KC, D + 1])
        w_kv = sb("w_kv", [128, KC + 1, 2 * D])
        w1 = sb("w1", [128, KC, D])
        w2 = sb("w2", [128, KC, D])
        wr = sb("wr", [128, KC, NX])
        b_in = sb("b_in", [P, D])
        b_add = sb("b_add", [P, 2, D])
        gam = sb("gam", [P, 2, D])
        lnrow = sb("lnrow", [128, 2, D])
        lncol = sb("lncol", [128, 2])
        b1c = sb("b1c", [128, KC])
        br = sb("br", [1, NX])
        ones = sb("ones", [128, 128])
        ones16 = sb("ones16", [128, 1], F16)
        iota16 = sb("iota16", [128, 128], F16)
        st = sb("st", [P, T, 6])
        mean, rstd, nmr, lnt = (sb(n, [P, T]) for n in ("mean", "rstd", "nmr", "lnt"))
        lnu = sb("lnu", [P, T])
        deg = sb("deg", [128, T])
        scale2 = sb("scale2", [128, 2])
        coef = sb("coef", [128, STEPS])
        invf = sb("invf", [128, STEPS])
        zeros = sb("zeros", [1, 512])
        wsum = sb("wsum", [128, (KC + 1) * 2 * HEADS])
        kvar = sb("kvar", [P, T * 2 * HEADS])
        hmx = sb("hmx", [P, T + 1])
        small = sb("small", [1, 64])
        small_i = sb("small_i", [1, 16], I32)
        idx_u = sb("idx_u", [1, 8], mybir.dt.uint32)
        g_sb = sb("g_sb", [128, KC, D])
        bias1 = sb("bias1", [128, KC])
        fl = sb("fl", [P, 2])
        REGION = 12000
        region = sb("region", [128, REGION])

        def view(at, words, dt=F32, parts=128):
            assert at + words <= REGION
            v = region[0:parts, at:at + words]
            return v if dt == F32 else v.bitcast(dt)

        eq = view(0, 2 * G).rearrange("p (a g) -> p a g", a=2)
        cur = view(2 * G, R * 2 * GPT).rearrange("p (r a g) -> p r a g", r=R, a=2)
        OH = 2 * G + R * 2 * GPT
        got = view(OH, GT * W, F32, P).rearrange("p (t e) -> p t e", t=GT)
        start_i = view(OH + GT * W, GT, I32, P)
        at = OH + GT * W + 8
        di, si, code = view(at, ECH, I32), view(at + ECH, ECH, I32), view(at + 2 * ECH, ECH)
        gds = view(at + 3 * ECH, 2 * NS).rearrange("p (a s) -> p a s", a=2)
        grp16 = view(at + 3 * ECH + 2 * NS, 320, F16)[:, 0:G]
        cmp = view(at + 3 * ECH + 2 * NS + 320, SR * 320, F16).rearrange("p (r g) -> p r g", r=SR)[:, :, 0:G]
        e_int = view(at, 3 * G, I32).rearrange("p (a g) -> p a g", a=3)
        e_f = view(at + 3 * G, 4 * G).rearrange("p (a g) -> p a g", a=4)
        oh_d = view(OH, GPT * 64, F16).rearrange("p (g m) -> p g m", m=128)
        oh_q = view(OH + GPT * 64, GPT * 64, F16).rearrange("p (g m) -> p g m", m=128)
        STAGE = OH + 2 * GPT * 64
        stage = view(STAGE, R * T * 32, U8).rearrange("p (r m) -> p r m", r=R)
        TOK = STAGE + R * T * 32
        xn = view(TOK, R * D, F32, P).rearrange("p (r f) -> p r f", r=R)
        xt = view(TOK + R * D, R * KC * P).rearrange("p (r k m) -> p r k m", r=R, k=KC)
        h_pre = view(TOK + R * D + R * KC * P, D, F32, P)
        sq = view(TOK + R * D + R * KC * P + D, 2 * D, F32, P)
        pool_t = b_add[:, 1, :]
        kvn = view(OH, R * 2 * D, F32, P).rearrange("p (r f) -> p r f", r=R)
        hb = view(TOK, KC * R * P).rearrange("p (k m) -> p k m", k=KC)
        lo_part = view(OH, R * D, F32, P).rearrange("p (r f) -> p r f", r=R)
        u_sum = view(OH + R * D, R * D, F32, P).rearrange("p (r f) -> p r f", r=R)
        orr = view(TOK, T * 32, I32, P)
        at = TOK
        kvs = view(at, 3 * 128).rearrange("p (a f) -> p a f", a=3)
        kv_bd = view(at + 384, KC * 128).rearrange("p (k f) -> p k f", k=KC)
        m1t = view(at + 640, KC * (D + 1)).rearrange("p (k f) -> p k f", k=KC)
        kstd = view(TOK + R * D + R * KC * P, T * 2 * HEADS, F32, P)
        at_in = view(TOK, R * D, F32, P).rearrange("p (r f) -> p r f", r=R)
        at_t = view(TOK + R * D, R * KC * P).rearrange("p (r k m) -> p r k m", r=R, k=KC)
        y_in = view(OH, R * D, F32, P).rearrange("p (r f) -> p r f", r=R)
        hid = big[:, 0:2 * FM * R * P].rearrange("p (e m t) -> p e m t", e=2, m=FM)
        o1 = 2 * FM * R * P
        w1e = big[:, o1:o1 + 2 * KC * FF].rearrange("p (e k f) -> p e k f", e=2, k=KC)
        w2e = big[:, o1 + 2 * KC * FF:o1 + 2 * KC * FF + 2 * FM * D].rearrange("p (e m f) -> p e m f", e=2, m=FM)
        b1e = view(0, 2 * FM).rearrange("p (e m) -> p e m", e=2)
        b2e = view(16, 2 * D, F32, P).rearrange("p (e f) -> p e f", e=2)
        topw = view(16 + 2 * D, 2)
        meant = view(20 + 2 * D, KC)
        yb = view(OH + R * D, R * D, F32, P).rearrange("p (r f) -> p r f", r=R)
        fin = view(STAGE, R * D, F32, P).rearrange("p (r f) -> p r f", r=R)
        x1b = view(STAGE + R * D, R * D, F32, P).rearrange("p (r f) -> p r f", r=R)
        node_row = big[0:P, 0:N]
        oh_g = big[0:P, N:2 * N]
        sums = big[0:P, 2 * N:2 * N + T * (D + 1)].rearrange("p (t f) -> p t f", t=T)
        EP = E // P
        src_all = view(OH, EP, I32, P)
        dst_all = view(OH + EP, EP, I32, P)
        dst_f = view(OH + 2 * EP, EP, F32, P)
        idx_g = view(OH + 3 * EP, 1, I32, P)
        rdeg = view(OH + 3 * EP + 8, T, F32, P)
        rows = view(OH + 3 * EP + 40, D + 1, F32, P)

        ps = ctx.enter_context(nc.psum_tensor("ps", [128, 8, 512], F32))

        def banks(b, n=1):
            return ps[:, b:b + n, :].rearrange("p b c -> p (b c)")

        names = {}

        def sems(*each):
            for n in each:
                names[n] = sem(n)

        sems("waited", "const_in", "pad_set", "edges_in", "x_in", "weights_in", "kvw_in",
             "ones_set", "code_ready", "windows_out", "cmp_ready", "cmp_used", "start_ready",
             "got_in", "code_turned", "dve_edge", "eq_ready", "stage_clear", "zero_set",
             "stats", "var_ready", "std_ready", "dve_norm", "norm_ready", "wkv_ready", "dve_w",
             "cur_ready", "ohd_ready", "ohq_ready", "batch_done", "batch_out", "deg_done",
             "xn_ready", "turned", "xt_ready", "xt_kept", "h_done", "kv_done", "h_biased", "kc_ready",
             "silu_done", "sq_ready", "sq_used", "pool_sum", "x1_bias", "h_kept",
             "kvar_ready", "kstd_ready", "rk_ready", "kvn_ready", "kv_summed", "dve_kv", "kvbd_ready",
             "m1_done", "m1_ready", "g_done", "g_ready", "hmax_ready", "hmax_turned", "dve_scale",
             "scale_ready", "scale_spread", "scale_kept", "mix_done", "gelu_done", "w2_done", "x1_mixed",
             "high_ready", "split_ready", "deg_ready", "deg_kept", "gen_batch", "gen_added", "stats2", "x1_stats",
             "tile_done", "low_part", "sum_ready", "high_kept", "or_done", "acc_done",
             "flag_part", "flag_sum", "flag_ready", "dve_flag",
             "gen_init", "gen_idx", "gen_rows", "gen_got", "gen_onehot", "gen_mm", "gen_add",
             "gen_dve", "gen_step", "gen_stored", "gen_end",
             "acc_in", "acc_turned", "at_ready", "out_done", "x1_ready", "y_ready", "y_kept", "y_turned",
             "yt_ready", "mean_done", "mean_ready", "logits_done", "dve_route", "exp_in", "exp_out",
             "route_ready", "route_spread", "top_ready", "experts_in", "w2_scaled", "b2_ready",
             "hid_done", "hid_ready", "ffn_done", "yb_ready", "r_ready", "var2_ready", "std2_ready",
             "dve_out", "norm2_ready", "fin_ready", "x1b_ready", "out_ready")
        S = names
        slot_out = [sem(f"slot_out{j}") for j in range(R)]
        slot_in = [sem(f"slot_in{j}") for j in range(R)]
        out_in = [sem(f"out_in{j}") for j in range(R)]

        block = ctx.enter_context(nc.Block())
        rounds_view = lambda ap: ap.rearrange("(t p) f -> p t f", p=P)
        x_v, out_v, term_v = rounds_view(a["x"]), rounds_view(out), rounds_view(term_dram)

        def row(ap, parts, n):
            return bass.AP(ap.tensor, 0, [[0, parts], [1, n]])

        def apart(eng):
            eng.sem_inc(S["waited"], 1)

        @block.sync
        def _(sp):
            for j in range(R):
                sp.sem_inc(slot_out[j], 16)
                sp.sem_inc(out_in[j], 16)
            sp.dma_start(cst[:, :], a["const"][:, 0:C_NODE]).then_inc(S["const_in"], 16)
            sp.wait_ge(S["pad_set"], 2)
            for lst, name in ((di, "dst"), (si, "src")):
                src = a[name]
                sp.dma_start(lst[0:FULLP, :], bass.AP(src.tensor, 0, [[EC, FULLP], [1, ECH]])).then_inc(S["edges_in"], 16)
                for p in range(FULLP, 128):
                    n = E - EC * p
                    sp.dma_start(lst[p:p + 1, 0:n], bass.AP(src.tensor, EC * p, [[n, 1], [1, n]])).then_inc(S["edges_in"], 16)
            for r in range(ROUNDS):
                sp.dma_start(x1[:, R * r:R * r + R, :], x_v[:, R * r:R * r + R, :]).then_inc(S["x_in"], 16)
            sp.wait_ge(S["code_ready"], 1)
            c0 = code[:, :]
            sp.dma_start(windows.rearrange("(p s) e -> p s e", p=128),
                         bass.AP(c0.tensor, c0.offset, [list(c0.ap[0]), [AL, NS], [1, W]])).then_inc(S["windows_out"], 16)

            def store(i, j):
                sp.wait_ge(S["batch_out"], 4 + NB * R * i + NB * (j + 1))
                sp.dma_start(counts[bass.ds(R * i + j, 1), :, :].rearrange("o p m -> p (o m)"),
                             stage[0:P, j, :]).then_inc(slot_out[j], 16)

            with sp.Fori(0, ROUNDS) as i:
                for j in range(R):
                    store(i, j)
            sp.wait_ge(S["silu_done"], 1 + T)
            sp.dma_start(term_v, acc[:, :, :]).then_inc(S["h_kept"], 16)

            for j in range(R):
                sp.wait_ge(slot_out[j], 16 + 16 * ROUNDS)
            sp.wait_ge(S["deg_done"], R + T)
            with sp.Fori(0, STEPS) as k:
                with sp.Fori(0, ROUNDS) as i:
                    for j in range(R):
                        sp.wait_ge(S["tile_done"], T * k + R * i + j + 1)
                        sp.wait_ge(S["or_done"], T * k + R * i + j + 1)
                        apart(sp)
                        sp.dma_start(stage[0:P, j, :],
                                     counts[bass.ds(R * i + j, 1), :, :].rearrange("o p m -> p (o m)")).then_inc(slot_in[j], 16)

            sp.wait_ge(S["flag_ready"], 1)
            bad = sp.value_load(small_i[0:1, 0:1], min_val=0, max_val=1)
            with sp.If(bad == 1):
                sp.dma_start(src_all, a["src"].rearrange("(p e) -> p e", p=P)).then_inc(S["gen_init"], 16)
                sp.dma_start(dst_all, a["dst"].rearrange("(p e) -> p e", p=P)).then_inc(S["gen_init"], 16)
                sp.dma_start(node_row, a["const"][0:P, C_NODE:C_END]).then_inc(S["gen_init"], 16)
                sp.wait_ge(S["h_kept"], 16)
                sp.dma_start(acc[:, :, :], term_v).then_inc(S["gen_init"], 16)
                with sp.Fori(0, STEPS) as k:
                    sp.wait_ge(S["gen_step"], k + 1)
                    sp.dma_start(term_v, sums[:, :, 0:D]).then_inc(S["gen_stored"], 16)
                sp.wait_ge(S["gen_stored"], 16 * STEPS)
            with sp.Else():
                pass

            sp.wait_ge(S["route_ready"], 1)
            sp.wait_ge(S["gen_end"], 1)
            for e in range(2):
                x = sp.value_load(small_i[0:1, 2 + e:3 + e], min_val=0, max_val=NX - 1)
                sp.dma_start(w1e[:, e, :, :], a["e_w1"][bass.ds(x, 1), :, :, :].rearrange("o k p f -> p (o k) f")).then_inc(S["experts_in"], 16)
                sp.dma_start(b1e[:, e, :], a["e_b1"][bass.ds(x, 1), :, :].rearrange("o p m -> p (o m)")).then_inc(S["experts_in"], 16)
                sp.dma_start(w2e[:, e, :, :], a["e_w2"][bass.ds(x, 1), :, :, :].rearrange("o k p f -> p (o k) f")).then_inc(S["experts_in"], 16)
                sp.dma_start(b2e[:, e, :], a["e_b2"][bass.ds(x, 1), :].to_broadcast([P, D])).then_inc(S["experts_in"], 16)

            with sp.Fori(0, ROUNDS) as i:
                for j in range(R):
                    sp.wait_ge(S["out_ready"], R + R * i + j + 1)
                    sp.dma_start(out_v[:, bass.ds(R * i + j, 1), :].rearrange("p o f -> p (o f)"),
                                 fin[:, j, :]).then_inc(out_in[j], 16)
            for j in range(R):
                sp.wait_ge(out_in[j], 16 + 16 * ROUNDS)
            sp.wait_ge(S["h_kept"], 16)

        @block.gpsimd
        def _(pool):
            pool.memset(di[:, :], PAD).then_inc(S["pad_set"], 1)
            pool.memset(si[:, :], 0).then_inc(S["pad_set"], 1)
            for k in range(STEPS):
                f = float(np.prod(np.arange(1, k + 2)))
                pool.memset(invf[:, k:k + 1], 1.0 / f).then_inc(S["pad_set"], 1)
            pool.sem_inc(S["ohd_ready"], NB * R)
            pool.sem_inc(S["xt_kept"], R)
            pool.sem_inc(S["y_kept"], R)
            pool.sem_inc(S["x1_bias"], 1)
            pool.wait_ge(S["start_ready"], 1)
            pool.wait_ge(S["windows_out"], 16)
            for t in range(GT):
                pool.indirect_dma_start(got[:, t, :], None, windows[:, :],
                                        bass.IndirectOffsetOnAxis(ap=start_i[:, t:t + 1], axis=0)).then_inc(S["got_in"], 16)
            pool.wait_ge(S["weights_in"], 16 * N_WEIGHTS)
            b_sum = b_add[:, 0, :]
            pool.tensor_tensor(b_sum, b_add[:, 0, :], b_add[:, 1, :], ALU.add).then_inc(S["pool_sum"], 1)
            pool.wait_ge(S["pool_sum"], 1)

            with pool.Fori(0, ROUNDS) as i:
                for j in range(R):
                    n = R * i + j
                    pool.wait_ge(S["cur_ready"], n + 1)
                    g = 0
                    for b, size in enumerate(BATCHES):
                        pool.wait_ge(S["batch_done"], NB * n + b + 1)
                        apart(pool)
                        for s in range(size):
                            ins = pool.tensor_scalar(oh_d[:, g, :], iota16[:, :], cur[:, j, 1, g:g + 1], None, ALU.is_equal)
                            g += 1
                        ins.then_inc(S["ohd_ready"], 1)
                        if b == 3:
                            pool.wait_ge(S["xn_ready"], n + 1)
                            pool.wait_ge(S["x1_bias"], n + 1)
                            pool.tensor_tensor(pool_t, xn[:, j, :], b_sum, ALU.add).then_inc(S["pool_sum"], 1)
                            pool.wait_ge(S["pool_sum"], n + 2)
                            xr = x1[:, bass.ds(n, 1), :].rearrange("p o f -> p (o f)")
                            pool.tensor_tensor(xr, xr, pool_t, ALU.add).then_inc(S["x1_bias"], 1)
                            pool.wait_ge(S["xt_ready"], 1 + n + 1)
                            pool.tensor_copy(xt_all[:, :, bass.ds(P * n, P)], xt[:, j, :, :]).then_inc(S["xt_kept"], 1)

            pool.wait_ge(S["flag_ready"], 1)
            bad = pool.value_load(small_i[0:1, 0:1], min_val=0, max_val=1)
            with pool.If(bad == 1):
                pool.wait_ge(S["gen_init"], 64)
                with pool.Fori(0, STEPS) as k:
                    pool.wait_ge(S["gen_dve"], k + 1)
                    apart(pool)
                    with pool.Fori(0, EP) as e:
                        n = EP * k + e
                        pool.wait_ge(S["gen_mm"], n + 1)
                        pool.tensor_copy(idx_g, src_all[:, bass.ds(e, 1)]).then_inc(S["gen_idx"], 1)
                        pool.wait_ge(S["gen_idx"], n + 1)
                        apart(pool)
                        pool.indirect_dma_start(rows[:, 0:D], None, term_dram[:, :],
                                                bass.IndirectOffsetOnAxis(ap=idx_g, axis=0)).then_inc(S["gen_rows"], 16)
                        pool.wait_ge(S["gen_rows"], 16)
                        pool.sem_clear(S["gen_rows"])
                        pool.sem_inc(S["gen_got"], 1)
            with pool.Else():
                pass

            with pool.Fori(0, ROUNDS) as i:
                for j in range(R):
                    n = R * i + j
                    pool.wait_ge(S["y_ready"], n + 1)
                    pool.tensor_copy(acc[:, bass.ds(n, 1), :].rearrange("p o f -> p (o f)"), y_in[:, j, :]).then_inc(S["y_kept"], 1)
            with pool.Fori(0, ROUNDS) as i:
                for j in range(R):
                    n = R * i + j
                    if j == 0:
                        pool.wait_ge(S["b2_ready"], 1)
                    pool.wait_ge(S["out_ready"], n + 1)
                    pool.tensor_tensor(yb[:, j, :], acc[:, bass.ds(n, 1), :].rearrange("p o f -> p (o f)"),
                                       b2e[:, 0, :], ALU.add).then_inc(S["yb_ready"], 1)
                    pool.tensor_tensor(x1b[:, j, :], x1[:, bass.ds(n, 1), :].rearrange("p o f -> p (o f)"),
                                       gam[:, 1, :], ALU.add).then_inc(S["x1b_ready"], 1)

        @block.scalar
        def _(act):
            loads = 0
            act.dma_start(w_kv[:, 0:KC, :], a["w_kv"].rearrange("(k p) f -> p k f", p=128)).then_inc(S["kvw_in"], 16)
            act.dma_start(w_kv[:, KC, :], row(a["b_kv"], 128, 2 * D)).then_inc(S["kvw_in"], 16)
            for dst, src in ((w_in[:, :, :], a["w_in_t"].rearrange("(k p) f -> p k f", p=128)),
                             (b_in[:, :], row(a["b_in"], P, D)),
                             (b_add[:, 0, :], row(a["b_out"], P, D)),
                             (b_add[:, 1, :], row(a["b2"], P, D)),
                             (wq_t[:, :, :], a["w_q_t"].rearrange("(k p) f -> p k f", p=128)),
                             (w1[:, :, :], a["w1"].rearrange("(k p) f -> p k f", p=128)),
                             (b1c[:, :], a["b1"]),
                             (lnrow[:, 0, :], row(a["vln_g"], 128, D)),
                             (lnrow[:, 1, :], row(a["vln_b"], 128, D)),
                             (lncol[:, :], a["kln"]),
                             (w2[:, :, :], a["w2"].rearrange("(k p) f -> p k f", p=128)),
                             (w_out[:, :, :], a["w_out_t"].rearrange("(k p) f -> p k f", p=128)),
                             (wr[:, :, :], a["wr"].rearrange("(k p) f -> p k f", p=128)),
                             (br[:, :], row(a["br"], 1, NX)),
                             (gam[:, 0, :], row(a["gamma"], P, D)),
                             (gam[:, 1, :], row(a["beta"], P, D))):
                act.dma_start(dst, src).then_inc(S["weights_in"], 16)
                loads += 1
            assert loads == N_WEIGHTS
            act.sem_inc(S["xt_ready"], 1)
            act.sem_inc(S["silu_done"], 1)
            act.sem_inc(S["deg_kept"], 1)
            act.sem_inc(S["batch_out"], 4)
            act.sem_inc(S["gelu_done"], KC)
            act.sem_inc(S["at_ready"], 1)
            act.sem_inc(S["hid_ready"], 2)
            act.wait_ge(S["var_ready"], 1)
            act.activation(lnu[:, :], lnt[:, :], ACT.Sqrt).then_inc(S["std_ready"], 1)

            with act.Fori(0, ROUNDS) as i:
                for j in range(R):
                    n = R * i + j
                    act.wait_ge(S["turned"], n + 1)
                    act.wait_ge(S["xt_kept"], n + 1)
                    act.activation(xt[:, j, :, :], banks(0)[:, 0:256].rearrange("p (k m) -> p k m", k=KC)[:, :, 0:P],
                                   ACT.Copy).then_inc(S["xt_ready"], 1)
                    g = 0
                    for b, size in enumerate(BATCHES):
                        if b == 0:
                            act.wait_ge(slot_out[j], 16 * i + 16)
                            act.wait_ge(S["deg_done"], n + 1)
                            act.wait_ge(S["stage_clear"], 1)
                        act.wait_ge(S["batch_done"], NB + NB * n + b + 1)
                        apart(act)
                        to = stage[0:P, j, :].bitcast(F8).rearrange("p (c m) -> p c m", c=T)
                        act.activation(to[:, :, GD * g:GD * (g + size)].rearrange("p c (s l) -> p s c l", l=GD),
                                       banks(4 + b % 4)[0:P, 0:size * P].rearrange("p (s c l) -> p s c l", s=size, l=GD),
                                       ACT.Copy, scale=0.125, saturate=False).then_inc(S["batch_out"], 1)
                        g += size
                        if b == 5:
                            act.wait_ge(S["h_biased"], 1 + n + 1)
                            act.activation(acc[:, bass.ds(n, 1), :].rearrange("p o f -> p (o f)"), h_pre[:, :],
                                           ACT.Silu).then_inc(S["silu_done"], 1)
                            act.wait_ge(S["kc_ready"], 1 + n + 1)
                            act.wait_ge(S["sq_used"], n + 1)
                            act.activation(sq[:, :], kc_all[:, bass.ds(n, 1), :].rearrange("p o f -> p (o f)"),
                                           ACT.Square).then_inc(S["sq_ready"], 1)
                act.wait_ge(S["deg_done"], R + R * i + R)
                act.activation(deg[:, bass.ds(R * i, R)], banks(3)[:, 0:R], ACT.Copy).then_inc(S["deg_kept"], 1)
            act.wait_ge(S["kvar_ready"], 1)
            act.activation(kstd[:, :], kvar[:, :], ACT.Sqrt).then_inc(S["kstd_ready"], 1)

            with act.Fori(0, ROUNDS) as i:
                for m in range(KC):
                    act.wait_ge(S["mix_done"], KC * i + m + 1)
                    if m == 0:
                        act.wait_ge(S["w2_done"], R * i + 1)
                    act.activation(hb[:, m, :], banks(2 * m, 2)[:, 0:R * P], ACT.Gelu,
                                   bias=bias1[:, m:m + 1]).then_inc(S["gelu_done"], 1)
                for j in range(R):
                    if j == 0:
                        act.wait_ge(S["scale_kept"], 1)
                        act.wait_ge(S["kv_summed"], R + T)
                    act.activation(u[0][:, bass.ds(R * i + j, 1), 0:D].rearrange("p o f -> p (o f)"),
                                   acc[:, bass.ds(R * i + j, 1), :].rearrange("p o f -> p (o f)"),
                                   ACT.Copy, scale=scale2[0:P, 0:1]).then_inc(S["high_ready"], 1)

            act.wait_ge(S["deg_ready"], 1)
            with act.Fori(0, STEPS // 2) as it:
                for par in range(2):
                    with act.Fori(0, ROUNDS) as i:
                        for j in range(R):
                            n = 2 * T * it + T * par + R * i + j
                            act.wait_ge(S["tile_done"], R + n + 1)
                            act.activation(lo_part[:, j, :], banks(j)[0:P, D:2 * D], ACT.Copy,
                                           scale=deg[0:P, bass.ds(R * i + j, 1)]).then_inc(S["low_part"], 1)
                            act.wait_ge(S["sum_ready"], R + n + 1)
                            act.activation(u[1 - par][:, bass.ds(R * i + j, 1), 0:D].rearrange("p o f -> p (o f)"),
                                           u_sum[:, j, :], ACT.Copy).then_inc(S["high_kept"], 1)

            act.wait_ge(S["gen_end"], 1)
            with act.Fori(0, ROUNDS) as i:
                for j in range(R):
                    n = R * i + j
                    act.wait_ge(S["out_done"], n + 1)
                    act.activation(at_in[:, j, :], acc[:, bass.ds(n, 1), :].rearrange("p o f -> p (o f)"),
                                   ACT.Copy).then_inc(S["acc_in"], 1)
                    act.wait_ge(S["acc_turned"], n + 1)
                    act.activation(at_t[:, j, :, :], banks(5)[:, 0:256].rearrange("p (k m) -> p k m", k=KC)[:, :, 0:P],
                                   ACT.Copy).then_inc(S["at_ready"], 1)
            act.wait_ge(S["var_ready"], 2)
            act.activation(lnu[:, :], lnt[:, :], ACT.Sqrt).then_inc(S["std_ready"], 1)
            act.wait_ge(S["norm_ready"], 1)
            with act.Fori(0, ROUNDS) as i:
                for j in range(R):
                    n = R * i + j
                    act.wait_ge(S["y_kept"], n + 1)
                    act.wait_ge(S["y_turned"], n + 1)
                    act.activation(y_in[:, j, :], x1[:, bass.ds(n, 1), :].rearrange("p o f -> p (o f)"), ACT.Identity,
                                   bias=nmr[:, bass.ds(n, 1)], scale=rstd[:, bass.ds(n, 1)]).then_inc(S["y_ready"], 1)
            for k in range(3):
                act.wait_ge(S["exp_in"], k + 1)
                act.activation(small[0:1, 24:32], small[0:1, 16:24], ACT.Exp).then_inc(S["exp_out"], 1)

            with act.Fori(0, ROUNDS) as i:
                for e in range(2):
                    for m in range(FM):
                        at = FM * e + m
                        act.wait_ge(S["hid_done"], 2 * FM * i + at + 1)
                        if at == 0:
                            act.wait_ge(S["ffn_done"], R * i + 1)
                        act.activation(hid[:, e, m, :], banks(2 * (at % 2), 2)[:, 0:R * P], ACT.Gelu,
                                       bias=b1e[:, e, m:m + 1]).then_inc(S["hid_ready"], 1)
                act.wait_ge(S["var2_ready"], i + 1)
                act.activation(lnu[:, 0:R], lnt[:, 0:R], ACT.Sqrt).then_inc(S["std2_ready"], 1)

        @block.vector
        def _(dve):
            def norm_front(link, s, t, v, count):
                link(dve.tensor_tensor(v, s[:, :, 1], s[:, :, 4], ALU.subtract))
                link(dve.tensor_tensor(v, v, v, ALU.mult))
                link(dve.tensor_tensor(t, s[:, :, 2], s[:, :, 5], ALU.add))
                link(dve.scalar_tensor_tensor(t, v, D / 4.0, t, ALU.mult, ALU.add))
                return dve.tensor_scalar(t, t, 1.0 / D, EPS, ALU.mult, ALU.add)

            def norm_back(link, s, v, m, r):
                link(dve.reciprocal(r, v))
                link(dve.tensor_tensor(m, s[:, :, 1], s[:, :, 4], ALU.add))
                link(dve.tensor_scalar(m, m, 0.5, None, ALU.mult))

            link = Links(dve, S["dve_edge"])
            dve.memset(ones[:, :], 1.0).then_inc(S["ones_set"], 1)
            dve.memset(ones16[:, :], 1.0).then_inc(S["ones_set"], 1)
            dve.memset(small[:, :], 0.0).then_inc(S["ones_set"], 1)
            dve.memset(zeros[:, :], 0.0).then_inc(S["ones_set"], 1)
            for name, c in (("h_biased", 1), ("kc_ready", 1), ("sq_used", 1), ("x1_mixed", R), ("sum_ready", R),
                            ("or_done", R), ("gen_added", 1), ("x1_ready", R), ("yt_ready", R), ("r_ready", R),
                            ("out_ready", R)):
                dve.sem_inc(S[name], c)
            dve.wait_ge(S["const_in"], 16)
            dve.wait_ge(S["edges_in"], 16 * 2 * (1 + 128 - FULLP))
            dve.scalar_tensor_tensor(code[:, :], si[:, :], 4096.0, di[:, :], ALU.mult, ALU.add).then_inc(S["code_ready"], 1)
            smp = di[:, 0:EC].rearrange("p (s l) -> p s l", l=AL)[:, :, 0]
            link(dve.tensor_scalar(gds[:, 0, :], smp, 1.0 / GD, -0.4, ALU.mult, ALU.add))
            link(dve.tensor_scalar(gds[:, 1, :], gds[:, 0, :], MAGIC, MAGIC, ALU.add, ALU.subtract))
            link(dve.tensor_copy(iota16[:, :], cst[:, C_IOTA:C_GRP]))
            link(dve.tensor_copy(grp16[:, :], grp))
            with dve.Fori(0, NS // SR) as i:
                for s in range(SR):
                    t = SR * i + s
                    dve.wait_ge(S["cmp_used"], t + 1)
                    dve.tensor_scalar(cmp[:, s, :], grp16[:, :], gds[:, 1, bass.ds(t, 1)], None,
                                      ALU.is_gt).then_inc(S["cmp_ready"], 1)

            dve.wait_ge(S["x_in"], 16 * ROUNDS)
            with dve.Fori(0, T) as n:
                dve.bn_stats(st[:, bass.ds(n, 1), :].rearrange("p o f -> p (o f)"),
                             x1[:, bass.ds(n, 1), :].rearrange("p o f -> p (o f)")).then_inc(S["stats"], 1)
            dve.wait_ge(S["stats"], T)
            nlink = Links(dve, S["dve_norm"])
            norm_front(nlink, st, lnt[:, :], lnu[:, :], T).then_inc(S["var_ready"], 1)
            wlink = Links(dve, S["dve_w"])
            dve.wait_ge(S["kvw_in"], 32)
            wv = w_kv[:, :, :].rearrange("p k (g l) -> p (k g) l", l=HD)
            wlink(dve.tensor_reduce(wsum[:, :], wv, AX.X, ALU.add))
            wlink(dve.tensor_scalar(wsum[:, :], wsum[:, :], -1.0 / HD, None, ALU.mult))
            dve.tensor_tensor(wv, wv, wsum[:, :].rearrange("p (g o) -> p g o", o=1).to_broadcast([128, (KC + 1) * 2 * HEADS, HD]),
                              ALU.add).then_inc(S["wkv_ready"], 1)
            dve.wait_ge(S["wkv_ready"], 1)
            dve.wait_ge(S["std_ready"], 1)
            norm_back(nlink, st, lnu[:, :], mean[:, :], rstd[:, :])

            dve.wait_ge(S["cmp_used"], SR + NS)
            dve.tensor_scalar(start_i[:, :], banks(0)[0:P, 0:GT], 1.0, 0.0, ALU.subtract, ALU.max).then_inc(S["start_ready"], 1)
            dve.wait_ge(S["code_turned"], GT)
            for b, n in ((1, 4), (2, 1)):
                link(dve.tensor_copy(e_int[:, 0, (b - 1) * 4 * P:(b - 1) * 4 * P + n * P].rearrange("p (t g) -> p t g", t=n),
                                     banks(b)[:, 0:n * 128].rearrange("p (t g) -> p t g", t=n)[:, :, 0:P]))
            link(dve.tensor_scalar(e_int[:, 1, :], e_int[:, 0, :], 12, None, ALU.logical_shift_right))
            link(dve.tensor_scalar(e_int[:, 2, :], e_int[:, 0, :], 4095, None, ALU.bitwise_and))
            src_i, dst_i = e_int[:, 1, :], e_int[:, 2, :]
            link(dve.tensor_scalar(e_f[:, 0, :], src_i, 1.0 / P, -0.496, ALU.mult, ALU.add))
            link(dve.tensor_scalar(e_f[:, 0, :], e_f[:, 0, :], MAGIC, MAGIC, ALU.add, ALU.subtract))
            link(dve.tensor_scalar(e_f[:, 1, :], dst_i, 1.0 / GD, -0.4, ALU.mult, ALU.add))
            link(dve.tensor_scalar(e_f[:, 1, :], e_f[:, 1, :], MAGIC, MAGIC, ALU.add, ALU.subtract))
            link(dve.scalar_tensor_tensor(eq[:, 1, :], e_f[:, 0, :], -float(P), src_i, ALU.mult, ALU.add))
            link(dve.scalar_tensor_tensor(e_f[:, 2, :], e_f[:, 0, :], float(GD), dst_i, ALU.mult, ALU.add))
            link(dve.scalar_tensor_tensor(e_f[:, 3, :], e_f[:, 1, :], 1000.0 - GD, e_f[:, 2, :], ALU.mult, ALU.add))
            link(dve.scalar_tensor_tensor(eq[:, 0, :], grp, -1000.0, e_f[:, 3, :], ALU.mult, ALU.add))
            dve.memset(stage[:, :, :].rearrange("p r (c m) -> p (r c) m", m=128)[:, :, P:128], 0).then_inc(S["stage_clear"], 1)

            def normalize(n, j):
                dve.tensor_scalar(xn[:, j, :], x1[:, bass.ds(n, 1), :].rearrange("p o f -> p (o f)"),
                                  mean[:, bass.ds(n, 1)], rstd[:, bass.ds(n, 1)],
                                  ALU.subtract, ALU.mult).then_inc(S["xn_ready"], 1)

            def square_sums(n):
                dve.wait_ge(S["sq_ready"], n + 1)
                dve.tensor_reduce(kvar[:, bass.ds(2 * HEADS * n, 2 * HEADS)], sq[:, :].rearrange("p (g l) -> p g l", l=HD),
                                  AX.X, ALU.add).then_inc(S["sq_used"], 1)

            for j in range(R):
                normalize(j, j)

            def tile_round(i, last):
                for j in range(R):
                    n = R * i + j
                    dve.wait_ge(S["ohd_ready"], NB * n + NB)
                    dve.tensor_copy(cur[:, j, :, :], eq[:, :, bass.ds(GPT * n, GPT)]).then_inc(S["cur_ready"], 1)
                    dve.wait_ge(S["cur_ready"], n + 1)
                    g = 0
                    for b, size in enumerate(BATCHES):
                        dve.wait_ge(S["batch_done"], NB * n + b + 1)
                        for s in range(size):
                            ins = dve.tensor_scalar(oh_q[:, g, 0:126], iota16[:, 0:126], cur[:, j, 0, g:g + 1], None, ALU.is_equal)
                            g += 1
                        ins.then_inc(S["ohq_ready"], 1)
                        if b == 4:
                            dve.wait_ge(S["h_done"], n + 1)
                            dve.wait_ge(S["silu_done"], n + 1)
                            dve.tensor_tensor(h_pre[:, :], banks(1)[0:P, 0:D], b_in[:, :], ALU.add).then_inc(S["h_biased"], 1)
                            dve.wait_ge(S["kv_done"], n + 1)
                            dve.tensor_tensor(kc_all[:, bass.ds(n, 1), :].rearrange("p o f -> p (o f)"), banks(2)[0:P, :],
                                              w_kv[0:P, KC, :], ALU.add).then_inc(S["kc_ready"], 1)
                        if b == 6 and not last:
                            dve.wait_ge(S["x1_bias"], 1 + n + 1)
                            normalize(n + R, j)
                    if j:
                        square_sums(n - 1)
                square_sums(R * i + R - 1)

            dve.wait_ge(S["weights_in"], 16 * N_WEIGHTS)
            with dve.Fori(0, ROUNDS - 1) as i:
                tile_round(i, False)
            tile_round(ROUNDS - 1, True)

            dve.wait_ge(S["deg_kept"], 1 + ROUNDS)
            klink = Links(dve, S["dve_kv"])
            dve.wait_ge(S["sq_used"], 1 + T)
            dve.tensor_scalar(kvar[:, :], kvar[:, :], 1.0 / HD, EPS, ALU.mult, ALU.add).then_inc(S["kvar_ready"], 1)
            dve.wait_ge(S["kstd_ready"], 1)
            klink(dve.reciprocal(kvar[:, :], kstd[:, :]))
            dve.wait_ge(S["batch_done"], NB + NB * T)
            with dve.Fori(0, ROUNDS) as i:
                for j in range(R):
                    n = R * i + j
                    dve.wait_ge(S["kv_summed"], n + 1)
                    dve.tensor_tensor(kvn[:, j, :].rearrange("p (g l) -> p g l", l=HD),
                                      kc_all[:, bass.ds(n, 1), :].rearrange("p o (g l) -> p (o g) l", l=HD),
                                      kvar[:, bass.ds(2 * HEADS * n, 2 * HEADS)].rearrange("p (g o) -> p g o", o=1)
                                      .to_broadcast([P, 2 * HEADS, HD]), ALU.mult).then_inc(S["kvn_ready"], 1)
                    dve.wait_ge(S["silu_done"], 1 + T)
                    dve.tensor_reduce(hmx[:, bass.ds(n, 1)], acc[:, bass.ds(n, 1), :].rearrange("p o f -> p (o f)"),
                                      AX.X, ALU.max).then_inc(S["hmax_ready"], 1)
            dve.wait_ge(S["hmax_ready"], T)
            dve.tensor_reduce(hmx[:, T:T + 1], hmx[:, 0:T], AX.X, ALU.max).then_inc(S["hmax_ready"], 1)

            dve.wait_ge(S["kv_summed"], R + T)
            dve.wait_ge(S["xt_kept"], R + T)
            for c in range(KC):
                at = slice(128 * c, 128 * c + 128)
                gv, bv = lnrow[:, 0, at], lnrow[:, 1, at]
                if c:
                    dve.wait_ge(S["kvbd_ready"], c)
                klink(dve.tensor_copy(kvs[:, 2, 0:1], banks(0)[:, D + c:D + c + 1]))
                klink(dve.tensor_tensor(kvs[:, 0, :], banks(0)[:, at], gv, ALU.mult))
                klink(dve.scalar_tensor_tensor(kvs[:, 0, :], bv, kvs[:, 2, 0:1], kvs[:, 0, :], ALU.mult, ALU.add))
                klink(dve.tensor_tensor(kvs[:, 1, :], banks(1)[:, at], gv, ALU.mult))
                klink(dve.scalar_tensor_tensor(kvs[:, 1, :], bv, float(N), kvs[:, 1, :], ALU.mult, ALU.add))
                klink(dve.tensor_scalar(kvs[:, 0, :], kvs[:, 0, :], lncol[:, 0:1], None, ALU.mult))
                klink(dve.scalar_tensor_tensor(kvs[:, 0, :], kvs[:, 1, :], lncol[:, 1:2], kvs[:, 0, :], ALU.mult, ALU.add))
                dve.scalar_tensor_tensor(kv_bd[:, c, :], kvs[:, 0, :], 1.0 / N, mask, ALU.mult, ALU.mult).then_inc(S["kvbd_ready"], 1)
            dve.wait_ge(S["m1_done"], 1)
            for c in range(KC):
                klink(dve.tensor_copy(m1t[:, c, :], banks(4 + c)[:, 0:D + 1]))
            for c in range(KC):
                at = slice(128 * c, 128 * c + 128)
                dve.tensor_tensor(m1t[:, c, at], m1t[:, c, at], ident, ALU.add).then_inc(S["m1_ready"], 1)
            dve.wait_ge(S["g_done"], 1)
            for c in range(KC):
                dve.tensor_copy(g_sb[:, c, :], banks(6)[:, D * c:D * c + D]).then_inc(S["g_ready"], 1)
            dve.tensor_tensor(bias1[:, :], banks(7)[:, 0:KC], b1c[:, :], ALU.add).then_inc(S["g_ready"], 1)
            slink = Links(dve, S["dve_scale"])
            dve.wait_ge(S["hmax_turned"], 1)
            slink(dve.tensor_reduce(small[0:1, 0:1], banks(2)[0:1, 0:P], AX.X, ALU.max))
            slink(dve.tensor_scalar(small[0:1, 0:1], small[0:1, 0:1], 0.28, None, ALU.max))
            slink(dve.tensor_scalar(small[0:1, 1:2].bitcast(I32), small[0:1, 0:1].bitcast(I32), 0x7F800000, None, ALU.bitwise_and))
            slink(dve.reciprocal(small[0:1, 2:3], small[0:1, 1:2]))
            slink(dve.tensor_scalar(small[0:1, 2:3], small[0:1, 2:3], 2.0 ** 14, None, ALU.mult))
            dve.tensor_scalar(small[0:1, 3:4], small[0:1, 1:2], 2.0 ** -14, None, ALU.mult).then_inc(S["scale_ready"], 1)
            dve.wait_ge(S["scale_spread"], 1)
            dve.tensor_copy(scale2[:, :], banks(3)[:, 0:2]).then_inc(S["scale_kept"], 1)
            dve.wait_ge(S["scale_kept"], 1)
            dve.wait_ge(S["pad_set"], 2 + STEPS)
            slink(dve.tensor_scalar(coef[:, :], invf[:, :], scale2[:, 1:2], None, ALU.mult))
            slink(dve.tensor_reduce(fl[:, 0:1], deg[0:P, :], AX.X, ALU.add))
            slink(dve.tensor_scalar(deg[:, :], deg[:, :], 0.125, None, ALU.max))
            dve.reciprocal(deg[:, :], deg[:, :]).then_inc(S["deg_ready"], 1)
            dve.wait_ge(S["deg_ready"], 1)

            with dve.Fori(0, ROUNDS) as i:
                for j in range(R):
                    n = R * i + j
                    dve.wait_ge(S["w2_done"], 1 + n + 1)
                    xr = x1[:, bass.ds(n, 1), :].rearrange("p o f -> p (o f)")
                    dve.tensor_tensor(xr, xr, banks(4 + j % 4)[0:P, 0:D], ALU.add).then_inc(S["x1_mixed"], 1)
                    dve.wait_ge(S["high_ready"], n + 1)
                    dve.scalar_tensor_tensor(u[0][:, bass.ds(n, 1), D:2 * D].rearrange("p o f -> p (o f)"),
                                             acc[:, bass.ds(n, 1), :].rearrange("p o f -> p (o f)"), scale2[0:P, 0:1],
                                             u[0][:, bass.ds(n, 1), 0:D].rearrange("p o f -> p (o f)"),
                                             ALU.mult, ALU.subtract).then_inc(S["split_ready"], 1)

            dve.wait_ge(S["w2_done"], 1 + T)
            slink(dve.memset(orr, 0))
            with dve.Fori(0, STEPS // 2) as it:
                for par in range(2):
                    with dve.Fori(0, ROUNDS) as i:
                        for j in range(R):
                            n = 2 * T * it + T * par + R * i + j
                            at = R * i + j
                            nxt = u[1 - par][:, bass.ds(at, 1), :].rearrange("p o f -> p (o f)")
                            dve.wait_ge(slot_in[j], 2 * 16 * ROUNDS * it + 16 * ROUNDS * par + 16 * i + 16)
                            dve.tensor_tensor(orr, orr, stage[0:P, j, :].bitcast(I32), ALU.bitwise_or).then_inc(S["or_done"], 1)
                            dve.wait_ge(S["low_part"], n + 1)
                            dve.scalar_tensor_tensor(u_sum[:, j, :], banks(j)[0:P, 0:D], deg[0:P, bass.ds(at, 1)],
                                                     lo_part[:, j, :], ALU.mult, ALU.add).then_inc(S["sum_ready"], 1)
                            dve.wait_ge(S["sum_ready"], R + n + 1)
                            xa = acc[:, bass.ds(at, 1), :].rearrange("p o f -> p (o f)")
                            dve.scalar_tensor_tensor(xa, u_sum[:, j, :], coef[0:P, bass.ds(2 * it + par, 1)], xa,
                                                     ALU.mult, ALU.add).then_inc(S["acc_done"], 1)
                            dve.wait_ge(S["high_kept"], n + 1)
                            dve.tensor_tensor(nxt[:, D:2 * D], u_sum[:, j, :], nxt[:, 0:D], ALU.subtract).then_inc(S["split_ready"], 1)

            flink = Links(dve, S["dve_flag"])
            dve.wait_ge(S["or_done"], R + STEPS * T)
            flink(dve.tensor_scalar(orr, orr, 0x40404040, None, ALU.bitwise_and))
            dve.tensor_reduce(fl[:, 1:2], orr, AX.X, ALU.max).then_inc(S["flag_part"], 1)
            dve.wait_ge(S["flag_sum"], 1)
            flink(dve.tensor_scalar(small[0:1, 4:5], banks(5)[0:1, 0:1], E / 8.0, None, ALU.not_equal))
            flink(dve.tensor_scalar(small[0:1, 5:6], banks(5)[0:1, 1:2], 0.0, None, ALU.is_gt))
            dve.tensor_tensor(small_i[0:1, 0:1], small[0:1, 4:5], small[0:1, 5:6], ALU.max).then_inc(S["flag_ready"], 1)
            dve.wait_ge(S["acc_done"], STEPS * T)

            dve.wait_ge(S["flag_ready"], 1)
            bad = dve.value_load(small_i[0:1, 0:1], min_val=0, max_val=1)
            with dve.If(bad == 1):
                dve.wait_ge(S["gen_init"], 64)
                glink = Links(dve, S["gen_add"])
                glink(dve.memset(rows[:, D:D + 1], 1.0))
                glink(dve.tensor_copy(dst_f, dst_all))
                dve.sem_inc(S["gen_dve"], 1)
                with dve.Fori(0, STEPS) as k:
                    glink = Links(dve, S["gen_add"], 2 + 4 * k)
                    glink(dve.memset(sums[:, :, :], 0.0))
                    apart(dve)
                    with dve.Fori(0, EP) as e:
                        n = EP * k + e
                        dve.wait_ge(S["gen_mm"], n + 1)
                        dve.tensor_scalar(oh_g, node_row, dst_f[:, bass.ds(e, 1)], None, ALU.is_equal).then_inc(S["gen_onehot"], 1)
                        for b in range(T // R):
                            dve.wait_ge(S["gen_batch"], R * n + b + 1)
                            for s in range(R):
                                t = R * b + s
                                ins = dve.tensor_tensor(sums[:, t, :], sums[:, t, :], banks(s)[0:P, 0:D + 1], ALU.add)
                            ins.then_inc(S["gen_added"], 1)
                    dve.wait_ge(S["gen_added"], 1 + R * EP * k + R * EP)
                    glink(dve.tensor_scalar(rdeg, sums[:, :, D], 1.0, None, ALU.max))
                    glink(dve.reciprocal(rdeg, rdeg))
                    glink(dve.tensor_tensor(sums[:, :, 0:D], sums[:, :, 0:D],
                                            rdeg.rearrange("p (t o) -> p t o", o=1).to_broadcast([P, T, D]), ALU.mult))
                    dve.scalar_tensor_tensor(acc[:, :, :], sums[:, :, 0:D], invf[0:P, bass.ds(k, 1)], acc[:, :, :],
                                             ALU.mult, ALU.add).then_inc(S["gen_step"], 1)
                    dve.wait_ge(S["gen_step"], k + 1)
                    dve.wait_ge(S["gen_stored"], 16 * k + 16)
                    dve.sem_inc(S["gen_dve"], 1)
            with dve.Else():
                pass
            dve.sem_inc(S["gen_end"], 1)
            with dve.Fori(0, ROUNDS) as i:
                for j in range(R):
                    n = R * i + j
                    dve.wait_ge(S["out_done"], R + n + 1)
                    xr = x1[:, bass.ds(n, 1), :].rearrange("p o f -> p (o f)")
                    dve.tensor_tensor(xr, xr, banks(j)[0:P, 0:D], ALU.add).then_inc(S["x1_ready"], 1)
                    dve.wait_ge(S["x1_ready"], R + n + 1)
                    dve.bn_stats(st[:, bass.ds(n, 1), :].rearrange("p o f -> p (o f)"), xr).then_inc(S["x1_stats"], 1)
            dve.wait_ge(S["x1_stats"], T)
            norm_front(nlink, st, lnt[:, :], lnu[:, :], T).then_inc(S["var_ready"], 1)
            dve.wait_ge(S["std_ready"], 2)
            norm_back(nlink, st, lnu[:, :], mean[:, :], rstd[:, :])
            dve.scalar_tensor_tensor(nmr[:, :], mean[:, :], -1.0, rstd[:, :], ALU.mult, ALU.mult).then_inc(S["norm_ready"], 1)
            with dve.Fori(0, ROUNDS) as i:
                for j in range(R):
                    n = R * i + j
                    dve.wait_ge(S["y_turned"], R + n + 1)
                    dve.tensor_copy(xt_all[:, :, bass.ds(P * n, P)],
                                    banks(j)[:, 0:256].rearrange("p (k m) -> p k m", k=KC)[:, :, 0:P]).then_inc(S["yt_ready"], 1)

            rlink = Links(dve, S["dve_route"])
            dve.wait_ge(S["y_turned"], R + T)
            dve.tensor_scalar(meant[:, :], banks(6)[:, 0:KC], 1.0 / N, None, ALU.mult).then_inc(S["mean_ready"], 1)
            dve.wait_ge(S["logits_done"], 1)
            prob, low, ex = small[0:1, 8:16], small[0:1, 16:24], small[0:1, 24:32]
            top, rec = small[0:1, 48:56], small[0:1, 40:41]

            def softmax(times):
                rlink(dve.tensor_reduce(rec, prob, AX.X, ALU.max))
                dve.tensor_scalar(low, prob, rec, None, ALU.subtract).then_inc(S["exp_in"], 1)
                dve.wait_ge(S["exp_out"], times)
                rlink(dve.tensor_reduce(rec, ex, AX.X, ALU.add))
                rlink(dve.reciprocal(rec, rec))
                rlink(dve.tensor_scalar(prob, ex, rec, None, ALU.mult))

            rlink(dve.tensor_tensor(prob, banks(7)[0:1, 0:NX], br[:, :], ALU.add))
            softmax(1)
            rlink(dve.tensor_scalar(low, prob, float(N), None, ALU.mult))
            rlink(dve.reciprocal(low, low))
            rlink(dve.tensor_scalar(low, low, CAP, 1.0, ALU.mult, ALU.min))
            rlink(dve.tensor_tensor(prob, prob, low, ALU.mult))
            softmax(2)
            rlink(dve.max(top, prob))
            rlink(dve.max_index(idx_u[:, :], top, prob))
            rlink(dve.tensor_copy(small_i[0:1, 2:4], idx_u[0:1, 0:2]))
            dve.sem_inc(S["route_ready"], 1)
            dve.tensor_scalar(low, top, top[:, 0:1], None, ALU.subtract).then_inc(S["exp_in"], 1)
            dve.wait_ge(S["exp_out"], 3)
            rlink(dve.tensor_tensor(rec, ex[:, 0:1], ex[:, 1:2], ALU.add))
            rlink(dve.reciprocal(rec, rec))
            dve.tensor_scalar(small[0:1, 56:58], ex[:, 0:2], rec, None, ALU.mult).then_inc(S["route_spread"], 1)
            dve.wait_ge(S["top_ready"], 1)
            rlink(dve.tensor_copy(topw[:, :], banks(7)[:, 16:18]))
            dve.wait_ge(S["experts_in"], 16 * 8)
            for e in range(2):
                dve.tensor_scalar(w2e[:, e, :, :], w2e[:, e, :, :], topw[:, e:e + 1], None, ALU.mult).then_inc(S["w2_scaled"], 1)
            rlink(dve.tensor_scalar(b2e[:, 0, :], b2e[:, 0, :], topw[0:P, 0:1], None, ALU.mult))
            dve.scalar_tensor_tensor(b2e[:, 0, :], b2e[:, 1, :], topw[0:P, 1:2], b2e[:, 0, :], ALU.mult, ALU.add).then_inc(S["b2_ready"], 1)

            with dve.Fori(0, ROUNDS) as i:
                for j in range(R):
                    n = R * i + j
                    dve.wait_ge(S["ffn_done"], 1 + n + 1)
                    dve.wait_ge(S["yb_ready"], n + 1)
                    dve.tensor_tensor(yb[:, j, :], yb[:, j, :], banks(4 + j % 4)[0:P, 0:D], ALU.add).then_inc(S["r_ready"], 1)
                    dve.wait_ge(S["r_ready"], R + n + 1)
                    dve.bn_stats(st[:, j, :], yb[:, j, :]).then_inc(S["stats2"], 1)
                dve.wait_ge(S["stats2"], R * i + R)
                olink = Links(dve, S["dve_out"], 17 * i)
                norm_front(olink, st[:, 0:R, :], lnt[:, 0:R], lnu[:, 0:R], R).then_inc(S["var2_ready"], 1)
                dve.wait_ge(S["std2_ready"], i + 1)
                norm_back(olink, st[:, 0:R, :], lnu[:, 0:R], mean[:, 0:R], rstd[:, 0:R])
                for j in range(R):
                    n = R * i + j
                    olink(dve.tensor_scalar(yb[:, j, :], yb[:, j, :], mean[:, j:j + 1], rstd[:, j:j + 1], ALU.subtract, ALU.mult))
                    dve.wait_ge(out_in[j], 16 * i + 16)
                    olink(dve.tensor_tensor(fin[:, j, :], yb[:, j, :], gam[:, 0, :], ALU.mult))
                    dve.wait_ge(S["x1b_ready"], n + 1)
                    dve.tensor_tensor(fin[:, j, :], fin[:, j, :], x1b[:, j, :], ALU.add).then_inc(S["out_ready"], 1)
                assert olink.n == 17

        @block.tensor
        def _(pe):
            mm = pe.matmul

            def clear(b, n):
                mm(banks(b)[:, 0:n], zeros[0:1, 0:128], zeros[0:1, 0:n], start=True, stop=True)

            def add(out, lhs, rhs):
                return mm(out, lhs, rhs, start=False, stop=False, skip_group_check=True)

            def turn(b, src):
                for c in range(KC):
                    ins = pe.transpose(banks(b)[:, 128 * c:128 * c + P], src[:, 128 * c:128 * c + 128], ident[0:P, 0:P])
                return ins

            for name, c in (("cmp_used", SR), ("batch_done", NB), ("deg_done", R), ("w2_done", 1), ("kv_summed", R),
                            ("tile_done", R), ("gen_mm", 1), ("out_done", R), ("y_turned", R), ("ffn_done", 1)):
                pe.sem_inc(S[name], c)
            pe.wait_ge(S["const_in"], 16)
            pe.wait_ge(S["ones_set"], 4)
            clear(0, GT)
            with pe.Fori(0, NS // SR) as i:
                for s in range(SR):
                    pe.wait_ge(S["cmp_ready"], SR * i + s + 1)
                    for t in range(GT):
                        ins = add(banks(0)[0:P, t:t + 1], cmp[:, s, P * t:P * t + P], ones16[:, :])
                    ins.then_inc(S["cmp_used"], 1)
            pe.wait_ge(S["got_in"], 16 * GT)
            for t in range(GT):
                pe.transpose(banks(1 + t // 4)[:, 128 * (t % 4):128 * (t % 4) + P], got[:, t, :], ident[0:P, 0:P]).then_inc(S["code_turned"], 1)
            pe.wait_ge(S["weights_in"], 16 * N_WEIGHTS)
            pe.wait_ge(S["wkv_ready"], 1)

            def degrees(i, j):
                if j == 0:
                    pe.wait_ge(S["deg_kept"], i + 1)
                pe.wait_ge(S["batch_out"], 4 + NB * (R * i + j) + NB)
                apart(pe)
                for c in range(T):
                    ins = mm(banks(3)[:, j:j + 1], stage[0:P, j, 128 * c:128 * c + 128].bitcast(F8), ones16[0:P, :],
                             start=(c == 0), stop=(c == T - 1))
                ins.then_inc(S["deg_done"], 1)

            with pe.Fori(0, ROUNDS) as i:
                for j in range(R):
                    n = R * i + j
                    pe.wait_ge(S["xn_ready"], n + 1)
                    pe.wait_ge(S["xt_ready"], n + 1)
                    turn(0, xn[:, j, :]).then_inc(S["turned"], 1)
                    for b, size in enumerate(BATCHES):
                        pe.wait_ge(S["ohq_ready"], NB * n + b + 1)
                        pe.wait_ge(S["ohd_ready"], NB * R + NB * n + b + 1)
                        pe.wait_ge(S["batch_out"], NB * n + b + 1)
                        g = sum(BATCHES[:b])
                        for s in range(size):
                            ins = mm(banks(4 + b % 4)[:, P * s:P * s + P], oh_d[:, g + s, :], oh_q[:, g + s, 0:P],
                                     start=True, stop=True)
                        ins.then_inc(S["batch_done"], 1)
                        if b == 2:
                            pe.wait_ge(S["xt_ready"], 1 + n + 1)
                            pe.wait_ge(S["h_biased"], n + 1)
                            for c in range(KC):
                                ins = mm(banks(1)[0:P, 0:D], xt[:, j, c, :], w_in[:, c, :], start=(c == 0), stop=(c == KC - 1))
                            ins.then_inc(S["h_done"], 1)
                            pe.wait_ge(S["kc_ready"], n + 1)
                            for c in range(KC):
                                ins = mm(banks(2)[0:P, :], xt[:, j, c, :], w_kv[:, c, :], start=(c == 0), stop=(c == KC - 1))
                            ins.then_inc(S["kv_done"], 1)
                    if j:
                        degrees(i, j - 1)
                degrees(i, R - 1)

            pe.wait_ge(S["h_biased"], 1 + T)
            clear(0, D + KC)
            clear(1, D)
            with pe.Fori(0, ROUNDS) as i:
                for j in range(R):
                    pe.wait_ge(S["kvn_ready"], R * i + j + 1)
                    for c in range(KC):
                        kk = kvn[:, j, 128 * c:128 * c + 128]
                        add(banks(0)[:, 128 * c:128 * c + 128], kk, kvn[:, j, D + 128 * c:D + 128 * c + 128])
                        add(banks(0)[:, D + c:D + c + 1], kk, ones[0:P, 0:1])
                    add(banks(1)[:, 0:D], ones[0:P, :], kvn[:, j, D:2 * D]).then_inc(S["kv_summed"], 1)
            pe.wait_ge(S["hmax_ready"], T + 1)
            mm(banks(2)[0:1, 0:P], hmx[:, T:T + 1], ident[0:P, 0:P], start=True, stop=True).then_inc(S["hmax_turned"], 1)
            pe.wait_ge(S["kvbd_ready"], KC)
            for c in range(KC):
                ins = mm(banks(4 + c)[:, 0:D + 1], kv_bd[:, c, :], wq_t[:, c, :], start=True, stop=True)
            ins.then_inc(S["m1_done"], 1)
            pe.wait_ge(S["m1_ready"], KC)
            for m in range(KC):
                for c in range(KC):
                    mm(banks(6)[:, D * m:D * m + D], m1t[:, c, 128 * m:128 * m + 128], w1[:, c, :],
                       start=(c == 0), stop=(c == KC - 1))
            for m in range(KC):
                for c in range(KC):
                    ins = mm(banks(7)[:, m:m + 1], w1[:, c, 128 * m:128 * m + 128], m1t[:, c, D:D + 1],
                             start=(c == 0), stop=(c == KC - 1))
            ins.then_inc(S["g_done"], 1)
            pe.wait_ge(S["scale_ready"], 1)
            pe.wait_ge(S["deg_kept"], 1 + ROUNDS)
            mm(banks(3)[:, 0:2], ones[0:1, :], small[0:1, 2:4], start=True, stop=True).then_inc(S["scale_spread"], 1)
            pe.wait_ge(S["g_ready"], KC + 1)
            pe.wait_ge(S["scale_kept"], 1)
            pe.wait_ge(S["xt_kept"], R + T)

            def wide(b, lhs, i, c, k):
                for at, n in ((0, 512), (512, R * P - 512)):
                    ins = mm(banks(b, 2)[:, at:at + n], lhs, xt_all[:, c, bass.ds(R * P * i + at, n)],
                             start=(c == 0), stop=(c == k - 1))
                return ins

            def tile_bank(sem, i, j):
                back = 1 if j == 0 else 4 if j == 4 else 5
                pe.wait_ge(sem, R + R * i + j - back + 1)

            with pe.Fori(0, ROUNDS) as i:
                for m in range(KC):
                    pe.wait_ge(S["gelu_done"], KC * i + m + 1)
                    for c in range(KC):
                        ins = wide(2 * m, g_sb[:, c, 128 * m:128 * m + 128], i, c, KC)
                    ins.then_inc(S["mix_done"], 1)
                pe.wait_ge(S["gelu_done"], KC + KC * i + KC)
                for j in range(R):
                    tile_bank(S["x1_mixed"], i, j)
                    for c in range(KC):
                        ins = mm(banks(4 + j % 4)[0:P, 0:D], hb[:, c, P * j:P * j + P], w2[:, c, :],
                                 start=(c == 0), stop=(c == KC - 1))
                    ins.then_inc(S["w2_done"], 1)

            pe.wait_ge(S["x1_mixed"], R + T)
            with pe.Fori(0, STEPS // 2) as it:
                for par in range(2):
                    with pe.Fori(0, ROUNDS) as i:
                        for j in range(R):
                            n = 2 * T * it + T * par + R * i + j
                            step = 2 * T * it + T * par
                            pe.wait_ge(slot_in[j], 2 * 16 * ROUNDS * it + 16 * ROUNDS * par + 16 * i + 16)
                            pe.wait_ge(S["sum_ready"], n + 1)
                            for c in range(T):
                                if j == 0 and c in (0, T - 2, T - 1):
                                    pe.wait_ge(S["split_ready"], step + (T - 2 if c == 0 else c + 1))
                                if c in (0, T - 2, T - 1):
                                    apart(pe)
                                ins = mm(banks(j)[:, :], stage[0:P, j, 128 * c:128 * c + 128].bitcast(F8), u[par][:, c, :],
                                         start=(c == 0), stop=(c == T - 1))
                            ins.then_inc(S["tile_done"], 1)

            pe.wait_ge(S["flag_part"], 1)
            mm(banks(5)[0:1, 0:2], ones[0:P, 0:1], fl[:, :], start=True, stop=True).then_inc(S["flag_sum"], 1)
            pe.wait_ge(S["flag_ready"], 1)
            bad = pe.value_load(small_i[0:1, 0:1], min_val=0, max_val=1)
            with pe.If(bad == 1):
                with pe.Fori(0, STEPS) as k:
                    with pe.Fori(0, EP) as e:
                        n = EP * k + e
                        pe.wait_ge(S["gen_got"], n + 1)
                        pe.wait_ge(S["gen_onehot"], n + 1)
                        for b in range(T // R):
                            pe.wait_ge(S["gen_added"], R * n + b + 1)
                            for s in range(R):
                                t = R * b + s
                                ins = mm(banks(s)[0:P, 0:D + 1], oh_g[:, P * t:P * t + P], rows, start=True, stop=True)
                            ins.then_inc(S["gen_batch"], 1)
                        pe.wait_ge(S["gen_batch"], R * n + R)
                        pe.sem_inc(S["gen_mm"], 1)
            with pe.Else():
                pass

            pe.wait_ge(S["gen_end"], 1)
            with pe.Fori(0, ROUNDS) as i:
                for j in range(R):
                    n = R * i + j
                    pe.wait_ge(S["acc_in"], n + 1)
                    pe.wait_ge(S["at_ready"], n + 1)
                    turn(5, at_in[:, j, :]).then_inc(S["acc_turned"], 1)
                    pe.wait_ge(S["at_ready"], 1 + n + 1)
                    pe.wait_ge(S["x1_ready"], n + 1)
                    for c in range(KC):
                        ins = mm(banks(j)[0:P, 0:D], at_t[:, j, c, :], w_out[:, c, :], start=(c == 0), stop=(c == KC - 1))
                    ins.then_inc(S["out_done"], 1)
            pe.wait_ge(S["x1_ready"], R + T)
            clear(6, KC)
            with pe.Fori(0, ROUNDS) as i:
                for j in range(R):
                    n = R * i + j
                    pe.wait_ge(S["y_ready"], n + 1)
                    for c in range(KC):
                        ins = add(banks(6)[:, c:c + 1], y_in[:, j, 128 * c:128 * c + 128], ones[0:P, 0:1])
                    pe.wait_ge(S["yt_ready"], n + 1)
                    turn(j, y_in[:, j, :]).then_inc(S["y_turned"], 1)
            pe.wait_ge(S["mean_ready"], 1)
            for c in range(KC):
                ins = mm(banks(7)[0:1, 0:NX], meant[:, c:c + 1], wr[:, c, :], start=(c == 0), stop=(c == KC - 1))
            ins.then_inc(S["logits_done"], 1)
            pe.wait_ge(S["route_spread"], 1)
            mm(banks(7)[:, 16:18], ones[0:1, :], small[0:1, 56:58], start=True, stop=True).then_inc(S["top_ready"], 1)

            pe.wait_ge(S["yt_ready"], R + T)
            pe.wait_ge(S["w2_scaled"], 2)
            with pe.Fori(0, ROUNDS) as i:
                for e in range(2):
                    for m in range(FM):
                        at = FM * e + m
                        pe.wait_ge(S["hid_ready"], 2 * FM * i + at + 1)
                        for c in range(KC):
                            ins = wide(2 * (at % 2), w1e[:, e, c, 128 * m:128 * m + 128], i, c, KC)
                        ins.then_inc(S["hid_done"], 1)
                for j in range(R):
                    tile_bank(S["r_ready"], i, j)
                    for e in range(2):
                        for m in range(FM):
                            if j == 0:
                                pe.wait_ge(S["hid_ready"], 2 + 2 * FM * i + FM * e + m + 1)
                            ins = mm(banks(4 + j % 4)[0:P, 0:D], hid[:, e, m, P * j:P * j + P], w2e[:, e, m, :],
                                     start=(e == 0 and m == 0), stop=(e == 1 and m == FM - 1))
                    ins.then_inc(S["ffn_done"], 1)


def kernel(**inputs):
    import concourse.bacc as _bacc
    from concourse.bass_utils import run_bass_kernel_spmd as _run

    x = {k: np.ascontiguousarray(v) for k, v in inputs.items()}
    m = "L0_mix_"
    heads = x[m + "w_qkv"].reshape(D, HEADS, 3, HD)
    bias = x[m + "b_qkv"].reshape(HEADS, 3, HD)
    laid = {
        "x": x["x"], "src": x["src"], "dst": x["dst"], "const": constants(),
        "w_in_t": x["L0_gnn_W_in"].T, "b_in": x["L0_gnn_b_in"],
        "w_out_t": x["L0_gnn_W_out"].T, "b_out": x["L0_gnn_b_out"],
        "w_q_t": np.concatenate([heads[:, :, 0].reshape(D, D).T, bias[:, 0].reshape(D, 1)], axis=1),
        "w_kv": heads[:, :, 1:].transpose(0, 2, 1, 3).reshape(D, 2 * D),
        "b_kv": bias[:, 1:].transpose(1, 0, 2).reshape(2 * D),
        "kln": np.stack([np.tile(x[m + "kln_g"], 4), np.tile(x[m + "kln_b"], 4)], axis=1),
        "vln_g": np.tile(x[m + "vln_g"], HEADS), "vln_b": np.tile(x[m + "vln_b"], HEADS),
        "w1": x[m + "w1"], "b1": x[m + "b1"].reshape(KC, 128).T, "w2": x[m + "w2"], "b2": x[m + "b2"],
        "wr": x["L0_ffn_Wr"], "br": x["L0_ffn_br"],
        "e_w1": x["L0_ffn_W1"].reshape(NX, KC, 128, FF),
        "e_b1": x["L0_ffn_b1"].reshape(NX, FM, 128).transpose(0, 2, 1),
        "e_w2": x["L0_ffn_W2"].reshape(NX, FM, 128, D), "e_b2": x["L0_ffn_b2"],
        "gamma": x["L0_ffn_gamma"], "beta": x["L0_ffn_beta"],
    }
    nc = _bacc.Bacc("TRN2", target_bir_lowering=False, num_devices=1)
    arrays, a = {}, {}
    for name, v in laid.items():
        arrays["in_" + name] = np.ascontiguousarray(v)
        a[name] = nc.dram_tensor("in_" + name, v.shape, mybir.dt.from_np(v.dtype), kind="ExternalInput").ap()
    out = nc.dram_tensor("out_0", (N, D), F32, kind="ExternalOutput").ap()
    gps_kernel(nc, a, out)
    return _run(nc, [arrays], core_ids=[0]).results[0]["out_0"]
```

```python
import numpy as np

import concourse.bass as bass
from concourse import mybir
from contextlib import ExitStack

F32, F16, I32 = mybir.dt.float32, mybir.dt.float16, mybir.dt.int32
U8, F8 = mybir.dt.uint8, mybir.dt.float8e4
ACT, ALU, AX = mybir.ActivationFunctionType, mybir.AluOpType, mybir.AxisListType

N, D, E = 3125, 256, 53125
P = 125
T = N // P
R = 5
ROUNDS = T // R
KC = D // 128
HEADS, HD = 8, 32
STEPS = 6
EPS = 1e-5
NX, FF = 8, 512
FM = FF // 128
CAP = float(-(-(N * 125) // (NX * 100)))

GD = 5
G = N // GD
GT = G // P
GPT = P // GD
W = 128
AL = 8
EC = 416
ECH = EC + W - AL
NS = EC // AL
PAD = 4095
LASTP = E - 127 * EC
FULLP = (E - ECH) // EC + 1
HALVES = (GPT // 2, GPT - GPT // 2)
BATCHES = [3] * 7 + [4]
NB = len(BATCHES)
SR = 4
N_WEIGHTS = 12
MAGIC = 12582912.0
CHUNK = 4
CW = CHUNK * P
LAG = 3

C_ID, C_MASK, C_IOTA, C_GRP, C_NODE, C_END = np.cumsum([0, 128, 128, 128, G, N]).tolist()


def constants():
    c = np.zeros((128, C_END), np.float32)
    c[:, C_ID:C_MASK] = np.eye(128)
    c[:, C_MASK:C_IOTA] = np.kron(np.eye(4), np.ones((32, 32)))
    c[:, C_IOTA:C_GRP] = np.arange(128)
    c[:, C_GRP:C_NODE] = np.arange(G)
    c[:, C_NODE:C_END] = np.arange(N)
    return c


class Links:

    def __init__(self, eng, sem, base=0):
        self.eng, self.sem, self.base, self.n = eng, sem, base, 0

    def __call__(self, ins):
        self.n += 1
        ins.then_inc(self.sem, 1)
        self.eng.wait_ge(self.sem, self.base + self.n)


def gps_kernel(nc, a, out):
    ctx = ExitStack()
    with ctx:
        def sb(name, shape, dt=F32):
            return ctx.enter_context(nc.sbuf_tensor(name, shape, dt))

        def dram(name, shape, dt=F32):
            return nc.dram_tensor(name, shape, dt, kind="Internal").ap()

        def sem(name):
            return ctx.enter_context(nc.semaphore(name))

        windows = dram("windows", (128 * NS, W))
        counts = dram("counts", (T, P, T * 128), U8)
        term_dram = dram("term_dram", (N, D))

        cst = sb("cst", [128, C_GRP])
        ident, mask = cst[:, C_ID:C_MASK], cst[:, C_MASK:C_IOTA]
        x1 = sb("x1", [P, T, D])
        acc = sb("acc", [P, T, D])
        xt_all = sb("xt_all", [128, KC, N])
        big = sb("big", [128, 2 * T * D])
        u = [big[0:P, s * T * D:(s + 1) * T * D].bitcast(F16).rearrange("p (t f) -> p t f", t=T)
             for s in range(2)]
        h_pre = big[0:P, 0:2 * D].rearrange("p (r f) -> p r f", r=2)
        sq = big[0:P, 2 * D:6 * D].rearrange("p (r f) -> p r f", r=2)
        kc = big[0:P, T * D:T * D + 2 * R * D].rearrange("p (r f) -> p r f", r=R)
        kvn = big[0:P, T * D + 2 * R * D:T * D + 4 * R * D].rearrange("p (r f) -> p r f", r=R)
        w_in = sb("w_in", [128, KC, D])
        w_out = sb("w_out", [128, KC, D])
        wq_t = sb("wq_t", [128, KC, D + 1])
        w_kv = sb("w_kv", [128, KC + 1, 2 * D])
        w1 = sb("w1", [128, KC, D])
        w2 = sb("w2", [128, KC, D])
        wr = sb("wr", [128, KC, NX])
        b_in = sb("b_in", [P, D])
        b_add = sb("b_add", [P, 2, D])
        gam = sb("gam", [P, 2, D])
        lnrow = sb("lnrow", [128, 2, D])
        lncol = sb("lncol", [128, 2])
        b1c = sb("b1c", [128, KC])
        br = sb("br", [1, NX])
        ones = sb("ones", [128, 128])
        ones16 = sb("ones16", [128, 1], F16)
        st = sb("st", [P, T, 6])
        mean, rstd, nmr, lnt = (sb(n, [P, T]) for n in ("mean", "rstd", "nmr", "lnt"))
        lnu = sb("lnu", [P, T])
        deg = sb("deg", [128, T])
        deg_raw = sb("deg_raw", [128, T])
        deg_t = sb("deg_t", [128, 2])
        mv = sb("mv", [P, 2])
        scale2 = sb("scale2", [128, 2])
        coef = sb("coef", [128, STEPS])
        invf = sb("invf", [128, STEPS])
        zeros = sb("zeros", [1, 128])
        wsum = sb("wsum", [128, (KC + 1) * 2 * HEADS])
        kvar = sb("kvar", [P, R * 2 * HEADS])
        hmx = sb("hmx", [P, T + 1])
        small = sb("small", [1, 64])
        small_i = sb("small_i", [1, 16], I32)
        idx_u = sb("idx_u", [1, 8], mybir.dt.uint32)
        g_sb = sb("g_sb", [128, KC, D])
        bias1 = sb("bias1", [128, KC])
        fl = sb("fl", [P, 2])
        REGION = 13460
        region = sb("region", [128, REGION])

        def view(at, words, dt=F32, parts=128):
            assert at + words <= REGION
            v = region[0:parts, at:at + words]
            return v if dt == F32 else v.bitcast(dt)

        eq = view(0, 640, F16)[:, 0:2 * G].rearrange("p (a g) -> p a g", a=2)
        iota_g = view(640, 64 * HALVES[1], F16).rearrange("p (m g) -> p m g", m=128)
        OH = 640 + 64 * HALVES[1]
        oh = [view(OH + h * 128 * HALVES[1], 128 * HALVES[1], F16).rearrange("p (a m g) -> p a m g", a=2, m=128)
              for h in range(2)]
        STAGE = OH + 2 * 128 * HALVES[1]
        stage = view(STAGE, R * T * 32, U8).rearrange("p (r m) -> p r m", r=R)
        TOK = STAGE + R * T * 32
        grp = view(OH, G)
        got = view(OH + G, GT * W, F32, P).rearrange("p (t e) -> p t e", t=GT)
        start_i = view(OH + G + GT * W, GT, I32, P)
        at = OH + G + GT * W + GT
        di, si, code = view(at, ECH, I32), view(at + ECH, ECH, I32), view(at + 2 * ECH, ECH)
        gds = view(at + 3 * ECH, 2 * NS).rearrange("p (a s) -> p a s", a=2)
        grp16 = view(at + 3 * ECH + 2 * NS, 320, F16)[:, 0:G]
        cmp = view(at + 3 * ECH + 2 * NS + 320, SR * 320, F16).rearrange("p (r g) -> p r g", r=SR)[:, :, 0:G]
        e_int = view(at, 3 * G, I32).rearrange("p (a g) -> p a g", a=3)
        e_f = view(at + 3 * G, 4 * G).rearrange("p (a g) -> p a g", a=4)
        assert at + 7 * G <= TOK
        xn = view(TOK, R * D, F32, P).rearrange("p (r f) -> p r f", r=R)
        xt = view(TOK + R * D, R * KC * P).rearrange("p (r k m) -> p r k m", r=R, k=KC)
        pool_t = b_add[:, 1, :]
        hb = view(TOK, KC * R * P).rearrange("p (k m) -> p k m", k=KC)
        lo_part = view(TOK + 2080, R * D, F32, P).rearrange("p (r f) -> p r f", r=R)
        u_sum = view(TOK + 2080 + R * D, R * D, F32, P).rearrange("p (r f) -> p r f", r=R)
        at = TOK
        kvs = view(at, 3 * 128).rearrange("p (a f) -> p a f", a=3)
        kv_bd = view(at + 384, KC * 128).rearrange("p (k f) -> p k f", k=KC)
        m1t = view(at + 640, KC * (D + 1)).rearrange("p (k f) -> p k f", k=KC)
        orr = view(TOK + 1280, T * 32, I32, P)
        at_in = view(OH, R * D, F32, P).rearrange("p (r f) -> p r f", r=R)
        at_t = view(OH + R * D, R * KC * P).rearrange("p (r k m) -> p r k m", r=R, k=KC)
        y_in = view(0, R * D, F32, P).rearrange("p (r f) -> p r f", r=R)
        hid = big[:, 0:2 * FM * R * P].rearrange("p (e m t) -> p e m t", e=2, m=FM)
        o1 = 2 * FM * R * P
        w1e = big[:, o1:o1 + 2 * KC * FF].rearrange("p (e k f) -> p e k f", e=2, k=KC)
        w2e = big[:, o1 + 2 * KC * FF:o1 + 2 * KC * FF + 2 * FM * D].rearrange("p (e m f) -> p e m f", e=2, m=FM)
        at = OH + 2 * R * D
        b1e = view(at, 2 * FM).rearrange("p (e m) -> p e m", e=2)
        b2e = view(at + 2 * FM, 2 * D, F32, P).rearrange("p (e f) -> p e f", e=2)
        topw = view(at + 2 * FM + 2 * D, 2)
        meant = view(at + 2 * FM + 2 * D + 2, KC)
        assert at + 2 * FM + 2 * D + 2 + KC <= STAGE
        yb = view(OH + R * D, R * D, F32, P).rearrange("p (r f) -> p r f", r=R)
        fin = view(STAGE, R * D, F32, P).rearrange("p (r f) -> p r f", r=R)
        x1b = view(STAGE + R * D, R * D, F32, P).rearrange("p (r f) -> p r f", r=R)
        node_row = big[0:P, 0:N]
        oh_g = big[0:P, N:2 * N]
        sums = big[0:P, 2 * N:2 * N + T * (D + 1)].rearrange("p (t f) -> p t f", t=T)
        EP = E // P
        src_all = view(OH, EP, I32, P)
        dst_all = view(OH + EP, EP, I32, P)
        dst_f = view(OH + 2 * EP, EP, F32, P)
        idx_g = view(OH + 3 * EP, 1, I32, P)
        rdeg = view(OH + 3 * EP + 8, T, F32, P)
        rows = view(OH + 3 * EP + 40, D + 1, F32, P)

        ps = ctx.enter_context(nc.psum_tensor("ps", [128, 8, 512], F32))

        def banks(b, n=1):
            return ps[:, b:b + n, :].rearrange("p b c -> p (b c)")

        names = {}

        def sems(*each):
            for n in each:
                names[n] = sem(n)

        sems("waited", "pad_set", "edges_in", "const_in", "code_ready", "windows_out", "silu_done",
             "h_kept", "batch_out", "tile_done", "or_done", "steps_done", "gen_init", "gen_step",
             "gen_stored", "route_ready", "out_ready", "xt_kept", "y_kept", "x1_bias", "token_in",
             "pool_sum", "xn_ready", "xt_ready", "start_ready", "got_in", "gen_dve", "gen_mm", "gen_idx",
             "gen_rows", "y_ready", "b2_ready", "yb_ready", "x1b_ready", "kvw_in", "weights_in",
             "gelu_done", "hid_ready", "var_ready", "std_ready", "turned", "h_biased", "kc_ready",
             "sq_used", "sq_ready", "kvar_ready", "kstd_ready", "scale_kept", "high_ready", "low_part",
             "sum_ready", "high_kept", "batch_done", "deg_ready", "stage_clear", "mix_done", "w2_done",
             "acc_turned", "at_ready", "var1_ready", "std1_ready", "y_turned", "norm_ready", "exp_in",
             "exp_out", "hid_done", "ffn_done", "var2_ready", "std2_ready", "dve_edge", "ones_set",
             "x1_mixed", "gen_added", "r_ready", "dve_w", "wkv_ready", "stats", "dve_norm", "hmax_ready",
             "h_done", "kv_done", "kvn_ready", "dve_kv", "kv_summed", "cmp_used", "cmp_ready",
             "code_turned", "dve_scale", "hmax_turned", "scale_ready", "scale_spread", "oh_ready",
             "split_ready", "kvbd_ready", "acc_done", "dve_deg", "deg_done", "raw_ready", "dve_flag",
             "m1_done", "m1_ready", "flag_part", "g_done", "g_ready", "flag_sum", "flag_ready", "gen_add",
             "gen_onehot", "gen_batch", "gen_end", "acc_in", "out_done", "x1_ready", "dve_last",
             "yt_ready", "dve_route", "mean_ready", "logits_done", "route_spread", "top_ready",
             "w2_scaled", "stats2", "dve_out")
        S = names
        slot_out = [sem(f"slot_out{j}") for j in range(R)]
        slot_in = [sem(f"slot_in{j}") for j in range(R)]
        out_in = [sem(f"out_in{j}") for j in range(R)]
        x_in = [sem(f"x_in{r}") for r in range(ROUNDS)]
        w1_in = [sem(f"w1_in{e}") for e in range(2)]
        w2_in = [sem(f"w2_in{e}") for e in range(2)]

        block = ctx.enter_context(nc.Block())
        rounds_view = lambda ap: ap.rearrange("(t p) f -> p t f", p=P)
        x_v, out_v, term_v = rounds_view(a["x"]), rounds_view(out), rounds_view(term_dram)

        def row(ap, parts, n):
            return bass.AP(ap.tensor, 0, [[0, parts], [1, n]])

        def apart(eng):
            eng.sem_inc(S["waited"], 1)

        def after(eng, sem, value):
            if not isinstance(value, int) or value > 0:
                eng.wait_ge(sem, value)

        def some(n):
            return not isinstance(n, int) or n >= 0

        def lies(n):
            return not isinstance(n, int) or n < T

        def some_later(n):
            return not isinstance(n, int) or n > 0

        def back(j):
            return 2 if j == 0 else 1

        @block.sync
        def _(sp):
            for j in range(R):
                sp.sem_inc(slot_out[j], 16)
                sp.sem_inc(out_in[j], 16)
            sp.wait_ge(S["pad_set"], 2)
            for lst, name in ((di, "dst"), (si, "src")):
                src = a[name]
                sp.dma_start(lst[0:FULLP, :], bass.AP(src.tensor, 0, [[EC, FULLP], [1, ECH]])).then_inc(S["edges_in"], 16)
                for p in range(FULLP, 128):
                    n = E - EC * p
                    sp.dma_start(lst[p:p + 1, 0:n], bass.AP(src.tensor, EC * p, [[n, 1], [1, n]])).then_inc(S["edges_in"], 16)
            sp.dma_start(cst[:, :], a["const"][:, 0:C_GRP]).then_inc(S["const_in"], 16)
            sp.dma_start(grp, a["const"][:, C_GRP:C_NODE]).then_inc(S["const_in"], 16)
            for r in range(ROUNDS):
                sp.dma_start(x1[:, R * r:R * r + R, :], x_v[:, R * r:R * r + R, :]).then_inc(x_in[r], 16)
            sp.wait_ge(S["code_ready"], 1)
            c0 = code[:, :]
            sp.dma_start(windows.rearrange("(p s) e -> p s e", p=128),
                         bass.AP(c0.tensor, c0.offset, [list(c0.ap[0]), [AL, NS], [1, W]])).then_inc(S["windows_out"], 16)
            sp.wait_ge(S["silu_done"], 2 + T)
            sp.dma_start(term_v, acc[:, :, :]).then_inc(S["h_kept"], 16)
            with sp.Fori(0, ROUNDS) as i:
                for j in range(R):
                    sp.wait_ge(S["batch_out"], 4 + NB * R * i + NB * (j + 1))
                    sp.dma_start(counts[bass.ds(R * i + j, 1), :, :].rearrange("o p m -> p (o m)"),
                                 stage[0:P, j, :]).then_inc(slot_out[j], 16)

            def load(k, i, j):
                sp.wait_ge(S["tile_done"], T * k + R * i + j - R + 1)
                apart(sp)
                sp.dma_start(stage[0:P, j, :],
                             counts[bass.ds(R * i + j, 1), :, :].rearrange("o p m -> p (o m)")).then_inc(slot_in[j], 16)

            for j in range(R):
                sp.wait_ge(slot_out[j], 16 + 16 * ROUNDS)
            sp.wait_ge(S["or_done"], T)
            with sp.Fori(1, STEPS - 1) as k:
                with sp.Fori(0, ROUNDS) as i:
                    for j in range(R):
                        load(k, i, j)
            for j in range(R):
                load(STEPS - 1, 0, j)

            sp.wait_ge(S["steps_done"], 1)
            bad = sp.value_load(small_i[0:1, 0:1], min_val=0, max_val=1)
            with sp.If(bad == 1):
                sp.dma_start(src_all, a["src"].rearrange("(p e) -> p e", p=P)).then_inc(S["gen_init"], 16)
                sp.dma_start(dst_all, a["dst"].rearrange("(p e) -> p e", p=P)).then_inc(S["gen_init"], 16)
                sp.dma_start(node_row, a["const"][0:P, C_NODE:C_END]).then_inc(S["gen_init"], 16)
                sp.wait_ge(S["h_kept"], 16)
                sp.dma_start(acc[:, :, :], term_v).then_inc(S["gen_init"], 16)
                with sp.Fori(0, STEPS) as k:
                    sp.wait_ge(S["gen_step"], k + 1)
                    sp.dma_start(term_v, sums[:, :, 0:D]).then_inc(S["gen_stored"], 16)
                sp.wait_ge(S["gen_stored"], 16 * STEPS)
            with sp.Else():
                pass
            with sp.Fori(1, ROUNDS) as i:
                for j in range(R):
                    load(STEPS - 1, i, j)

            sp.wait_ge(S["route_ready"], 1)
            for e in range(2):
                x = sp.value_load(small_i[0:1, 2 + e:3 + e], min_val=0, max_val=NX - 1)
                sp.dma_start(w1e[:, e, :, :], a["e_w1"][bass.ds(x, 1), :, :, :].rearrange("o k p f -> p (o k) f")).then_inc(w1_in[e], 16)
                sp.dma_start(b1e[:, e, :], a["e_b1"][bass.ds(x, 1), :, :].rearrange("o p m -> p (o m)")).then_inc(w1_in[e], 16)
                sp.dma_start(w2e[:, e, :, :], a["e_w2"][bass.ds(x, 1), :, :, :].rearrange("o k p f -> p (o k) f")).then_inc(w2_in[e], 16)
                sp.dma_start(b2e[:, e, :], a["e_b2"][bass.ds(x, 1), :].to_broadcast([P, D])).then_inc(w2_in[e], 16)

            with sp.Fori(0, ROUNDS) as i:
                for j in range(R):
                    sp.wait_ge(S["out_ready"], R + R * i + j + 1)
                    sp.dma_start(out_v[:, bass.ds(R * i + j, 1), :].rearrange("p o f -> p (o f)"),
                                 fin[:, j, :]).then_inc(out_in[j], 16)
            for j in range(R):
                sp.wait_ge(out_in[j], 16 + 16 * ROUNDS)
            sp.wait_ge(S["h_kept"], 16)

        @block.gpsimd
        def _(pool):
            pool.memset(di[:, :], PAD).then_inc(S["pad_set"], 1)
            pool.memset(si[:, :], 0).then_inc(S["pad_set"], 1)
            for k in range(STEPS):
                f = float(np.prod(np.arange(1, k + 2)))
                pool.memset(invf[:, k:k + 1], 1.0 / f).then_inc(S["pad_set"], 1)
            pool.sem_inc(S["xt_kept"], R)
            pool.sem_inc(S["y_kept"], R)
            pool.sem_inc(S["x1_bias"], 1)
            pool.wait_ge(S["token_in"], 16 * 4)
            b_sum = b_add[:, 0, :]
            pool.tensor_tensor(b_sum, b_add[:, 0, :], b_add[:, 1, :], ALU.add).then_inc(S["pool_sum"], 1)
            pool.wait_ge(S["pool_sum"], 1)

            def token_round(i):
                for j in range(R):
                    n = R * i + j
                    pool.wait_ge(S["xn_ready"], n + 1)
                    pool.wait_ge(S["x1_bias"], n + 1)
                    pool.tensor_tensor(pool_t, xn[:, j, :], b_sum, ALU.add).then_inc(S["pool_sum"], 1)
                    pool.wait_ge(S["pool_sum"], n + 2)
                    xr = x1[:, bass.ds(n, 1), :].rearrange("p o f -> p (o f)")
                    pool.tensor_tensor(xr, xr, pool_t, ALU.add).then_inc(S["x1_bias"], 1)
                    pool.wait_ge(S["xt_ready"], 1 + n + 1)
                    pool.tensor_copy(xt_all[:, :, bass.ds(P * n, P)], xt[:, j, :, :]).then_inc(S["xt_kept"], 1)

            token_round(0)
            pool.wait_ge(S["start_ready"], 1)
            pool.wait_ge(S["windows_out"], 16)
            for t in range(GT):
                pool.indirect_dma_start(got[:, t, :], None, windows[:, :],
                                        bass.IndirectOffsetOnAxis(ap=start_i[:, t:t + 1], axis=0)).then_inc(S["got_in"], 16)
            with pool.Fori(1, ROUNDS) as i:
                token_round(i)

            pool.wait_ge(S["steps_done"], 1)
            bad = pool.value_load(small_i[0:1, 0:1], min_val=0, max_val=1)
            with pool.If(bad == 1):
                pool.wait_ge(S["gen_init"], 64)
                with pool.Fori(0, STEPS) as k:
                    pool.wait_ge(S["gen_dve"], k + 1)
                    apart(pool)
                    with pool.Fori(0, EP) as e:
                        n = EP * k + e
                        pool.wait_ge(S["gen_mm"], n + 1)
                        pool.tensor_copy(idx_g, src_all[:, bass.ds(e, 1)]).then_inc(S["gen_idx"], 1)
                        pool.wait_ge(S["gen_idx"], n + 1)
                        apart(pool)
                        pool.indirect_dma_start(rows[:, 0:D], None, term_dram[:, :],
                                                bass.IndirectOffsetOnAxis(ap=idx_g, axis=0)).then_inc(S["gen_rows"], 16)
            with pool.Else():
                pass

            with pool.Fori(0, ROUNDS) as i:
                for j in range(R):
                    n = R * i + j
                    pool.wait_ge(S["y_ready"], n + 1)
                    pool.tensor_copy(acc[:, bass.ds(n, 1), :].rearrange("p o f -> p (o f)"), y_in[:, j, :]).then_inc(S["y_kept"], 1)
            pool.wait_ge(S["b2_ready"], 1)
            with pool.Fori(0, ROUNDS) as i:
                for j in range(R):
                    n = R * i + j
                    pool.wait_ge(S["out_ready"], n + 1)
                    pool.tensor_tensor(yb[:, j, :], acc[:, bass.ds(n, 1), :].rearrange("p o f -> p (o f)"),
                                       b2e[:, 0, :], ALU.add).then_inc(S["yb_ready"], 1)
                    pool.tensor_tensor(x1b[:, j, :], x1[:, bass.ds(n, 1), :].rearrange("p o f -> p (o f)"),
                                       gam[:, 1, :], ALU.add).then_inc(S["x1b_ready"], 1)

        @block.scalar
        def _(act):
            act.dma_start(w_kv[:, 0:KC, :], a["w_kv"].rearrange("(k p) f -> p k f", p=128)).then_inc(S["kvw_in"], 16)
            act.dma_start(w_kv[:, KC, :], row(a["b_kv"], 128, 2 * D)).then_inc(S["kvw_in"], 16)
            for dst, src in ((w_in[:, :, :], a["w_in_t"].rearrange("(k p) f -> p k f", p=128)),
                             (b_in[:, :], row(a["b_in"], P, D)),
                             (b_add[:, 0, :], row(a["b_out"], P, D)),
                             (b_add[:, 1, :], row(a["b2"], P, D))):
                act.dma_start(dst, src).then_inc(S["token_in"], 16)
            loads = 0
            for dst, src in ((wq_t[:, :, :], a["w_q_t"].rearrange("(k p) f -> p k f", p=128)),
                             (w1[:, :, :], a["w1"].rearrange("(k p) f -> p k f", p=128)),
                             (b1c[:, :], a["b1"]),
                             (lnrow[:, 0, :], row(a["vln_g"], 128, D)),
                             (lnrow[:, 1, :], row(a["vln_b"], 128, D)),
                             (lncol[:, :], a["kln"]),
                             (w2[:, :, :], a["w2"].rearrange("(k p) f -> p k f", p=128)),
                             (w_out[:, :, :], a["w_out_t"].rearrange("(k p) f -> p k f", p=128)),
                             (wr[:, :, :], a["wr"].rearrange("(k p) f -> p k f", p=128)),
                             (br[:, :], row(a["br"], 1, NX)),
                             (gam[:, 0, :], row(a["gamma"], P, D)),
                             (gam[:, 1, :], row(a["beta"], P, D))):
                act.dma_start(dst, src).then_inc(S["weights_in"], 16)
                loads += 1
            assert loads == N_WEIGHTS
            act.sem_inc(S["xt_ready"], 1)
            act.sem_inc(S["silu_done"], 2)
            act.sem_inc(S["batch_out"], 4)
            act.sem_inc(S["gelu_done"], KC)
            act.sem_inc(S["hid_ready"], 2)
            act.wait_ge(S["var_ready"], 1)
            act.activation(lnu[:, :], lnt[:, :], ACT.Sqrt).then_inc(S["std_ready"], 1)

            def token_round(i):
                for j in range(R):
                    n = R * i + j
                    act.wait_ge(S["turned"], n + 1)
                    act.wait_ge(S["xt_kept"], n + 1)
                    act.activation(xt[:, j, :, :], banks(4)[:, 0:256].rearrange("p (k m) -> p k m", k=KC)[:, :, 0:P],
                                   ACT.Copy).then_inc(S["xt_ready"], 1)
                    act.wait_ge(S["h_biased"], 1 + n + 1)
                    act.activation(acc[:, bass.ds(n, 1), :].rearrange("p o f -> p (o f)"), h_pre[:, j % 2, :],
                                   ACT.Silu).then_inc(S["silu_done"], 1)
                    act.wait_ge(S["kc_ready"], 2 + n + 1)
                    act.wait_ge(S["sq_used"], n + back(j))
                    act.activation(sq[:, j % 2, :], kc[:, j, :], ACT.Square).then_inc(S["sq_ready"], 1)
                act.wait_ge(S["kvar_ready"], i + 1)
                act.activation(kvar[:, :], kvar[:, :], ACT.Sqrt).then_inc(S["kstd_ready"], 1)

            with act.Fori(0, ROUNDS) as i:
                token_round(i)

            act.wait_ge(S["scale_kept"], 1)
            with act.Fori(0, ROUNDS) as i:
                for j in range(R):
                    act.activation(u[0][:, bass.ds(R * i + j, 1), 0:D].rearrange("p o f -> p (o f)"),
                                   acc[:, bass.ds(R * i + j, 1), :].rearrange("p o f -> p (o f)"),
                                   ACT.Copy, scale=scale2[0:P, 0:1]).then_inc(S["high_ready"], 1)

            def low(n, at, j):
                act.wait_ge(S["tile_done"], n + 1)
                act.activation(lo_part[:, j, :], banks(j % 3)[0:P, D:2 * D], ACT.Copy,
                               scale=deg[0:P, bass.ds(at, 1)]).then_inc(S["low_part"], 1)

            def high(n, at, j, to):
                act.wait_ge(S["sum_ready"], 2 + n + 1)
                act.activation(u[to][:, bass.ds(at, 1), 0:D].rearrange("p o f -> p (o f)"),
                               u_sum[:, j, :], ACT.Copy).then_inc(S["high_kept"], 1)

            def count_tile(i, j):
                n = R * i + j
                act.wait_ge(slot_out[j], 16 * i + 16)
                after(act, S["tile_done"], n - R + 1)
                after(act, S["or_done"], n - R + 1)
                for b, size in enumerate(BATCHES):
                    g = sum(BATCHES[:b])
                    act.wait_ge(S["batch_done"], NB + NB * n + b + 1)
                    apart(act)
                    to = stage[0:P, j, :].bitcast(F8).rearrange("p (c m) -> p c m", c=T)
                    act.activation(to[:, :, GD * g:GD * (g + size)].rearrange("p c (s l) -> p s c l", l=GD),
                                   banks(4 + b % 4)[0:P, 0:size * P].rearrange("p (s c l) -> p s c l", s=size, l=GD),
                                   ACT.Copy, scale=0.125, saturate=False).then_inc(S["batch_out"], 1)

            def first_step(n, j):
                act.wait_ge(S["deg_ready"], 1 + n + 1)
                low(n, n, j)
                high(n, n, j, 1)

            act.wait_ge(S["stage_clear"], 1)
            for j in range(R):
                count_tile(0, j)
                if j:
                    first_step(j - 1, j - 1)
            with act.Fori(1, ROUNDS) as i:
                for j in range(R):
                    count_tile(i, j)
                    first_step(R * i + j - 1, (j - 1) % R)
            first_step(T - 1, R - 1)

            with act.Fori(0, ROUNDS) as i:
                for m in range(KC):
                    act.wait_ge(S["mix_done"], KC * i + m + 1)
                    if m == 0:
                        act.wait_ge(S["w2_done"], R * i + 1)
                    act.activation(hb[:, m, :], banks(2 * m, 2)[:, 0:R * P], ACT.Gelu,
                                   bias=bias1[:, m:m + 1]).then_inc(S["gelu_done"], 1)

            with act.Fori(0, (STEPS - 2) // 2) as it:
                for par in range(2):
                    with act.Fori(0, ROUNDS) as i:
                        for j in range(R):
                            n = T * (1 + par) + 2 * T * it + R * i + j
                            low(n, R * i + j, j)
                            high(n, R * i + j, j, par)

            def last_step(i, j, main):
                n = R * i + j
                if main:
                    low((STEPS - 1) * T + n, n, j)
                if some(n - 1) and lies(n - 1):
                    act.wait_ge(S["acc_turned"], n)
                    act.activation(at_t[:, (j - 1) % R, :, :], banks(5)[:, 0:256].rearrange("p (k m) -> p k m", k=KC)[:, :, 0:P],
                                   ACT.Copy).then_inc(S["at_ready"], 1)
                if some(n - 2) and lies(n - 2):
                    s = (j - 2) % R
                    act.wait_ge(S["var1_ready"], n - 1)
                    act.activation(lnu[:, s:s + 1], lnt[:, s:s + 1], ACT.Sqrt).then_inc(S["std1_ready"], 1)
                    act.wait_ge(S["y_kept"], n - 1)
                    act.wait_ge(S["y_turned"], n - 1)
                    act.wait_ge(S["norm_ready"], n - 1)
                    act.activation(y_in[:, s, :], x1[:, bass.ds(n - 2, 1), :].rearrange("p o f -> p (o f)"), ACT.Identity,
                                   bias=nmr[:, s:s + 1], scale=rstd[:, s:s + 1]).then_inc(S["y_ready"], 1)

            for j in range(R):
                last_step(0, j, True)
            with act.Fori(1, ROUNDS) as i:
                for j in range(R):
                    last_step(i, j, True)
            for j in range(LAG):
                last_step(ROUNDS, j, False)

            for k in range(3):
                act.wait_ge(S["exp_in"], k + 1)
                act.activation(small[0:1, 24:32], small[0:1, 16:24], ACT.Exp).then_inc(S["exp_out"], 1)

            for e in range(2):
                act.wait_ge(w1_in[e], 32)
            with act.Fori(0, ROUNDS) as i:
                for e in range(2):
                    for m in range(FM):
                        at = FM * e + m
                        act.wait_ge(S["hid_done"], 2 * FM * i + at + 1)
                        if at == 0:
                            act.wait_ge(S["ffn_done"], R * i + 1)
                        act.activation(hid[:, e, m, :], banks(2 * (at % 2), 2)[:, 0:R * P], ACT.Gelu,
                                       bias=b1e[:, e, m:m + 1]).then_inc(S["hid_ready"], 1)
                act.wait_ge(S["var2_ready"], i + 1)
                act.activation(lnu[:, 0:R], lnt[:, 0:R], ACT.Sqrt).then_inc(S["std2_ready"], 1)

        @block.vector
        def _(dve):
            def norm_front(link, s, t, v, count):
                link(dve.tensor_tensor(v, s[:, :, 1], s[:, :, 4], ALU.subtract))
                link(dve.tensor_tensor(v, v, v, ALU.mult))
                link(dve.tensor_tensor(t, s[:, :, 2], s[:, :, 5], ALU.add))
                link(dve.scalar_tensor_tensor(t, v, D / 4.0, t, ALU.mult, ALU.add))
                return dve.tensor_scalar(t, t, 1.0 / D, EPS, ALU.mult, ALU.add)

            def norm_back(link, s, v, m, r):
                link(dve.reciprocal(r, v))
                link(dve.tensor_tensor(m, s[:, :, 1], s[:, :, 4], ALU.add))
                link(dve.tensor_scalar(m, m, 0.5, None, ALU.mult))

            link = Links(dve, S["dve_edge"])
            dve.memset(ones[:, :], 1.0).then_inc(S["ones_set"], 1)
            dve.memset(ones16[:, :], 1.0).then_inc(S["ones_set"], 1)
            dve.memset(small[:, :], 0.0).then_inc(S["ones_set"], 1)
            dve.memset(zeros[:, :], 0.0).then_inc(S["ones_set"], 1)
            for name, c in (("h_biased", 1), ("kc_ready", 2), ("sq_used", 2), ("x1_mixed", R), ("sum_ready", 2), ("gen_added", 1), ("deg_ready", 1),
                            ("r_ready", R), ("out_ready", R)):
                dve.sem_inc(S[name], c)
            dve.wait_ge(S["edges_in"], 16 * 2 * (1 + 128 - FULLP))
            dve.scalar_tensor_tensor(code[:, :], si[:, :], 4096.0, di[:, :], ALU.mult, ALU.add).then_inc(S["code_ready"], 1)
            smp = di[:, 0:EC].rearrange("p (s l) -> p s l", l=AL)[:, :, 0]
            link(dve.tensor_scalar(gds[:, 0, :], smp, 1.0 / GD, -0.4, ALU.mult, ALU.add))
            link(dve.tensor_scalar(gds[:, 1, :], gds[:, 0, :], MAGIC, MAGIC, ALU.add, ALU.subtract))
            dve.wait_ge(S["const_in"], 32)
            link(dve.tensor_copy(grp16[:, :], grp))

            wlink = Links(dve, S["dve_w"])
            dve.wait_ge(S["kvw_in"], 32)
            wv = w_kv[:, :, :].rearrange("p k (g l) -> p (k g) l", l=HD)
            wlink(dve.tensor_reduce(wsum[:, :], wv, AX.X, ALU.add))
            wlink(dve.tensor_scalar(wsum[:, :], wsum[:, :], -1.0 / HD, None, ALU.mult))
            dve.tensor_tensor(wv, wv, wsum[:, :].rearrange("p (g o) -> p g o", o=1).to_broadcast([128, (KC + 1) * 2 * HEADS, HD]),
                              ALU.add).then_inc(S["wkv_ready"], 1)
            for r in range(ROUNDS):
                dve.wait_ge(x_in[r], 16)
                for j in range(R):
                    dve.bn_stats(st[:, R * r + j, :], x1[:, R * r + j, :]).then_inc(S["stats"], 1)
            dve.wait_ge(S["stats"], T)
            nlink = Links(dve, S["dve_norm"])
            norm_front(nlink, st, lnt[:, :], lnu[:, :], T).then_inc(S["var_ready"], 1)
            dve.wait_ge(S["wkv_ready"], 1)
            dve.wait_ge(S["std_ready"], 1)
            norm_back(nlink, st, lnu[:, :], mean[:, :], rstd[:, :])

            def normalize(n, j):
                dve.tensor_scalar(xn[:, j, :], x1[:, bass.ds(n, 1), :].rearrange("p o f -> p (o f)"),
                                  mean[:, bass.ds(n, 1)], rstd[:, bass.ds(n, 1)],
                                  ALU.subtract, ALU.mult).then_inc(S["xn_ready"], 1)

            def head_sums(n, j):
                dve.wait_ge(S["sq_ready"], n + 1)
                dve.tensor_reduce(kvar[:, 2 * HEADS * j:2 * HEADS * (j + 1)],
                                  sq[:, j % 2, :].rearrange("p (g l) -> p g l", l=HD), AX.X, ALU.add).then_inc(S["sq_used"], 1)
                dve.wait_ge(S["silu_done"], 2 + n + 1)
                dve.tensor_reduce(hmx[:, bass.ds(n, 1)], acc[:, bass.ds(n, 1), :].rearrange("p o f -> p (o f)"),
                                  AX.X, ALU.max).then_inc(S["hmax_ready"], 1)

            def token_round(i, last):
                for j in range(R):
                    n = R * i + j
                    dve.wait_ge(S["h_done"], n + 1)
                    dve.wait_ge(S["silu_done"], n + back(j))
                    dve.tensor_tensor(h_pre[:, j % 2, :], banks(5)[0:P, 0:D], b_in[:, :], ALU.add).then_inc(S["h_biased"], 1)
                    dve.wait_ge(S["kv_done"], n + 1)
                    after(dve, S["kvn_ready"], n - R + 1)
                    dve.tensor_tensor(kc[:, j, :], banks(6 + j % 2)[0:P, :], w_kv[0:P, KC, :], ALU.add).then_inc(S["kc_ready"], 1)
                    if not last:
                        dve.wait_ge(S["x1_bias"], 1 + n + 1)
                        dve.wait_ge(S["turned"], n + 1)
                        apart(dve)
                        normalize(n + R, j)
                    if j:
                        head_sums(n - 1, j - 1)
                head_sums(R * i + R - 1, R - 1)
                klink = Links(dve, S["dve_kv"], 2 * i)
                dve.wait_ge(S["sq_used"], 2 + R * i + R)
                dve.tensor_scalar(kvar[:, :], kvar[:, :], 1.0 / HD, EPS, ALU.mult, ALU.add).then_inc(S["kvar_ready"], 1)
                dve.wait_ge(S["kstd_ready"], i + 1)
                klink(dve.reciprocal(kvar[:, :], kvar[:, :]))
                klink(dve.tensor_copy(fl[:, 0:1], kvar[:, 0:1]))
                for j in range(R):
                    after(dve, S["kv_summed"], R * i + j - R + 1)
                    dve.tensor_tensor(kvn[:, j, :].rearrange("p (g l) -> p g l", l=HD),
                                      kc[:, j, :].rearrange("p (g l) -> p g l", l=HD),
                                      kvar[:, 2 * HEADS * j:2 * HEADS * (j + 1)].rearrange("p (g o) -> p g o", o=1)
                                      .to_broadcast([P, 2 * HEADS, HD]), ALU.mult).then_inc(S["kvn_ready"], 1)

            dve.wait_ge(S["token_in"], 16 * 4)
            for j in range(R):
                normalize(j, j)
            token_round(0, False)
            with dve.Fori(0, NS // SR) as i:
                for s in range(SR):
                    t = SR * i + s
                    dve.wait_ge(S["cmp_used"], t + 1)
                    dve.tensor_scalar(cmp[:, s, :], grp16[:, :], gds[:, 1, bass.ds(t, 1)], None,
                                      ALU.is_gt).then_inc(S["cmp_ready"], 1)
            dve.wait_ge(S["cmp_used"], SR + NS)
            dve.tensor_scalar(start_i[:, :], banks(0)[0:P, 0:GT], 1.0, 0.0, ALU.subtract, ALU.max).then_inc(S["start_ready"], 1)
            with dve.Fori(1, 3) as i:
                token_round(i, False)
            dve.wait_ge(S["code_turned"], GT)
            for b, at, n in ((3, 0, 4), (0, 4, 1)):
                link(dve.tensor_copy(e_int[:, 0, at * P:(at + n) * P].rearrange("p (t g) -> p t g", t=n),
                                     banks(b)[:, 0:n * 128].rearrange("p (t g) -> p t g", t=n)[:, :, 0:P]))
            link(dve.tensor_scalar(e_int[:, 1, :], e_int[:, 0, :], 12, None, ALU.logical_shift_right))
            link(dve.tensor_scalar(e_int[:, 2, :], e_int[:, 0, :], 4095, None, ALU.bitwise_and))
            src_i, dst_i = e_int[:, 1, :], e_int[:, 2, :]
            link(dve.tensor_scalar(e_f[:, 0, :], src_i, 1.0 / P, -0.496, ALU.mult, ALU.add))
            link(dve.tensor_scalar(e_f[:, 0, :], e_f[:, 0, :], MAGIC, MAGIC, ALU.add, ALU.subtract))
            link(dve.tensor_scalar(e_f[:, 1, :], dst_i, 1.0 / GD, -0.4, ALU.mult, ALU.add))
            link(dve.tensor_scalar(e_f[:, 1, :], e_f[:, 1, :], MAGIC, MAGIC, ALU.add, ALU.subtract))
            link(dve.scalar_tensor_tensor(eq[:, 1, :], e_f[:, 0, :], -float(P), src_i, ALU.mult, ALU.add))
            link(dve.scalar_tensor_tensor(e_f[:, 2, :], e_f[:, 0, :], float(GD), dst_i, ALU.mult, ALU.add))
            link(dve.scalar_tensor_tensor(e_f[:, 3, :], e_f[:, 1, :], 1000.0 - GD, e_f[:, 2, :], ALU.mult, ALU.add))
            link(dve.scalar_tensor_tensor(e_f[:, 3, :], grp, -1000.0, e_f[:, 3, :], ALU.mult, ALU.add))
            link(dve.tensor_scalar(eq[:, 0, :], e_f[:, 3, :], -1000.0, 1000.0, ALU.max, ALU.min))
            link(dve.tensor_copy(iota_g, cst[:, C_IOTA:C_GRP].rearrange("p (m o) -> p m o", o=1).to_broadcast([128, 128, HALVES[1]])))
            dve.memset(stage[:, :, :].rearrange("p r (c m) -> p (r c) m", m=128)[:, :, P:128], 0).then_inc(S["stage_clear"], 1)
            with dve.Fori(3, ROUNDS - 1) as i:
                token_round(i, False)
            token_round(ROUNDS - 1, True)

            slink = Links(dve, S["dve_scale"])
            dve.wait_ge(S["hmax_ready"], T)
            dve.tensor_reduce(hmx[:, T:T + 1], hmx[:, 0:T], AX.X, ALU.max).then_inc(S["hmax_ready"], 1)
            dve.wait_ge(S["hmax_turned"], 1)
            slink(dve.tensor_reduce(small[0:1, 0:1], banks(0)[0:1, 0:P], AX.X, ALU.max))
            slink(dve.tensor_scalar(small[0:1, 0:1], small[0:1, 0:1], 0.28, None, ALU.max))
            slink(dve.tensor_scalar(small[0:1, 1:2].bitcast(I32), small[0:1, 0:1].bitcast(I32), 0x7F800000, None, ALU.bitwise_and))
            slink(dve.reciprocal(small[0:1, 2:3], small[0:1, 1:2]))
            slink(dve.tensor_scalar(small[0:1, 2:3], small[0:1, 2:3], 2.0 ** 14, None, ALU.mult))
            dve.tensor_scalar(small[0:1, 3:4], small[0:1, 1:2], 2.0 ** -14, None, ALU.mult).then_inc(S["scale_ready"], 1)
            dve.wait_ge(S["scale_spread"], 1)
            dve.tensor_copy(scale2[:, :], banks(3)[:, 0:2]).then_inc(S["scale_kept"], 1)
            dve.wait_ge(S["scale_kept"], 1)
            dve.wait_ge(S["pad_set"], 2 + STEPS)
            slink(dve.tensor_scalar(coef[:, :], invf[:, :], scale2[:, 1:2], None, ALU.mult))

            def one_hots(n):
                for h in range(2):
                    size = HALVES[h]
                    dve.wait_ge(S["batch_done"], NB * n + (NB // 2) * (h + 1))
                    dve.tensor_tensor(
                        oh[h][:, :, :, 0:size],
                        iota_g[:, :, 0:size].rearrange("p (o m) g -> p o m g", o=1).to_broadcast([128, 2, 128, size]),
                        eq[:, :, bass.ds(GPT * n + HALVES[0] * h, size)].rearrange("p a (o g) -> p a o g", o=1)
                        .to_broadcast([128, 2, 128, size]), ALU.is_equal).then_inc(S["oh_ready"], 1)

            one_hots(0)
            with dve.Fori(0, ROUNDS) as i:
                for j in range(R):
                    n = R * i + j
                    dve.wait_ge(S["high_ready"], n + 1)
                    dve.scalar_tensor_tensor(u[0][:, bass.ds(n, 1), D:2 * D].rearrange("p o f -> p (o f)"),
                                             acc[:, bass.ds(n, 1), :].rearrange("p o f -> p (o f)"), scale2[0:P, 0:1],
                                             u[0][:, bass.ds(n, 1), 0:D].rearrange("p o f -> p (o f)"),
                                             ALU.mult, ALU.subtract).then_inc(S["split_ready"], 1)

            klink = Links(dve, S["dve_kv"], 2 * ROUNDS)
            dve.wait_ge(S["weights_in"], 16 * N_WEIGHTS)
            dve.wait_ge(S["kv_summed"], T)
            dve.wait_ge(S["xt_kept"], R + T)
            for c in range(KC):
                at = slice(128 * c, 128 * c + 128)
                gv, bv = lnrow[:, 0, at], lnrow[:, 1, at]
                if c:
                    dve.wait_ge(S["kvbd_ready"], c)
                klink(dve.tensor_copy(kvs[:, 2, 0:1], banks(2)[:, c:c + 1]))
                klink(dve.tensor_tensor(kvs[:, 0, :], banks(1)[:, at], gv, ALU.mult))
                klink(dve.scalar_tensor_tensor(kvs[:, 0, :], bv, kvs[:, 2, 0:1], kvs[:, 0, :], ALU.mult, ALU.add))
                klink(dve.tensor_tensor(kvs[:, 1, :], banks(1)[:, D + 128 * c:D + 128 * c + 128], gv, ALU.mult))
                klink(dve.scalar_tensor_tensor(kvs[:, 1, :], bv, float(N), kvs[:, 1, :], ALU.mult, ALU.add))
                klink(dve.tensor_scalar(kvs[:, 0, :], kvs[:, 0, :], lncol[:, 0:1], None, ALU.mult))
                klink(dve.scalar_tensor_tensor(kvs[:, 0, :], kvs[:, 1, :], lncol[:, 1:2], kvs[:, 0, :], ALU.mult, ALU.add))
                dve.scalar_tensor_tensor(kv_bd[:, c, :], kvs[:, 0, :], 1.0 / N, mask, ALU.mult, ALU.mult).then_inc(S["kvbd_ready"], 1)

            def new_term(n, at, j, k, to):
                nxt = u[to][:, bass.ds(at, 1), :].rearrange("p o f -> p (o f)")
                dve.wait_ge(S["low_part"], n + 1)
                dve.scalar_tensor_tensor(u_sum[:, j, :], banks(j % 3)[0:P, 0:D], deg[0:P, bass.ds(at, 1)],
                                         lo_part[:, j, :], ALU.mult, ALU.add).then_inc(S["sum_ready"], 1)
                dve.wait_ge(S["sum_ready"], 2 + n + 1)
                xa = acc[:, bass.ds(at, 1), :].rearrange("p o f -> p (o f)")
                dve.scalar_tensor_tensor(xa, u_sum[:, j, :], coef[0:P, bass.ds(k, 1)], xa,
                                         ALU.mult, ALU.add).then_inc(S["acc_done"], 1)
                dve.wait_ge(S["high_kept"], n + 1)
                dve.tensor_tensor(nxt[:, D:2 * D], u_sum[:, j, :], nxt[:, 0:D], ALU.subtract).then_inc(S["split_ready"], 1)

            def first_step(n, j):
                dlink = Links(dve, S["dve_deg"], 2 * n)
                dve.wait_ge(S["deg_done"], n + 1)
                dve.tensor_scalar(deg_raw[:, bass.ds(n, 1)], banks(3)[:, 0:1], 1.0, None, ALU.mult).then_inc(S["raw_ready"], 1)
                dlink(dve.tensor_scalar(deg_t[:, 0:1], banks(3)[:, 0:1], 0.125, None, ALU.max))
                dlink(dve.reciprocal(deg_t[:, 1:2], deg_t[:, 0:1]))
                dve.tensor_scalar(deg[:, bass.ds(n, 1)], deg_t[:, 1:2], 1.0, None, ALU.mult).then_inc(S["deg_ready"], 1)
                dve.wait_ge(S["batch_out"], 4 + NB * n + NB)
                dve.tensor_tensor(orr, orr, stage[0:P, j, :].bitcast(I32), ALU.bitwise_or).then_inc(S["or_done"], 1)
                dve.wait_ge(S["deg_ready"], 1 + n + 1)
                new_term(n, n, j, 0, 1)

            slink(dve.memset(orr, 0))
            dve.wait_ge(S["h_kept"], 16)
            for j in range(R):
                if j:
                    one_hots(j)
                if j >= 2:
                    first_step(j - 2, j - 2)
            with dve.Fori(1, ROUNDS) as i:
                for j in range(R):
                    one_hots(R * i + j)
                    first_step(R * i + j - 2, (j - 2) % R)
            for j in (R - 2, R - 1):
                first_step(R * (ROUNDS - 1) + j, j)

            flink = Links(dve, S["dve_flag"])
            dve.wait_ge(S["m1_done"], 1)
            for c in range(KC):
                klink(dve.tensor_copy(m1t[:, c, :], banks(5 + 2 * c)[:, 0:D + 1]))
            for c in range(KC):
                at = slice(128 * c, 128 * c + 128)
                dve.tensor_tensor(m1t[:, c, at], m1t[:, c, at], ident, ALU.add).then_inc(S["m1_ready"], 1)
            dve.wait_ge(S["or_done"], T)
            dve.wait_ge(S["raw_ready"], T)
            flink(dve.tensor_scalar(orr, orr, 0x40404040, None, ALU.bitwise_and))
            flink(dve.tensor_reduce(fl[:, 0:1], deg_raw[0:P, :], AX.X, ALU.add))
            dve.tensor_reduce(fl[:, 1:2], orr, AX.X, ALU.max).then_inc(S["flag_part"], 1)
            dve.wait_ge(S["g_done"], 1)
            for c in range(KC):
                dve.tensor_copy(g_sb[:, c, :], banks(6)[:, D * c:D * c + D]).then_inc(S["g_ready"], 1)
            dve.tensor_tensor(bias1[:, :], banks(5)[:, 0:KC], b1c[:, :], ALU.add).then_inc(S["g_ready"], 1)
            dve.wait_ge(S["flag_sum"], 1)
            flink(dve.tensor_scalar(small[0:1, 4:5], banks(4)[0:1, 0:1], E / 8.0, None, ALU.not_equal))
            flink(dve.tensor_scalar(small[0:1, 5:6], banks(4)[0:1, 1:2], 0.0, None, ALU.is_gt))
            dve.tensor_tensor(small_i[0:1, 0:1], small[0:1, 4:5], small[0:1, 5:6], ALU.max).then_inc(S["flag_ready"], 1)

            with dve.Fori(0, ROUNDS) as i:
                for j in range(R):
                    n = R * i + j
                    dve.wait_ge(S["w2_done"], 1 + n + 1)
                    xr = x1[:, bass.ds(n, 1), :].rearrange("p o f -> p (o f)")
                    dve.tensor_tensor(xr, xr, banks(4 + j % 4)[0:P, 0:D], ALU.add).then_inc(S["x1_mixed"], 1)

            with dve.Fori(0, (STEPS - 2) // 2) as it:
                for par in range(2):
                    with dve.Fori(0, ROUNDS) as i:
                        for j in range(R):
                            new_term(T * (1 + par) + 2 * T * it + R * i + j, R * i + j, j, 1 + 2 * it + par, par)
            dve.wait_ge(S["acc_done"], (STEPS - 1) * T)
            dve.wait_ge(S["flag_ready"], 1)
            dve.sem_inc(S["steps_done"], 1)

            bad = dve.value_load(small_i[0:1, 0:1], min_val=0, max_val=1)
            with dve.If(bad == 1):
                dve.wait_ge(S["gen_init"], 64)
                glink = Links(dve, S["gen_add"])
                glink(dve.memset(rows[:, D:D + 1], 1.0))
                glink(dve.tensor_copy(dst_f, dst_all))
                dve.sem_inc(S["gen_dve"], 1)
                with dve.Fori(0, STEPS) as k:
                    glink = Links(dve, S["gen_add"], 2 + 4 * k)
                    glink(dve.memset(sums[:, :, :], 0.0))
                    apart(dve)
                    with dve.Fori(0, EP) as e:
                        n = EP * k + e
                        dve.wait_ge(S["gen_mm"], n + 1)
                        dve.tensor_scalar(oh_g, node_row, dst_f[:, bass.ds(e, 1)], None, ALU.is_equal).then_inc(S["gen_onehot"], 1)
                        for b in range(T // R):
                            dve.wait_ge(S["gen_batch"], R * n + b + 1)
                            for s in range(R):
                                t = R * b + s
                                ins = dve.tensor_tensor(sums[:, t, :], sums[:, t, :], banks(s)[0:P, 0:D + 1], ALU.add)
                            ins.then_inc(S["gen_added"], 1)
                    dve.wait_ge(S["gen_added"], 1 + R * EP * k + R * EP)
                    glink(dve.tensor_scalar(rdeg, sums[:, :, D], 1.0, None, ALU.max))
                    glink(dve.reciprocal(rdeg, rdeg))
                    glink(dve.tensor_tensor(sums[:, :, 0:D], sums[:, :, 0:D],
                                            rdeg.rearrange("p (t o) -> p t o", o=1).to_broadcast([P, T, D]), ALU.mult))
                    dve.scalar_tensor_tensor(acc[:, :, :], sums[:, :, 0:D], invf[0:P, bass.ds(k, 1)], acc[:, :, :],
                                             ALU.mult, ALU.add).then_inc(S["gen_step"], 1)
                    dve.wait_ge(S["gen_step"], k + 1)
                    dve.wait_ge(S["gen_stored"], 16 * k + 16)
                    dve.sem_inc(S["gen_dve"], 1)
                dve.memset(big[0:P, T * D:2 * T * D], 0.0).then_inc(S["gen_end"], 1)
            with dve.Else():
                pass

            def last_step(i, j, main):
                n = R * i + j
                if main:
                    at = (STEPS - 1) * T + n
                    dve.wait_ge(S["low_part"], at + 1)
                    dve.scalar_tensor_tensor(u_sum[:, j, :], banks(j % 3)[0:P, 0:D], deg[0:P, bass.ds(n, 1)],
                                             lo_part[:, j, :], ALU.mult, ALU.add).then_inc(S["sum_ready"], 1)
                    dve.wait_ge(S["sum_ready"], 2 + at + 1)
                    after(dve, S["acc_turned"], n - R + 1)
                    dve.scalar_tensor_tensor(at_in[:, j, :], u_sum[:, j, :], coef[0:P, STEPS - 1:STEPS],
                                             acc[:, bass.ds(n, 1), :].rearrange("p o f -> p (o f)"),
                                             ALU.mult, ALU.add).then_inc(S["acc_in"], 1)
                if some(n - 2) and lies(n - 2):
                    s, m = (j - 2) % R, n - 2
                    dve.wait_ge(S["out_done"], m + 1)
                    xr = x1[:, bass.ds(m, 1), :].rearrange("p o f -> p (o f)")
                    dve.tensor_tensor(xr, xr, banks(6)[0:P, 0:D], ALU.add).then_inc(S["x1_ready"], 1)
                    dve.wait_ge(S["x1_ready"], m + 1)
                    slink = Links(dve, S["dve_last"], 3 * m)
                    apart(dve)
                    slink(dve.bn_stats(st[:, s, :], xr))
                    apart(dve)
                    slink(dve.bn_aggr(mv[:, :], st[:, s, :]))
                    dve.tensor_scalar(lnt[:, s:s + 1], mv[:, 1:2], EPS, None, ALU.add).then_inc(S["var1_ready"], 1)
                    dve.wait_ge(S["std1_ready"], m + 1)
                    slink(dve.reciprocal(rstd[:, s:s + 1], lnu[:, s:s + 1]))
                    dve.scalar_tensor_tensor(nmr[:, s:s + 1], mv[:, 0:1], -1.0, rstd[:, s:s + 1], ALU.mult, ALU.mult).then_inc(S["norm_ready"], 1)
                if some(n - 3) and lies(n - 3):
                    m = n - 3
                    dve.wait_ge(S["y_turned"], R + m + 1)
                    dve.tensor_copy(xt_all[:, :, bass.ds(P * m, P)],
                                    banks(7)[:, 0:256].rearrange("p (k m) -> p k m", k=KC)[:, :, 0:P]).then_inc(S["yt_ready"], 1)

            for j in range(R):
                last_step(0, j, True)
            with dve.Fori(1, ROUNDS) as i:
                for j in range(R):
                    last_step(i, j, True)
            for j in range(LAG):
                last_step(ROUNDS, j, False)

            rlink = Links(dve, S["dve_route"])
            dve.wait_ge(S["y_turned"], R + T)
            dve.tensor_scalar(meant[:, :], banks(3)[:, 0:KC], 1.0 / N, None, ALU.mult).then_inc(S["mean_ready"], 1)
            dve.wait_ge(S["logits_done"], 1)
            prob, low, ex = small[0:1, 8:16], small[0:1, 16:24], small[0:1, 24:32]
            top, rec = small[0:1, 48:56], small[0:1, 40:41]

            def softmax(times):
                rlink(dve.tensor_reduce(rec, prob, AX.X, ALU.max))
                dve.tensor_scalar(low, prob, rec, None, ALU.subtract).then_inc(S["exp_in"], 1)
                dve.wait_ge(S["exp_out"], times)
                rlink(dve.tensor_reduce(rec, ex, AX.X, ALU.add))
                rlink(dve.reciprocal(rec, rec))
                rlink(dve.tensor_scalar(prob, ex, rec, None, ALU.mult))

            rlink(dve.tensor_tensor(prob, banks(4)[0:1, 0:NX], br[:, :], ALU.add))
            softmax(1)
            rlink(dve.tensor_scalar(low, prob, float(N), None, ALU.mult))
            rlink(dve.reciprocal(low, low))
            rlink(dve.tensor_scalar(low, low, CAP, 1.0, ALU.mult, ALU.min))
            rlink(dve.tensor_tensor(prob, prob, low, ALU.mult))
            softmax(2)
            rlink(dve.max(top, prob))
            rlink(dve.max_index(idx_u[:, :], top, prob))
            rlink(dve.tensor_copy(small_i[0:1, 2:4], idx_u[0:1, 0:2]))
            dve.sem_inc(S["route_ready"], 1)
            dve.tensor_scalar(low, top, top[:, 0:1], None, ALU.subtract).then_inc(S["exp_in"], 1)
            dve.wait_ge(S["exp_out"], 3)
            rlink(dve.tensor_tensor(rec, ex[:, 0:1], ex[:, 1:2], ALU.add))
            rlink(dve.reciprocal(rec, rec))
            dve.tensor_scalar(small[0:1, 56:58], ex[:, 0:2], rec, None, ALU.mult).then_inc(S["route_spread"], 1)
            dve.wait_ge(S["top_ready"], 1)
            rlink(dve.tensor_copy(topw[:, :], banks(4)[:, 16:18]))
            for e in range(2):
                dve.wait_ge(w2_in[e], 32)
                dve.tensor_scalar(w2e[:, e, :, :], w2e[:, e, :, :], topw[:, e:e + 1], None, ALU.mult).then_inc(S["w2_scaled"], 1)
            rlink(dve.tensor_scalar(b2e[:, 0, :], b2e[:, 0, :], topw[0:P, 0:1], None, ALU.mult))
            dve.scalar_tensor_tensor(b2e[:, 0, :], b2e[:, 1, :], topw[0:P, 1:2], b2e[:, 0, :], ALU.mult, ALU.add).then_inc(S["b2_ready"], 1)

            with dve.Fori(0, ROUNDS) as i:
                for j in range(R):
                    n = R * i + j
                    dve.wait_ge(S["ffn_done"], 1 + n + 1)
                    dve.wait_ge(S["yb_ready"], n + 1)
                    dve.tensor_tensor(yb[:, j, :], yb[:, j, :], banks(4 + j % 4)[0:P, 0:D], ALU.add).then_inc(S["r_ready"], 1)
                    dve.wait_ge(S["r_ready"], R + n + 1)
                    dve.bn_stats(st[:, j, :], yb[:, j, :]).then_inc(S["stats2"], 1)
                dve.wait_ge(S["stats2"], R * i + R)
                olink = Links(dve, S["dve_out"], 17 * i)
                norm_front(olink, st[:, 0:R, :], lnt[:, 0:R], lnu[:, 0:R], R).then_inc(S["var2_ready"], 1)
                dve.wait_ge(S["std2_ready"], i + 1)
                norm_back(olink, st[:, 0:R, :], lnu[:, 0:R], mean[:, 0:R], rstd[:, 0:R])
                for j in range(R):
                    n = R * i + j
                    olink(dve.tensor_scalar(yb[:, j, :], yb[:, j, :], mean[:, j:j + 1], rstd[:, j:j + 1], ALU.subtract, ALU.mult))
                    dve.wait_ge(out_in[j], 16 * i + 16)
                    olink(dve.tensor_tensor(fin[:, j, :], yb[:, j, :], gam[:, 0, :], ALU.mult))
                    dve.wait_ge(S["x1b_ready"], n + 1)
                    dve.tensor_tensor(fin[:, j, :], fin[:, j, :], x1b[:, j, :], ALU.add).then_inc(S["out_ready"], 1)
                assert olink.n == 17

        @block.tensor
        def _(pe):
            mm = pe.matmul

            def clear(b, n):
                for at in range(0, n, 128):
                    m = min(128, n - at)
                    mm(banks(b)[:, at:at + m], zeros[0:1, :], zeros[0:1, 0:m], start=True, stop=True)

            def add(out, lhs, rhs):
                return mm(out, lhs, rhs, start=False, stop=False, skip_group_check=True)

            def turn(to, src):
                for c in range(KC):
                    ins = pe.transpose(to[:, 128 * c:128 * c + P], src[:, 128 * c:128 * c + 128], ident[0:P, 0:P])
                return ins

            for name, c in (("cmp_used", SR), ("batch_done", NB), ("w2_done", 1), ("y_turned", R), ("gen_mm", 1), ("ffn_done", 1)):
                pe.sem_inc(S[name], c)
            pe.wait_ge(S["const_in"], 32)
            pe.wait_ge(S["ones_set"], 4)
            clear(1, 512)
            clear(2, KC)
            pe.wait_ge(S["token_in"], 16 * 4)
            pe.wait_ge(S["wkv_ready"], 1)

            def turn_token(i, j):
                n = R * i + j
                pe.wait_ge(S["xn_ready"], n + 1)
                pe.wait_ge(S["xt_ready"], n + 1)
                turn(banks(4), xn[:, j, :]).then_inc(S["turned"], 1)

            def token_round(i):
                turn_token(i, 0)
                for j in range(R):
                    n = R * i + j
                    if j < R - 1:
                        turn_token(i, j + 1)
                    pe.wait_ge(S["xt_ready"], 1 + n + 1)
                    pe.wait_ge(S["h_biased"], n + 1)
                    for c in range(KC):
                        ins = mm(banks(5)[0:P, 0:D], xt[:, j, c, :], w_in[:, c, :],
                                 start=(c == 0), stop=(c == KC - 1))
                    ins.then_inc(S["h_done"], 1)
                    pe.wait_ge(S["kc_ready"], n + back(j))
                    for c in range(KC):
                        ins = mm(banks(6 + j % 2)[0:P, :], xt[:, j, c, :], w_kv[:, c, :], start=(c == 0), stop=(c == KC - 1))
                    ins.then_inc(S["kv_done"], 1)

            def head_products(i):
                for j in range(R):
                    pe.wait_ge(S["kvn_ready"], R * i + j + 1)
                    for c in range(KC):
                        kk = kvn[:, j, 128 * c:128 * c + 128]
                        add(banks(1)[:, 128 * c:128 * c + 128], kk, kvn[:, j, D + 128 * c:D + 128 * c + 128])
                        add(banks(2)[:, c:c + 1], kk, ones[0:P, 0:1])
                    add(banks(1)[:, D:2 * D], ones[0:P, :], kvn[:, j, D:2 * D]).then_inc(S["kv_summed"], 1)

            token_round(0)
            clear(0, GT)
            with pe.Fori(0, NS // SR) as i:
                for s in range(SR):
                    pe.wait_ge(S["cmp_ready"], SR * i + s + 1)
                    for t in range(GT):
                        ins = add(banks(0)[0:P, t:t + 1], cmp[:, s, P * t:P * t + P], ones16[:, :])
                    ins.then_inc(S["cmp_used"], 1)
            with pe.Fori(1, 3) as i:
                token_round(i)
                head_products(i - 1)
            pe.wait_ge(S["got_in"], 16 * GT)
            pe.wait_ge(S["start_ready"], 1)
            for t in range(GT):
                at = 128 * (t % 4)
                pe.transpose(banks(3 if t < 4 else 0)[:, at:at + P], got[:, t, :], ident[0:P, 0:P]).then_inc(S["code_turned"], 1)
            with pe.Fori(3, ROUNDS) as i:
                token_round(i)
                head_products(i - 1)
            head_products(ROUNDS - 1)

            pe.wait_ge(S["stage_clear"], 1)
            pe.wait_ge(S["hmax_ready"], T + 1)
            mm(banks(0)[0:1, 0:P], hmx[:, T:T + 1], ident[0:P, 0:P], start=True, stop=True).then_inc(S["hmax_turned"], 1)
            pe.wait_ge(S["scale_ready"], 1)
            mm(banks(3)[:, 0:2], ones[0:1, :], small[0:1, 2:4], start=True, stop=True).then_inc(S["scale_spread"], 1)
            pe.wait_ge(S["kc_ready"], 2 + T)
            pe.wait_ge(S["scale_kept"], 1)

            def products(n):
                for b, size in enumerate(BATCHES):
                    h = 2 * b // NB
                    if b % (NB // 2) == 0:
                        pe.wait_ge(S["oh_ready"], 2 * n + h + 1)
                    pe.wait_ge(S["batch_out"], NB * n + b + 1)
                    g = sum(BATCHES[:b]) - HALVES[0] * h
                    for s in range(size):
                        ins = mm(banks(4 + b % 4)[:, P * s:P * s + P], oh[h][:, 1, :, g + s], oh[h][:, 0, 0:P, g + s],
                                 start=True, stop=True)
                    ins.then_inc(S["batch_done"], 1)

            def first_step(n, j):
                pe.wait_ge(S["batch_out"], 4 + NB * n + NB)
                pe.wait_ge(S["deg_ready"], n + 1)
                apart(pe)
                for c in range(T):
                    ins = mm(banks(3)[:, 0:1], stage[0:P, j, 128 * c:128 * c + 128].bitcast(F8), ones16[0:P, :],
                             start=(c == 0), stop=(c == T - 1))
                ins.then_inc(S["deg_done"], 1)
                pe.wait_ge(S["sum_ready"], n + 1)
                apart(pe)
                for c in range(T):
                    if not some_later(n):
                        pe.wait_ge(S["split_ready"], c + 1)
                    ins = mm(banks(j % 3)[:, :], stage[0:P, j, 128 * c:128 * c + 128].bitcast(F8), u[0][:, c, :],
                             start=(c == 0), stop=(c == T - 1))
                ins.then_inc(S["tile_done"], 1)

            for j in range(R):
                products(j)
                if j == 1:
                    pe.wait_ge(S["kvbd_ready"], KC)
                if j:
                    first_step(j - 1, j - 1)
            with pe.Fori(1, ROUNDS) as i:
                for j in range(R):
                    products(R * i + j)
                    first_step(R * i + j - 1, (j - 1) % R)
            first_step(T - 1, R - 1)

            pe.wait_ge(S["batch_out"], 4 + NB * T)
            pe.wait_ge(S["weights_in"], 16 * N_WEIGHTS)
            for c in range(KC):
                ins = mm(banks(5 + 2 * c)[:, 0:D + 1], kv_bd[:, c, :], wq_t[:, c, :], start=True, stop=True)
            ins.then_inc(S["m1_done"], 1)
            pe.wait_ge(S["m1_ready"], KC)
            for m in range(KC):
                for c in range(KC):
                    mm(banks(6)[:, D * m:D * m + D], m1t[:, c, 128 * m:128 * m + 128], w1[:, c, :],
                       start=(c == 0), stop=(c == KC - 1))
            for m in range(KC):
                for c in range(KC):
                    ins = mm(banks(5)[:, m:m + 1], w1[:, c, 128 * m:128 * m + 128], m1t[:, c, D:D + 1],
                             start=(c == 0), stop=(c == KC - 1))
            ins.then_inc(S["g_done"], 1)
            pe.wait_ge(S["flag_part"], 1)
            mm(banks(4)[0:1, 0:2], ones[0:P, 0:1], fl[:, :], start=True, stop=True).then_inc(S["flag_sum"], 1)
            pe.wait_ge(S["flag_ready"], 1)
            pe.wait_ge(S["sum_ready"], 2 + T)
            pe.wait_ge(S["xt_kept"], R + T)

            def wide(b, lhs, i, c, k):
                for at, n in ((0, 512), (512, R * P - 512)):
                    ins = mm(banks(b, 2)[:, at:at + n], lhs, xt_all[:, c, bass.ds(R * P * i + at, n)],
                             start=(c == 0), stop=(c == k - 1))
                return ins

            def tile_bank(sem, i, j):
                last = 1 if j == 0 else 4 if j == 4 else 5
                pe.wait_ge(sem, R + R * i + j - last + 1)

            with pe.Fori(0, ROUNDS) as i:
                for m in range(KC):
                    pe.wait_ge(S["gelu_done"], KC * i + m + 1)
                    for c in range(KC):
                        ins = wide(2 * m, g_sb[:, c, 128 * m:128 * m + 128], i, c, KC)
                    ins.then_inc(S["mix_done"], 1)
                pe.wait_ge(S["gelu_done"], KC + KC * i + KC)
                for j in range(R):
                    tile_bank(S["x1_mixed"], i, j)
                    for c in range(KC):
                        ins = mm(banks(4 + j % 4)[0:P, 0:D], hb[:, c, P * j:P * j + P], w2[:, c, :],
                                 start=(c == 0), stop=(c == KC - 1))
                    ins.then_inc(S["w2_done"], 1)

            def diffuse(k, loads, i, j, src):
                n = T * k + R * i + j
                pe.wait_ge(slot_in[j], 16 * (loads + i + 1))
                pe.wait_ge(S["sum_ready"], n + 1)
                for c in range(T):
                    if j == 0 and c in (0, T - 2, T - 1):
                        pe.wait_ge(S["split_ready"], T * k + (T - 2 if c == 0 else c + 1))
                    if c in (0, T - 2, T - 1):
                        apart(pe)
                    ins = mm(banks(j % 3)[:, :], stage[0:P, j, 128 * c:128 * c + 128].bitcast(F8), u[src][:, c, :],
                             start=(c == 0), stop=(c == T - 1))
                ins.then_inc(S["tile_done"], 1)

            with pe.Fori(0, (STEPS - 2) // 2) as it:
                for par in range(2):
                    with pe.Fori(0, ROUNDS) as i:
                        for j in range(R):
                            diffuse(1 + par + 2 * it, ROUNDS * (2 * it + par), i, j, 1 - par)

            bad = pe.value_load(small_i[0:1, 0:1], min_val=0, max_val=1)
            with pe.If(bad == 1):
                with pe.Fori(0, STEPS) as k:
                    with pe.Fori(0, EP) as e:
                        n = EP * k + e
                        pe.wait_ge(S["gen_rows"], 16 * n + 16)
                        pe.wait_ge(S["gen_onehot"], n + 1)
                        for b in range(T // R):
                            pe.wait_ge(S["gen_added"], R * n + b + 1)
                            for s in range(R):
                                t = R * b + s
                                ins = mm(banks(s)[0:P, 0:D + 1], oh_g[:, P * t:P * t + P], rows, start=True, stop=True)
                            ins.then_inc(S["gen_batch"], 1)
                        pe.wait_ge(S["gen_batch"], R * n + R)
                        pe.sem_inc(S["gen_mm"], 1)
                pe.wait_ge(S["gen_end"], 1)
            with pe.Else():
                pass

            def last_step(i, j, main):
                n = R * i + j
                if main:
                    diffuse(STEPS - 1, (STEPS - 2) * ROUNDS, i, j, 1)
                if some(n - 1) and lies(n - 1):
                    pe.wait_ge(S["acc_in"], n)
                    after(pe, S["at_ready"], n - 1)
                    turn(banks(5), at_in[:, (j - 1) % R, :]).then_inc(S["acc_turned"], 1)
                if some(n - 2) and lies(n - 2):
                    pe.wait_ge(S["at_ready"], n - 1)
                    after(pe, S["x1_ready"], n - 2)
                    for c in range(KC):
                        ins = mm(banks(6)[0:P, 0:D], at_t[:, (j - 2) % R, c, :], w_out[:, c, :], start=(c == 0), stop=(c == KC - 1))
                    ins.then_inc(S["out_done"], 1)
                if some(n - 3) and lies(n - 3):
                    y = y_in[:, (j - 3) % R, :]
                    pe.wait_ge(S["y_ready"], n - 2)
                    for c in range(KC):
                        add(banks(3)[:, c:c + 1], y[:, 128 * c:128 * c + 128], ones[0:P, 0:1])
                    after(pe, S["yt_ready"], n - 3)
                    turn(banks(7), y).then_inc(S["y_turned"], 1)

            pe.wait_ge(S["x1_mixed"], R + T)
            clear(3, KC)
            for j in range(R):
                last_step(0, j, True)
            with pe.Fori(1, ROUNDS) as i:
                for j in range(R):
                    last_step(i, j, True)
            for j in range(LAG):
                last_step(ROUNDS, j, False)

            pe.wait_ge(S["mean_ready"], 1)
            for c in range(KC):
                ins = mm(banks(4)[0:1, 0:NX], meant[:, c:c + 1], wr[:, c, :], start=(c == 0), stop=(c == KC - 1))
            ins.then_inc(S["logits_done"], 1)
            pe.wait_ge(S["route_spread"], 1)
            mm(banks(4)[:, 16:18], ones[0:1, :], small[0:1, 56:58], start=True, stop=True).then_inc(S["top_ready"], 1)

            pe.wait_ge(S["yt_ready"], T)
            pe.wait_ge(S["sum_ready"], 2 + STEPS * T)
            with pe.Fori(0, ROUNDS) as i:
                for e in range(2):
                    pe.wait_ge(w1_in[e], 32)
                    for m in range(FM):
                        at = FM * e + m
                        pe.wait_ge(S["hid_ready"], 2 * FM * i + at + 1)
                        for c in range(KC):
                            ins = wide(2 * (at % 2), w1e[:, e, c, 128 * m:128 * m + 128], i, c, KC)
                        ins.then_inc(S["hid_done"], 1)
                pe.wait_ge(S["w2_scaled"], 2)
                for j in range(R):
                    tile_bank(S["r_ready"], i, j)
                    for e in range(2):
                        for m in range(FM):
                            if j == 0:
                                pe.wait_ge(S["hid_ready"], 2 + 2 * FM * i + FM * e + m + 1)
                            ins = mm(banks(4 + j % 4)[0:P, 0:D], hid[:, e, m, P * j:P * j + P], w2e[:, e, m, :],
                                     start=(e == 0 and m == 0), stop=(e == 1 and m == FM - 1))
                    ins.then_inc(S["ffn_done"], 1)


def kernel(**inputs):
    import concourse.bacc as _bacc
    from concourse.bass_utils import run_bass_kernel_spmd as _run

    x = {k: np.ascontiguousarray(v) for k, v in inputs.items()}
    m = "L0_mix_"
    heads = x[m + "w_qkv"].reshape(D, HEADS, 3, HD)
    bias = x[m + "b_qkv"].reshape(HEADS, 3, HD)
    laid = {
        "x": x["x"], "src": x["src"], "dst": x["dst"], "const": constants(),
        "w_in_t": x["L0_gnn_W_in"].T, "b_in": x["L0_gnn_b_in"],
        "w_out_t": x["L0_gnn_W_out"].T, "b_out": x["L0_gnn_b_out"],
        "w_q_t": np.concatenate([heads[:, :, 0].reshape(D, D).T, bias[:, 0].reshape(D, 1)], axis=1),
        "w_kv": heads[:, :, 1:].transpose(0, 2, 1, 3).reshape(D, 2 * D),
        "b_kv": bias[:, 1:].transpose(1, 0, 2).reshape(2 * D),
        "kln": np.stack([np.tile(x[m + "kln_g"], 4), np.tile(x[m + "kln_b"], 4)], axis=1),
        "vln_g": np.tile(x[m + "vln_g"], HEADS), "vln_b": np.tile(x[m + "vln_b"], HEADS),
        "w1": x[m + "w1"], "b1": x[m + "b1"].reshape(KC, 128).T, "w2": x[m + "w2"], "b2": x[m + "b2"],
        "wr": x["L0_ffn_Wr"], "br": x["L0_ffn_br"],
        "e_w1": x["L0_ffn_W1"].reshape(NX, KC, 128, FF),
        "e_b1": x["L0_ffn_b1"].reshape(NX, FM, 128).transpose(0, 2, 1),
        "e_w2": x["L0_ffn_W2"].reshape(NX, FM, 128, D), "e_b2": x["L0_ffn_b2"],
        "gamma": x["L0_ffn_gamma"], "beta": x["L0_ffn_beta"],
    }
    nc = _bacc.Bacc("TRN2", target_bir_lowering=False, num_devices=1)
    arrays, a = {}, {}
    for name, v in laid.items():
        arrays["in_" + name] = np.ascontiguousarray(v)
        a[name] = nc.dram_tensor("in_" + name, v.shape, mybir.dt.from_np(v.dtype), kind="ExternalInput").ap()
    out = nc.dram_tensor("out_0", (N, D), F32, kind="ExternalOutput").ap()
    gps_kernel(nc, a, out)
    return _run(nc, [arrays], core_ids=[0]).results[0]["out_0"]
```

```python
import numpy as np

import concourse.bass as bass
from concourse import mybir
from contextlib import ExitStack

F32, F16, I32 = mybir.dt.float32, mybir.dt.float16, mybir.dt.int32
U8, F8 = mybir.dt.uint8, mybir.dt.float8e4
ACT, ALU, AX = mybir.ActivationFunctionType, mybir.AluOpType, mybir.AxisListType

N, D, E = 3125, 256, 53125
P = 125
T = N // P
R = 5
ROUNDS = T // R
KC = D // 128
HEADS, HD = 8, 32
STEPS = 6
EPS = 1e-5
NX, FF = 8, 512
FM = FF // 128
CAP = float(-(-(N * 125) // (NX * 100)))

GD = 5
G = N // GD
GT = G // P
GPT = P // GD
W = 128
AL = 8
EC = 416
ECH = EC + W - AL
NS = EC // AL
PAD = 4095
FULLP = (E - ECH) // EC + 1
HALVES = (GPT // 2, GPT - GPT // 2)
BATCHES = [3] * 7 + [4]
NB = len(BATCHES)
SAMPLES = (5, 5, 5, 5, 6)
assert 2 * sum(SAMPLES) == NS
REST = G - 512
N_WEIGHTS = 12
MAGIC = 12582912.0
Y_SCALE = 2.0 ** 11
TINY = 2.0 ** -60
LAG = 3

C_ID, C_MASK, C_IOTA, C_GRP, C_NODE, C_END = np.cumsum([0, 128, 128, 128, G, N]).tolist()


def constants():
    c = np.zeros((128, C_END), np.float32)
    c[:, C_ID:C_MASK] = np.eye(128)
    c[:, C_MASK:C_IOTA] = np.kron(np.eye(4), np.ones((32, 32)))
    c[:, C_IOTA:C_GRP] = np.arange(128)
    c[:, C_GRP:C_NODE] = np.arange(G)
    c[:, C_NODE:C_END] = np.arange(N)
    return c


class Links:

    def __init__(self, eng, sem, base=0):
        self.eng, self.sem, self.base, self.n = eng, sem, base, 0

    def __call__(self, ins):
        self.n += 1
        ins.then_inc(self.sem, 1)
        self.eng.wait_ge(self.sem, self.base + self.n)


def gps_kernel(nc, a, out):
    ctx = ExitStack()
    with ctx:
        def sb(name, shape, dt=F32):
            return ctx.enter_context(nc.sbuf_tensor(name, shape, dt))

        def dram(name, shape, dt=F32):
            return nc.dram_tensor(name, shape, dt, kind="Internal").ap()

        def sem(name):
            return ctx.enter_context(nc.semaphore(name))

        windows = dram("windows", (128 * NS, W))
        counts = dram("counts", (T, P, T * 128), U8)
        term_dram = dram("term_dram", (N, D))

        cst = sb("cst", [128, C_GRP])
        ident, mask = cst[:, C_ID:C_MASK], cst[:, C_MASK:C_IOTA]
        x1 = sb("x1", [P, T, D])
        acc = sb("acc", [P, T, D])
        xt_all = sb("xt_all", [128, KC, N])
        big = sb("big", [128, 2 * T * D])
        u = [big[0:P, s * T * D:(s + 1) * T * D].bitcast(F16).rearrange("p (t f) -> p t f", t=T)
             for s in range(2)]
        h_pre = big[0:P, 0:2 * D].rearrange("p (r f) -> p r f", r=2)
        sq = big[0:P, 2 * D:6 * D].rearrange("p (r f) -> p r f", r=2)
        kc = big[0:P, T * D:T * D + 2 * R * D].rearrange("p (r f) -> p r f", r=R)
        kvn = big[0:P, T * D + 2 * R * D:T * D + 2 * R * D + R * 2 * KC * 129].rearrange("p (r b f) -> p r b f", r=R, b=2 * KC)
        w_in = sb("w_in", [128, KC, D])
        w_out = sb("w_out", [128, KC, D])
        wq_t = sb("wq_t", [128, KC, D + 1])
        w_kv = sb("w_kv", [128, KC + 1, 2 * D])
        w1 = sb("w1", [128, KC, D])
        w2 = sb("w2", [128, KC, D])
        wr = sb("wr", [128, KC, NX])
        b_in = sb("b_in", [P, D])
        b_add = sb("b_add", [P, 2, D])
        gam = sb("gam", [P, 2, D])
        lnrow = sb("lnrow", [128, 2, D])
        lncol = sb("lncol", [128, 2])
        b1c = sb("b1c", [128, KC])
        br = sb("br", [1, NX])
        ones = sb("ones", [128, 128])
        ones16 = sb("ones16", [128, 1], F16)
        st = sb("st", [P, T, 6])
        mean, rstd, nmr, lnt = (sb(n, [P, T]) for n in ("mean", "rstd", "nmr", "lnt"))
        lnu = sb("lnu", [P, T])
        deg = sb("deg", [128, T])
        deg_raw = sb("deg_raw", [128, T])
        ysum = sb("ysum", [128, KC, T])
        mv = sb("mv", [P, R, 2])
        scale2 = sb("scale2", [128, 2])
        coef = sb("coef", [128, STEPS])
        invf = sb("invf", [128, STEPS])
        zeros = sb("zeros", [1, 128])
        wsum = sb("wsum", [128, (KC + 1) * 2 * HEADS])
        kvar = sb("kvar", [P, R * 2 * HEADS])
        hmx = sb("hmx", [P, T + 1])
        small = sb("small", [1, 64])
        small_i = sb("small_i", [1, 16], I32)
        idx_u = sb("idx_u", [1, 8], mybir.dt.uint32)
        g_sb = sb("g_sb", [128, KC, D])
        bias1 = sb("bias1", [128, KC])
        fl = sb("fl", [P, 2])
        REGION = 13460
        region = sb("region", [128, REGION])

        def view(at, words, dt=F32, parts=128):
            assert at + words <= REGION
            v = region[0:parts, at:at + words]
            return v if dt == F32 else v.bitcast(dt)

        eq = view(0, 640, F16)[:, 0:2 * G].rearrange("p (a g) -> p a g", a=2)
        iota_g = view(640, 64 * HALVES[1], F16).rearrange("p (m g) -> p m g", m=128)
        OH = 640 + 64 * HALVES[1]
        oh = [view(OH + h * 128 * HALVES[1], 128 * HALVES[1], F16).rearrange("p (a m g) -> p a m g", a=2, m=128)
              for h in range(2)]
        STAGE = OH + 2 * 128 * HALVES[1]
        stage = view(STAGE, R * T * 32, U8).rearrange("p (r m) -> p r m", r=R)
        TOK = STAGE + R * T * 32
        grp = view(OH, G)
        got = view(OH + G, GT * W, F32, P).rearrange("p (t e) -> p t e", t=GT)
        start_i = view(OH + G + GT * W, GT, I32, P)
        at = OH + G + GT * W + GT
        di, si, code = view(at, ECH, I32), view(at + ECH, ECH, I32), view(at + 2 * ECH, ECH)
        gds = view(at + 3 * ECH, 2 * NS).rearrange("p (a s) -> p a s", a=2)
        grp16 = view(at + 3 * ECH + 2 * NS, 320, F16)[:, 0:G]
        cmp = view(at + 3 * ECH + 2 * NS + 320, max(SAMPLES) * 320, F16).rearrange("p (r g) -> p r g", r=max(SAMPLES))[:, :, 0:G]
        below = view(OH + G, G, F32, 1)
        e_int = view(at, 3 * G, I32).rearrange("p (a g) -> p a g", a=3)
        e_f = view(at + 3 * G, 4 * G).rearrange("p (a g) -> p a g", a=4)
        assert at + 7 * G <= TOK
        oh_l = view(at, GD * 320, F16).rearrange("p (d g) -> p d g", d=GD)[:, :, 0:G]
        local = view(at + GD * 320, 320, F16)[:, 0:G]
        assert at + (GD + 1) * 320 <= STAGE
        xn = view(TOK, R * D, F32, P).rearrange("p (r f) -> p r f", r=R)
        xt = view(TOK + R * D, R * KC * P).rearrange("p (r k m) -> p r k m", r=R, k=KC)
        deg_row = view(TOK + R * D + R * KC * P, (N + 1) // 2, F16, 1)[:, 0:N]
        pool_t = b_add[:, 1, :]
        hb = view(TOK, KC * R * P).rearrange("p (k m) -> p k m", k=KC)
        lo_part = view(TOK + 2080, R * D, F32, P).rearrange("p (r f) -> p r f", r=R)
        u_sum = view(TOK + 2080 + R * D, R * D, F32, P).rearrange("p (r f) -> p r f", r=R)
        at = TOK
        kvs = view(at, 3 * 128).rearrange("p (a f) -> p a f", a=3)
        kv_bd = view(at + 384, KC * 128).rearrange("p (k f) -> p k f", k=KC)
        m1t = view(at + 640, KC * (D + 1)).rearrange("p (k f) -> p k f", k=KC)
        orr = view(TOK + 1280, T * 32, I32, P)
        at_in = view(OH, R * D, F32, P).rearrange("p (r f) -> p r f", r=R)
        at_t = view(OH + R * D, R * KC * P).rearrange("p (r k m) -> p r k m", r=R, k=KC)
        y_in = view(0, R * D, F32, P).rearrange("p (r f) -> p r f", r=R)
        HID = FM * R * P
        hid_hi, hid_lo = (big[:, h * HID:(h + 1) * HID].bitcast(F16).rearrange("p (e m t) -> p e m t", e=2, m=FM)
                          for h in range(2))
        o1 = 2 * FM * R * P
        w1e = big[:, o1:o1 + 2 * KC * FF].rearrange("p (e k f) -> p e k f", e=2, k=KC)
        w2e = big[:, o1 + 2 * KC * FF:o1 + 2 * KC * FF + 2 * FM * D].rearrange("p (e m f) -> p e m f", e=2, m=FM)
        y_hi, y_lo = (xt_all[:, h, :].bitcast(F16).rearrange("p (k n) -> p k n", k=KC) for h in range(2))
        WORDS = 2 * KC * FF // 2
        o2 = o1 + 4 * WORDS
        w1_hi, w1_lo = (big[:, o2 + h * WORDS:o2 + (h + 1) * WORDS].bitcast(F16).rearrange("p (e k f) -> p e k f", e=2, k=KC)
                        for h in range(2))
        w2_hi, w2_lo = (big[:, o1 + h * WORDS:o1 + (h + 1) * WORDS].bitcast(F16).rearrange("p (e m f) -> p e m f", e=2, m=FM)
                        for h in range(2))
        o3 = o2 + 2 * WORDS
        gelu_out = big[:, o3:o3 + 2 * R * P].rearrange("p (s t) -> p s t", s=2)
        assert o3 + 2 * R * P <= 2 * T * D
        at = OH + 2 * R * D
        b1e = view(at, 2 * FM).rearrange("p (e m) -> p e m", e=2)
        b2e = view(at + 2 * FM, 2 * D, F32, P).rearrange("p (e f) -> p e f", e=2)
        topw = view(at + 2 * FM + 2 * D, 2)
        meant = view(at + 2 * FM + 2 * D + 2, KC)
        at += 2 * FM + 2 * D + 2 + KC
        biggest = view(at, 8)
        scale_row = view(at + 8, 8)
        scale3 = view(at + 16, 8)
        w2_top = view(at + 24, 2)
        assert at + 26 <= STAGE
        yb = view(OH + R * D, R * D, F32, P).rearrange("p (r f) -> p r f", r=R)
        fin = view(STAGE, R * D, F32, P).rearrange("p (r f) -> p r f", r=R)
        x1b = view(STAGE + R * D, R * D, F32, P).rearrange("p (r f) -> p r f", r=R)
        node_row = big[0:P, 0:N]
        oh_g = big[0:P, N:2 * N]
        sums = big[0:P, 2 * N:2 * N + T * (D + 1)].rearrange("p (t f) -> p t f", t=T)
        EP = E // P
        src_all = view(OH, EP, I32, P)
        dst_all = view(OH + EP, EP, I32, P)
        dst_f = view(OH + 2 * EP, EP, F32, P)
        idx_g = view(OH + 3 * EP, 1, I32, P)
        rdeg = view(OH + 3 * EP + 8, T, F32, P)
        rows = view(OH + 3 * EP + 40, D + 1, F32, P)

        ps = ctx.enter_context(nc.psum_tensor("ps", [128, 8, 512], F32))

        def banks(b, n=1):
            return ps[:, b:b + n, :].rearrange("p b c -> p (b c)")

        names = {}

        def sems(*each):
            for n in each:
                names[n] = sem(n)

        sems("waited", "cst_in", "pad_set", "edges_in", "const_in", "code_ready", "windows_out",
             "weights_in", "silu_done", "h_kept", "batch_out", "tile_done", "or_done", "steps_done",
             "gen_init", "gen_step", "gen_stored", "route_ready", "out_ready", "xt_kept", "y_kept",
             "pool_split", "x1_bias", "token_in", "pool_sum", "xn_ready", "xt_ready", "start_ready",
             "got_in", "scale_kept", "sq_used", "pool_high", "gen_dve", "gen_mm", "gen_idx", "gen_rows",
             "y_ready", "b2_ready", "yb_ready", "x1b_ready", "kvw_in", "gelu_done", "hid_ready",
             "var_ready", "std_ready", "turned", "h_biased", "kc_ready", "sq_ready", "kvar_ready",
             "kstd_ready", "row_done", "row_kept", "high_ready", "low_part", "sum_ready", "high_kept",
             "batch_done", "stage_clear", "deg_ready", "mix_done", "w2_done", "acc_turned", "at_ready",
             "var1_ready", "std1_ready", "y_turned", "norm_ready", "warmed", "exp_in", "exp_out",
             "scale3_ready", "halves_high", "hid_done", "hid_split", "ffn_done", "hid_high", "w2_scaled",
             "var2_ready", "std2_ready", "dve_chain", "ones_set", "wkv_ready",
             "stats", "hmax_ready", "cmp_used", "cmp_ready", "code_turned", "local_ready", "h_done",
             "kv_done", "kvn_ready", "dve_kv", "kv_summed", "below_ready", "rows_turned",
             "scale_products", "scale_ready", "oh_ready", "split_ready", "acc_done", "kvbd_ready",
             "matrix_products", "matrices_ready", "flag_part", "x1_mixed", "flag_sum", "flag_ready",
             "gen_add", "gen_onehot", "gen_batch", "gen_added", "gen_end", "acc_in", "out_done",
             "x1_ready", "dve_last", "y_summed", "y_high", "yt_ready", "route_row", "route_products",
             "scales_turned", "maxima_ready", "halves_low", "r_ready", "dve_out")
        S = names
        slot_out = [sem(f"slot_out{j}") for j in range(R)]
        slot_in = [sem(f"slot_in{j}") for j in range(R)]
        out_in = [sem(f"out_in{j}") for j in range(R)]
        x_in = [sem(f"x_in{r}") for r in range(ROUNDS)]
        w1_in = [sem(f"w1_in{e}") for e in range(2)]
        w2_in = [sem(f"w2_in{e}") for e in range(2)]

        block = ctx.enter_context(nc.Block())
        rounds_view = lambda ap: ap.rearrange("(t p) f -> p t f", p=P)
        x_v, out_v, term_v = rounds_view(a["x"]), rounds_view(out), rounds_view(term_dram)

        def row(ap, parts, n):
            return bass.AP(ap.tensor, 0, [[0, parts], [1, n]])

        def apart(eng):
            eng.sem_inc(S["waited"], 1)

        def after(eng, sem, value):
            if not isinstance(value, int) or value > 0:
                eng.wait_ge(sem, value)

        def some(n):
            return not isinstance(n, int) or n >= 0

        def lies(n):
            return not isinstance(n, int) or n < T

        def back(j):
            return 2 if j == 0 else 1

        @block.sync
        def _(sp):
            for j in range(R):
                sp.sem_inc(slot_out[j], 16)
                sp.sem_inc(out_in[j], 16)
            sp.dma_start(cst[:, :], a["const"][:, 0:C_GRP]).then_inc(S["cst_in"], 16)
            for r in range(ROUNDS):
                sp.dma_start(x1[:, R * r:R * r + R, :], x_v[:, R * r:R * r + R, :]).then_inc(x_in[r], 16)
            sp.wait_ge(S["pad_set"], 2)
            for lst, name in ((di, "dst"), (si, "src")):
                src = a[name]
                sp.dma_start(lst[0:FULLP, :], bass.AP(src.tensor, 0, [[EC, FULLP], [1, ECH]])).then_inc(S["edges_in"], 16)
                for p in range(FULLP, 128):
                    n = E - EC * p
                    sp.dma_start(lst[p:p + 1, 0:n], bass.AP(src.tensor, EC * p, [[n, 1], [1, n]])).then_inc(S["edges_in"], 16)
            sp.dma_start(grp, a["const"][:, C_GRP:C_NODE]).then_inc(S["const_in"], 16)
            sp.wait_ge(S["code_ready"], 1)
            c0 = code[:, :]
            sp.dma_start(windows.rearrange("(p s) e -> p s e", p=128),
                         bass.AP(c0.tensor, c0.offset, [list(c0.ap[0]), [AL, NS], [1, W]])).then_inc(S["windows_out"], 16)
            loads = 0
            for dst, src in ((wq_t[:, :, :], a["w_q_t"].rearrange("(k p) f -> p k f", p=128)),
                             (w1[:, :, :], a["w1"].rearrange("(k p) f -> p k f", p=128)),
                             (b1c[:, :], a["b1"]),
                             (lnrow[:, 0, :], row(a["vln_g"], 128, D)),
                             (lnrow[:, 1, :], row(a["vln_b"], 128, D)),
                             (lncol[:, :], a["kln"]),
                             (w2[:, :, :], a["w2"].rearrange("(k p) f -> p k f", p=128)),
                             (w_out[:, :, :], a["w_out_t"].rearrange("(k p) f -> p k f", p=128)),
                             (wr[:, :, :], a["wr"].rearrange("(k p) f -> p k f", p=128)),
                             (br[:, :], row(a["br"], 1, NX)),
                             (gam[:, 0, :], row(a["gamma"], P, D)),
                             (gam[:, 1, :], row(a["beta"], P, D))):
                sp.dma_start(dst, src).then_inc(S["weights_in"], 16)
                loads += 1
            assert loads == N_WEIGHTS
            sp.wait_ge(S["silu_done"], 2 + T)
            sp.dma_start(term_v, acc[:, :, :]).then_inc(S["h_kept"], 16)
            with sp.Fori(0, ROUNDS) as i:
                for j in range(R):
                    sp.wait_ge(S["batch_out"], 4 + NB * R * i + NB * (j + 1))
                    sp.dma_start(counts[bass.ds(R * i + j, 1), :, :].rearrange("o p m -> p (o m)"),
                                 stage[0:P, j, :]).then_inc(slot_out[j], 16)

            def load(k, i, j):
                sp.wait_ge(S["tile_done"], T * k + R * i + j - R + 1)
                apart(sp)
                sp.dma_start(stage[0:P, j, :],
                             counts[bass.ds(R * i + j, 1), :, :].rearrange("o p m -> p (o m)")).then_inc(slot_in[j], 16)

            for j in range(R):
                sp.wait_ge(slot_out[j], 16 + 16 * ROUNDS)
            sp.wait_ge(S["or_done"], T)
            with sp.Fori(1, STEPS - 1) as k:
                with sp.Fori(0, ROUNDS) as i:
                    for j in range(R):
                        load(k, i, j)
            for j in range(R):
                load(STEPS - 1, 0, j)

            sp.wait_ge(S["steps_done"], 1)
            bad = sp.value_load(small_i[0:1, 0:1], min_val=0, max_val=1)
            with sp.If(bad == 1):
                sp.dma_start(src_all, a["src"].rearrange("(p e) -> p e", p=P)).then_inc(S["gen_init"], 16)
                sp.dma_start(dst_all, a["dst"].rearrange("(p e) -> p e", p=P)).then_inc(S["gen_init"], 16)
                sp.dma_start(node_row, a["const"][0:P, C_NODE:C_END]).then_inc(S["gen_init"], 16)
                sp.wait_ge(S["h_kept"], 16)
                sp.dma_start(acc[:, :, :], term_v).then_inc(S["gen_init"], 16)
                with sp.Fori(0, STEPS) as k:
                    sp.wait_ge(S["gen_step"], k + 1)
                    sp.dma_start(term_v, sums[:, :, 0:D]).then_inc(S["gen_stored"], 16)
                sp.wait_ge(S["gen_stored"], 16 * STEPS)
            with sp.Else():
                pass
            with sp.Fori(1, ROUNDS) as i:
                for j in range(R):
                    load(STEPS - 1, i, j)

            sp.wait_ge(S["route_ready"], 1)
            chosen = [sp.value_load(small_i[0:1, 2 + e:3 + e], min_val=0, max_val=NX - 1) for e in range(2)]
            for e, x in enumerate(chosen):
                sp.dma_start(w1e[:, e, :, :], a["e_w1"][bass.ds(x, 1), :, :, :].rearrange("o k p f -> p (o k) f")).then_inc(w1_in[e], 16)
                sp.dma_start(b1e[:, e, :], a["e_b1"][bass.ds(x, 1), :, :].rearrange("o p m -> p (o m)")).then_inc(w1_in[e], 16)
            for e, x in enumerate(chosen):
                sp.dma_start(w2e[:, e, :, :], a["e_w2"][bass.ds(x, 1), :, :, :].rearrange("o k p f -> p (o k) f")).then_inc(w2_in[e], 16)
                sp.dma_start(b2e[:, e, :], a["e_b2"][bass.ds(x, 1), :].to_broadcast([P, D])).then_inc(w2_in[e], 16)

            with sp.Fori(0, ROUNDS) as i:
                for j in range(R):
                    sp.wait_ge(S["out_ready"], R + R * i + j + 1)
                    sp.dma_start(out_v[:, bass.ds(R * i + j, 1), :].rearrange("p o f -> p (o f)"),
                                 fin[:, j, :]).then_inc(out_in[j], 16)
            for j in range(R):
                sp.wait_ge(out_in[j], 16 + 16 * ROUNDS)
            sp.wait_ge(S["h_kept"], 16)

        @block.gpsimd
        def _(pool):
            pool.memset(di[:, :], PAD).then_inc(S["pad_set"], 1)
            pool.memset(si[:, :], 0).then_inc(S["pad_set"], 1)
            for k in range(STEPS):
                f = float(np.prod(np.arange(1, k + 2)))
                pool.memset(invf[:, k:k + 1], 1.0 / f).then_inc(S["pad_set"], 1)
            pool.sem_inc(S["xt_kept"], R)
            pool.sem_inc(S["y_kept"], R)
            pool.sem_inc(S["pool_split"], 1)
            pool.sem_inc(S["x1_bias"], 1)
            pool.wait_ge(S["token_in"], 16 * 4)
            b_sum = b_add[:, 0, :]
            pool.tensor_tensor(b_sum, b_add[:, 0, :], b_add[:, 1, :], ALU.add).then_inc(S["pool_sum"], 1)
            pool.wait_ge(S["pool_sum"], 1)

            def token_round(i):
                for j in range(R):
                    n = R * i + j
                    pool.wait_ge(S["xn_ready"], n + 1)
                    pool.wait_ge(S["x1_bias"], n + 1)
                    pool.tensor_tensor(pool_t, xn[:, j, :], b_sum, ALU.add).then_inc(S["pool_sum"], 1)
                    pool.wait_ge(S["pool_sum"], n + 2)
                    xr = x1[:, bass.ds(n, 1), :].rearrange("p o f -> p (o f)")
                    pool.tensor_tensor(xr, xr, pool_t, ALU.add).then_inc(S["x1_bias"], 1)
                    pool.wait_ge(S["xt_ready"], 1 + n + 1)
                    pool.tensor_copy(xt_all[:, :, bass.ds(P * n, P)], xt[:, j, :, :]).then_inc(S["xt_kept"], 1)

            with pool.Fori(0, 3) as i:
                token_round(i)
            pool.wait_ge(S["start_ready"], 1)
            pool.wait_ge(S["windows_out"], 16)
            for t in range(GT):
                pool.indirect_dma_start(got[:, t, :], None, windows[:, :],
                                        bass.IndirectOffsetOnAxis(ap=start_i[:, t:t + 1], axis=0)).then_inc(S["got_in"], 16)
            with pool.Fori(3, ROUNDS) as i:
                token_round(i)

            pool.wait_ge(S["scale_kept"], 1)
            pool.wait_ge(S["x1_bias"], 1 + T)
            pool.wait_ge(S["sq_used"], 2 + T)
            for i in range(ROUNDS):
                t = R * i + R - 1
                hi = u[0][:, t, 0:D]
                pool.wait_ge(S["pool_split"], i + 1)
                pool.tensor_scalar(pool_t, acc[:, t, :], scale2[0:P, 0:1], None, ALU.mult).then_inc(S["pool_high"], 1)
                pool.wait_ge(S["pool_high"], 2 * i + 1)
                pool.tensor_copy(hi, pool_t).then_inc(S["pool_high"], 1)
                pool.wait_ge(S["pool_high"], 2 * i + 2)
                pool.tensor_tensor(u[0][:, t, D:2 * D], pool_t, hi, ALU.subtract).then_inc(S["pool_split"], 1)

            pool.wait_ge(S["steps_done"], 1)
            bad = pool.value_load(small_i[0:1, 0:1], min_val=0, max_val=1)
            with pool.If(bad == 1):
                pool.wait_ge(S["gen_init"], 64)
                with pool.Fori(0, STEPS) as k:
                    pool.wait_ge(S["gen_dve"], k + 1)
                    apart(pool)
                    with pool.Fori(0, EP) as e:
                        n = EP * k + e
                        pool.wait_ge(S["gen_mm"], n + 1)
                        pool.tensor_copy(idx_g, src_all[:, bass.ds(e, 1)]).then_inc(S["gen_idx"], 1)
                        pool.wait_ge(S["gen_idx"], n + 1)
                        apart(pool)
                        pool.indirect_dma_start(rows[:, 0:D], None, term_dram[:, :],
                                                bass.IndirectOffsetOnAxis(ap=idx_g, axis=0)).then_inc(S["gen_rows"], 16)
            with pool.Else():
                pass

            with pool.Fori(0, ROUNDS) as i:
                for j in range(R):
                    n = R * i + j
                    pool.wait_ge(S["y_ready"], n + 1)
                    pool.tensor_copy(acc[:, bass.ds(n, 1), :].rearrange("p o f -> p (o f)"), y_in[:, j, :]).then_inc(S["y_kept"], 1)
            pool.wait_ge(S["b2_ready"], 1)
            with pool.Fori(0, ROUNDS) as i:
                for j in range(R):
                    n = R * i + j
                    pool.wait_ge(S["out_ready"], n + 1)
                    pool.tensor_tensor(yb[:, j, :], acc[:, bass.ds(n, 1), :].rearrange("p o f -> p (o f)"),
                                       b2e[:, 0, :], ALU.add).then_inc(S["yb_ready"], 1)
                    pool.tensor_tensor(x1b[:, j, :], x1[:, bass.ds(n, 1), :].rearrange("p o f -> p (o f)"),
                                       gam[:, 1, :], ALU.add).then_inc(S["x1b_ready"], 1)

        @block.scalar
        def _(act):
            act.dma_start(w_kv[:, 0:KC, :], a["w_kv"].rearrange("(k p) f -> p k f", p=128)).then_inc(S["kvw_in"], 16)
            act.dma_start(w_kv[:, KC, :], row(a["b_kv"], 128, 2 * D)).then_inc(S["kvw_in"], 16)
            for dst, src in ((w_in[:, :, :], a["w_in_t"].rearrange("(k p) f -> p k f", p=128)),
                             (b_in[:, :], row(a["b_in"], P, D)),
                             (b_add[:, 0, :], row(a["b_out"], P, D)),
                             (b_add[:, 1, :], row(a["b2"], P, D))):
                act.dma_start(dst, src).then_inc(S["token_in"], 16)
            act.sem_inc(S["xt_ready"], 1)
            act.sem_inc(S["silu_done"], 2)
            act.sem_inc(S["batch_out"], 4)
            act.sem_inc(S["gelu_done"], KC)
            act.sem_inc(S["hid_ready"], 2)
            act.wait_ge(S["var_ready"], 1)
            act.activation(lnu[:, 0:R], lnt[:, 0:R], ACT.Sqrt).then_inc(S["std_ready"], 1)

            def keep_turned(i, j):
                n = R * i + j
                act.wait_ge(S["turned"], n + 1)
                act.wait_ge(S["xt_kept"], n + 1)
                act.activation(xt[:, j, :, :], banks(4)[:, 0:256].rearrange("p (k m) -> p k m", k=KC)[:, :, 0:P],
                               ACT.Copy).then_inc(S["xt_ready"], 1)

            def token_round(i, first=False, last=False):
                for j in range(R):
                    n = R * i + j
                    if first and j == ROUNDS - 2:
                        act.wait_ge(S["var_ready"], 2)
                        act.activation(lnu[:, R:T], lnt[:, R:T], ACT.Sqrt).then_inc(S["std_ready"], 1)
                    if j < R - 1:
                        keep_turned(i, j + 1)
                    elif not last:
                        keep_turned(i + 1, 0)
                    act.wait_ge(S["h_biased"], 1 + n + 1)
                    act.activation(acc[:, bass.ds(n, 1), :].rearrange("p o f -> p (o f)"), h_pre[:, j % 2, :],
                                   ACT.Silu).then_inc(S["silu_done"], 1)
                    act.wait_ge(S["kc_ready"], 2 + n + 1)
                    act.wait_ge(S["sq_used"], n + back(j))
                    act.activation(sq[:, j % 2, :], kc[:, j, :], ACT.Square).then_inc(S["sq_ready"], 1)
                act.wait_ge(S["kvar_ready"], i + 1)
                act.activation(kvar[:, :], kvar[:, :], ACT.Sqrt).then_inc(S["kstd_ready"], 1)

            keep_turned(0, 0)
            token_round(0, first=True)
            with act.Fori(1, ROUNDS - 1) as i:
                token_round(i)
            token_round(ROUNDS - 1, last=True)

            of_place = deg_row.rearrange("p (g d) -> p d g", d=GD)
            for d in range(GD):
                act.wait_ge(S["row_done"], d + 1)
                act.activation(of_place[:, d, 0:512], banks(3 + d)[0:1, :], ACT.Copy).then_inc(S["row_kept"], 1)
            act.wait_ge(S["row_done"], GD + 1)
            act.activation(of_place[:, 0:GD - 1, 512:G], banks(0)[0:1, 0:REST * (GD - 1)].rearrange("p (d g) -> p d g", d=GD - 1),
                           ACT.Copy).then_inc(S["row_kept"], 1)
            act.activation(of_place[:, GD - 1, 512:G], banks(4)[0:1, 0:REST], ACT.Copy).then_inc(S["row_kept"], 1)

            act.wait_ge(S["scale_kept"], 1)
            act.wait_ge(S["sq_used"], 2 + T)
            with act.Fori(0, ROUNDS) as i:
                for j in range(R - 1):
                    act.activation(u[0][:, bass.ds(R * i + j, 1), 0:D].rearrange("p o f -> p (o f)"),
                                   acc[:, bass.ds(R * i + j, 1), :].rearrange("p o f -> p (o f)"),
                                   ACT.Copy, scale=scale2[0:P, 0:1]).then_inc(S["high_ready"], 1)

            def low(n, at, j):
                act.wait_ge(S["tile_done"], n + 1)
                act.activation(lo_part[:, j, :], banks(j % 3)[0:P, D:2 * D], ACT.Copy,
                               scale=deg[0:P, bass.ds(at, 1)]).then_inc(S["low_part"], 1)

            def high(n, at, j, to):
                act.wait_ge(S["sum_ready"], 2 + n + 1)
                act.activation(u[to][:, bass.ds(at, 1), 0:D].rearrange("p o f -> p (o f)"),
                               u_sum[:, j, :], ACT.Copy).then_inc(S["high_kept"], 1)

            def keep_counts(n, j, batches):
                for b in batches:
                    g, size = sum(BATCHES[:b]), BATCHES[b]
                    act.wait_ge(S["batch_done"], NB + NB * n + b + 1)
                    apart(act)
                    to = stage[0:P, j, :].bitcast(F8).rearrange("p (c m) -> p c m", c=T)
                    act.activation(to[:, :, GD * g:GD * (g + size)].rearrange("p c (s l) -> p s c l", l=GD),
                                   banks(4 + b % 4)[0:P, 0:size * P].rearrange("p (s c l) -> p s c l", s=size, l=GD),
                                   ACT.Copy, scale=0.125, saturate=False).then_inc(S["batch_out"], 1)

            def count_tile(i, j):
                n = R * i + j
                if some(n - 2):
                    low(n - 2, n - 2, (j - 2) % R)
                act.wait_ge(slot_out[j], 16 * i + 16)
                after(act, S["tile_done"], n - R + 1)
                after(act, S["or_done"], n - R + 1)
                keep_counts(n, j, range(NB // 2))
                if some(n - 2):
                    high(n - 2, n - 2, (j - 2) % R, 1)
                keep_counts(n, j, range(NB // 2, NB))

            act.wait_ge(S["stage_clear"], 1)
            act.wait_ge(S["deg_ready"], 1)
            for j in range(R):
                count_tile(0, j)
            with act.Fori(1, ROUNDS) as i:
                for j in range(R):
                    count_tile(i, j)
            for n in (T - 2, T - 1):
                low(n, n, n % R)
                high(n, n, n % R, 1)

            with act.Fori(0, ROUNDS) as i:
                for m in range(KC):
                    act.wait_ge(S["mix_done"], KC * i + m + 1)
                    if m == 0:
                        act.wait_ge(S["w2_done"], R * i + 1)
                    act.activation(hb[:, m, :], banks(2 * m, 2)[:, 0:R * P], ACT.Gelu,
                                   bias=bias1[:, m:m + 1]).then_inc(S["gelu_done"], 1)

            with act.Fori(0, (STEPS - 2) // 2) as it:
                for par in range(2):
                    with act.Fori(0, ROUNDS) as i:
                        for j in range(R):
                            n = T * (1 + par) + 2 * T * it + R * i + j
                            low(n, R * i + j, j)
                            high(n, R * i + j, j, par)

            def last_step(i, j, main):
                n = R * i + j
                if main:
                    low((STEPS - 1) * T + n, n, j)
                if some(n - 1) and lies(n - 1):
                    act.wait_ge(S["acc_turned"], n)
                    act.activation(at_t[:, (j - 1) % R, :, :], banks(5)[:, 0:256].rearrange("p (k m) -> p k m", k=KC)[:, :, 0:P],
                                   ACT.Copy).then_inc(S["at_ready"], 1)
                if some(n - 2) and lies(n - 2):
                    s = (j - 2) % R
                    act.wait_ge(S["var1_ready"], n - 1)
                    act.activation(lnu[:, s:s + 1], lnt[:, s:s + 1], ACT.Sqrt).then_inc(S["std1_ready"], 1)
                    act.wait_ge(S["y_kept"], n - 1)
                    act.wait_ge(S["y_turned"], n - 1)
                    act.wait_ge(S["norm_ready"], n - 1)
                    act.activation(y_in[:, s, :], x1[:, bass.ds(n - 2, 1), :].rearrange("p o f -> p (o f)"), ACT.Identity,
                                   bias=nmr[:, s:s + 1], scale=rstd[:, s:s + 1]).then_inc(S["y_ready"], 1)

            for j in range(R):
                last_step(0, j, True)
            with act.Fori(1, ROUNDS) as i:
                for j in range(R):
                    last_step(i, j, True)
            for j in range(LAG):
                last_step(ROUNDS, j, False)

            act.activation(small[0:1, 33:34], small[0:1, 32:33], ACT.Exp).then_inc(S["warmed"], 1)
            for k in range(3):
                act.wait_ge(S["exp_in"], k + 1)
                act.activation(small[0:1, 24:32], small[0:1, 16:24], ACT.Exp).then_inc(S["exp_out"], 1)

            act.activation(small[0:1, 34:35], small[0:1, 32:33], ACT.Gelu).then_inc(S["warmed"], 1)
            act.wait_ge(S["scale3_ready"], 1)
            for e in range(2):
                act.activation(w1_hi[:, e, :, :], w1e[:, e, :, :], ACT.Copy, scale=scale3[:, 0:1]).then_inc(S["halves_high"], 1)

            def expert_round(i, first=False):
                for e in range(2):
                    for m in range(FM):
                        at = FM * e + m
                        n = 2 * FM * i + at
                        act.wait_ge(S["hid_done"], n + 1)
                        act.wait_ge(S["hid_split"], n + 1)
                        act.activation(gelu_out[:, at % 2, :], banks(2 * (at % 2), 2)[:, 0:R * P], ACT.Gelu,
                                       bias=b1e[:, e, m:m + 1], scale=scale3[:, 6:7]).then_inc(S["hid_ready"], 1)
                        act.wait_ge(S["hid_ready"], 2 + n + 1)
                        if at == 0:
                            act.wait_ge(S["ffn_done"], R * i + 1)
                        act.activation(hid_hi[:, e, m, :], gelu_out[:, at % 2, :], ACT.Copy,
                                       scale=scale3[:, 1:2]).then_inc(S["hid_high"], 1)
                        if first and at in (FM, FM + 2):
                            b = (at - FM) // 2
                            act.wait_ge(S["w2_scaled"], b + 1)
                            act.activation(w2_hi[:, b, :, :], w2e[:, b, :, :], ACT.Copy).then_inc(S["halves_high"], 1)
                for j in range(R):
                    n = R * i + j
                    act.wait_ge(S["var2_ready"], n + 1)
                    act.activation(lnu[:, j:j + 1], lnt[:, j:j + 1], ACT.Sqrt).then_inc(S["std2_ready"], 1)

            expert_round(0, True)
            with act.Fori(1, ROUNDS) as i:
                expert_round(i)

        @block.vector
        def _(dve):
            def norm_front(link, s, t, v):
                link(dve.tensor_tensor(v, s[:, :, 1], s[:, :, 4], ALU.subtract))
                link(dve.tensor_tensor(v, v, v, ALU.mult))
                link(dve.tensor_tensor(t, s[:, :, 2], s[:, :, 5], ALU.add))
                link(dve.scalar_tensor_tensor(t, v, D / 4.0, t, ALU.mult, ALU.add))
                return dve.tensor_scalar(t, t, 1.0 / D, EPS, ALU.mult, ALU.add)

            def norm_back(link, s, v, m, r):
                link(dve.reciprocal(r, v))
                link(dve.tensor_tensor(m, s[:, :, 1], s[:, :, 4], ALU.add))
                link(dve.tensor_scalar(m, m, 0.5, None, ALU.mult))

            link = Links(dve, S["dve_chain"])
            dve.memset(ones[:, :], 1.0).then_inc(S["ones_set"], 1)
            dve.memset(ones16[:, :], 1.0).then_inc(S["ones_set"], 1)
            dve.memset(small[:, :], 0.0).then_inc(S["ones_set"], 1)
            dve.memset(zeros[:, :], 0.0).then_inc(S["ones_set"], 1)
            dve.memset(kvn[:, :, :, 128], 1.0).then_inc(S["ones_set"], 1)
            for name, c in (("h_biased", 1), ("kc_ready", 2), ("sq_used", 2), ("x1_mixed", R), ("sum_ready", 2), ("gen_added", 1),
                            ("r_ready", R), ("out_ready", R), ("hid_split", 2)):
                dve.sem_inc(S[name], c)
            dve.wait_ge(S["cst_in"], 16)
            link(dve.tensor_copy(iota_g, cst[:, C_IOTA:C_GRP].rearrange("p (m o) -> p m o", o=1).to_broadcast([128, 128, HALVES[1]])))
            dve.wait_ge(S["kvw_in"], 32)
            wv = w_kv[:, :, :].rearrange("p k (g l) -> p (k g) l", l=HD)
            link(dve.tensor_reduce(wsum[:, :], wv, AX.X, ALU.add))
            link(dve.tensor_scalar(wsum[:, :], wsum[:, :], -1.0 / HD, None, ALU.mult))
            dve.tensor_tensor(wv, wv, wsum[:, :].rearrange("p (g o) -> p g o", o=1).to_broadcast([128, (KC + 1) * 2 * HEADS, HD]),
                              ALU.add).then_inc(S["wkv_ready"], 1)

            def statistics(r):
                dve.wait_ge(x_in[r], 16)
                for j in range(R):
                    dve.bn_stats(st[:, R * r + j, :], x1[:, R * r + j, :]).then_inc(S["stats"], 1)

            def deviations(t0, t1, times):
                dve.wait_ge(S["stats"], t1)
                s = st[:, t0:t1, :]
                norm_front(link, s, lnt[:, t0:t1], lnu[:, t0:t1]).then_inc(S["var_ready"], 1)
                dve.wait_ge(S["std_ready"], times)
                norm_back(link, s, lnu[:, t0:t1], mean[:, t0:t1], rstd[:, t0:t1])

            statistics(0)
            deviations(0, R, 1)
            dve.wait_ge(S["wkv_ready"], 1)

            def normalize(n, j):
                dve.tensor_scalar(xn[:, j, :], x1[:, bass.ds(n, 1), :].rearrange("p o f -> p (o f)"),
                                  mean[:, bass.ds(n, 1)], rstd[:, bass.ds(n, 1)],
                                  ALU.subtract, ALU.mult).then_inc(S["xn_ready"], 1)

            def head_sums(n, j):
                dve.wait_ge(S["sq_ready"], n + 1)
                dve.tensor_reduce(kvar[:, 2 * HEADS * j:2 * HEADS * (j + 1)],
                                  sq[:, j % 2, :].rearrange("p (g l) -> p g l", l=HD), AX.X, ALU.add).then_inc(S["sq_used"], 1)
                dve.wait_ge(S["silu_done"], 2 + n + 1)
                dve.tensor_reduce(hmx[:, bass.ds(n, 1)], acc[:, bass.ds(n, 1), :].rearrange("p o f -> p (o f)"),
                                  AX.X, ALU.max).then_inc(S["hmax_ready"], 1)

            def compare(i, j):
                first = sum(SAMPLES) * (i - 1) + sum(SAMPLES[:j])
                dve.wait_ge(S["cmp_used"], first + 1)
                apart(dve)
                for s in range(SAMPLES[j]):
                    dve.tensor_scalar(cmp[:, s, :], grp16[:, :], gds[:, 1, bass.ds(first + s, 1)], None,
                                      ALU.is_gt).then_inc(S["cmp_ready"], 1)

            def decode(step):
                src_i, dst_i = e_int[:, 1, :], e_int[:, 2, :]
                if step == 0:
                    dve.wait_ge(S["code_turned"], GT)
                    for b, at, n in ((3, 0, 4), (0, 4, 1)):
                        link(dve.tensor_copy(e_int[:, 0, at * P:(at + n) * P].rearrange("p (t g) -> p t g", t=n),
                                             banks(b)[:, 0:n * 128].rearrange("p (t g) -> p t g", t=n)[:, :, 0:P]))
                    link(dve.tensor_scalar(src_i, e_int[:, 0, :], 12, None, ALU.logical_shift_right))
                    link(dve.tensor_scalar(dst_i, e_int[:, 0, :], 4095, None, ALU.bitwise_and))
                if step == 1:
                    link(dve.tensor_scalar(e_f[:, 0, :], src_i, 1.0 / P, -0.496, ALU.mult, ALU.add))
                    link(dve.tensor_scalar(e_f[:, 0, :], e_f[:, 0, :], MAGIC, MAGIC, ALU.add, ALU.subtract))
                    link(dve.tensor_scalar(e_f[:, 1, :], dst_i, 1.0 / GD, -0.4, ALU.mult, ALU.add))
                    link(dve.tensor_scalar(e_f[:, 1, :], e_f[:, 1, :], MAGIC, MAGIC, ALU.add, ALU.subtract))
                if step == 2:
                    link(dve.scalar_tensor_tensor(eq[:, 1, :], e_f[:, 0, :], -float(P), src_i, ALU.mult, ALU.add))
                    link(dve.scalar_tensor_tensor(e_f[:, 2, :], e_f[:, 0, :], float(GD), dst_i, ALU.mult, ALU.add))
                if step == 3:
                    link(dve.scalar_tensor_tensor(e_f[:, 3, :], e_f[:, 1, :], 1000.0 - GD, e_f[:, 2, :], ALU.mult, ALU.add))
                    link(dve.scalar_tensor_tensor(e_f[:, 3, :], grp, -1000.0, e_f[:, 3, :], ALU.mult, ALU.add))
                if step == 4:
                    link(dve.tensor_scalar(eq[:, 0, :], e_f[:, 3, :], -1000.0, 1000.0, ALU.max, ALU.min))
                    link(dve.scalar_tensor_tensor(local, e_f[:, 0, :], -float(GD), eq[:, 0, :], ALU.mult, ALU.add))
                    for d in range(GD):
                        dve.tensor_scalar(oh_l[:, d, :], local, float(d), None, ALU.is_equal).then_inc(S["local_ready"], 1)

            def token_round(i, last, samples=False, first=False, decoding=False):
                for j in range(R):
                    n = R * i + j
                    dve.wait_ge(S["h_done"], n + 1)
                    dve.wait_ge(S["silu_done"], n + back(j))
                    dve.tensor_tensor(h_pre[:, j % 2, :], banks(5)[0:P, 0:D], b_in[:, :], ALU.add).then_inc(S["h_biased"], 1)
                    if samples:
                        compare(i, j)
                    if decoding:
                        decode(j)
                    if first and j < ROUNDS - 1:
                        statistics(j + 1)
                    dve.wait_ge(S["kv_done"], n + 1)
                    after(dve, S["kvn_ready"], n - R + 1)
                    dve.tensor_tensor(kc[:, j, :], banks(6 + j % 2)[0:P, :], w_kv[0:P, KC, :], ALU.add).then_inc(S["kc_ready"], 1)
                    if first and j == ROUNDS - 2:
                        deviations(R, T, 2)
                    if not last and not (first and j < ROUNDS - 2):
                        for s in range(ROUNDS - 1) if first and j == ROUNDS - 2 else [j]:
                            dve.wait_ge(S["x1_bias"], 1 + R * i + s + 1)
                            dve.wait_ge(S["turned"], R * i + s + 1)
                            apart(dve)
                            normalize(R * i + s + R, s)
                    if j:
                        head_sums(n - 1, j - 1)
                head_sums(R * i + R - 1, R - 1)
                if last:
                    dve.wait_ge(S["hmax_ready"], T)
                    dve.tensor_reduce(hmx[:, T:T + 1], hmx[:, 0:T], AX.X, ALU.max).then_inc(S["hmax_ready"], 1)
                klink = Links(dve, S["dve_kv"], i)
                dve.wait_ge(S["sq_used"], 2 + R * i + R)
                dve.tensor_scalar(kvar[:, :], kvar[:, :], 1.0 / HD, EPS, ALU.mult, ALU.add).then_inc(S["kvar_ready"], 1)
                dve.wait_ge(S["kstd_ready"], i + 1)
                klink(dve.reciprocal(kvar[:, :], kvar[:, :]))
                for j in range(R):
                    after(dve, S["kv_summed"], R * i + j - R + 1)
                    dve.tensor_tensor(kvn[:, j, :, 0:128].rearrange("p b (g l) -> p b g l", l=HD),
                                      kc[:, j, :].rearrange("p (b g l) -> p b g l", b=4, l=HD),
                                      kvar[:, 2 * HEADS * j:2 * HEADS * (j + 1)].rearrange("p (b g o) -> p b g o", b=4, o=1)
                                      .to_broadcast([P, 4, 4, HD]), ALU.mult).then_inc(S["kvn_ready"], 1)

            dve.wait_ge(S["token_in"], 16 * 4)
            for j in range(R):
                normalize(j, j)
            dve.wait_ge(S["edges_in"], 16 * 2 * (1 + 128 - FULLP))
            dve.scalar_tensor_tensor(code[:, :], si[:, :], 4096.0, di[:, :], ALU.mult, ALU.add).then_inc(S["code_ready"], 1)
            token_round(0, False, first=True)
            smp = di[:, 0:EC].rearrange("p (s l) -> p s l", l=AL)[:, :, 0]
            link(dve.tensor_scalar(gds[:, 0, :], smp, 1.0 / GD, -0.4, ALU.mult, ALU.add))
            link(dve.tensor_scalar(gds[:, 1, :], gds[:, 0, :], MAGIC, MAGIC, ALU.add, ALU.subtract))
            dve.wait_ge(S["const_in"], 16)
            link(dve.tensor_copy(grp16[:, :], grp))
            with dve.Fori(1, 3) as i:
                token_round(i, False, True)
            dve.wait_ge(S["cmp_used"], 1 + NS)
            dve.tensor_copy(below[:, 0:512], banks(0)[0:1, :]).then_inc(S["below_ready"], 1)
            dve.tensor_copy(below[:, 512:G], banks(3)[0:1, 0:G - 512]).then_inc(S["below_ready"], 1)
            dve.wait_ge(S["rows_turned"], 1)
            dve.tensor_scalar(start_i[:, :], banks(0)[0:P, 0:GT], 1.0, 0.0, ALU.subtract, ALU.max).then_inc(S["start_ready"], 1)
            token_round(3, False)
            token_round(4, True, decoding=True)

            dve.memset(stage[:, :, :].rearrange("p r (c m) -> p (r c) m", m=128)[:, :, P:128], 0).then_inc(S["stage_clear"], 1)
            dve.wait_ge(S["scale_products"], 1)
            link(dve.tensor_reduce(small[0:1, 0:1], banks(0)[0:1, 0:P], AX.X, ALU.max))
            link(dve.tensor_scalar(small[0:1, 0:1], small[0:1, 0:1], 0.28, None, ALU.max))
            link(dve.tensor_scalar(small[0:1, 1:2].bitcast(I32), small[0:1, 0:1].bitcast(I32), 0x7F800000, None, ALU.bitwise_and))
            link(dve.reciprocal(small[0:1, 2:3], small[0:1, 1:2]))
            link(dve.tensor_scalar(small[0:1, 2:3], small[0:1, 2:3], 2.0 ** 14, None, ALU.mult))
            dve.tensor_scalar(small[0:1, 3:4], small[0:1, 1:2], 2.0 ** -14, None, ALU.mult).then_inc(S["scale_ready"], 1)
            dve.wait_ge(S["scale_products"], 2)
            dve.tensor_copy(scale2[:, :], banks(3)[:, 0:2]).then_inc(S["scale_kept"], 1)
            dve.wait_ge(S["scale_kept"], 1)
            dve.wait_ge(S["pad_set"], 2 + STEPS)
            link(dve.tensor_scalar(coef[:, :], invf[:, :], scale2[:, 1:2], None, ALU.mult))

            def one_hots(n):
                for h in range(2):
                    size = HALVES[h]
                    dve.wait_ge(S["batch_done"], NB * n + (NB // 2) * (h + 1))
                    dve.tensor_tensor(
                        oh[h][:, :, :, 0:size],
                        iota_g[:, :, 0:size].rearrange("p (o m) g -> p o m g", o=1).to_broadcast([128, 2, 128, size]),
                        eq[:, :, bass.ds(GPT * n + HALVES[0] * h, size)].rearrange("p a (o g) -> p a o g", o=1)
                        .to_broadcast([128, 2, 128, size]), ALU.is_equal).then_inc(S["oh_ready"], 1)

            dve.wait_ge(S["row_done"], GD + 1)
            one_hots(0)
            with dve.Fori(0, ROUNDS) as i:
                for j in range(R - 1):
                    n = R * i + j
                    dve.wait_ge(S["high_ready"], (R - 1) * i + j + 1)
                    dve.scalar_tensor_tensor(u[0][:, bass.ds(n, 1), D:2 * D].rearrange("p o f -> p (o f)"),
                                             acc[:, bass.ds(n, 1), :].rearrange("p o f -> p (o f)"), scale2[0:P, 0:1],
                                             u[0][:, bass.ds(n, 1), 0:D].rearrange("p o f -> p (o f)"),
                                             ALU.mult, ALU.subtract).then_inc(S["split_ready"], 1)

            def new_term(n, at, j, k, to, guard=False):
                nxt = u[to][:, bass.ds(at, 1), :].rearrange("p o f -> p (o f)")
                dve.wait_ge(S["low_part"], n + 1)
                dve.scalar_tensor_tensor(u_sum[:, j, :], banks(j % 3)[0:P, 0:D], deg[0:P, bass.ds(at, 1)],
                                         lo_part[:, j, :], ALU.mult, ALU.add).then_inc(S["sum_ready"], 1)
                dve.wait_ge(S["sum_ready"], 2 + n + 1)
                xa = acc[:, bass.ds(at, 1), :].rearrange("p o f -> p (o f)")
                dve.scalar_tensor_tensor(xa, u_sum[:, j, :], coef[0:P, bass.ds(k, 1)], xa,
                                         ALU.mult, ALU.add).then_inc(S["acc_done"], 1)
                if guard:
                    dve.wait_ge(S["batch_out"], 4 + NB * n + NB)
                    dve.tensor_tensor(orr, orr, stage[0:P, j, :].bitcast(I32), ALU.bitwise_or).then_inc(S["or_done"], 1)
                dve.wait_ge(S["high_kept"], n + 1)
                dve.tensor_tensor(nxt[:, D:2 * D], u_sum[:, j, :], nxt[:, 0:D], ALU.subtract).then_inc(S["split_ready"], 1)

            def first_step(n, j):
                new_term(n, n, j, 0, 1, guard=True)

            dve.wait_ge(S["rows_turned"], 2)
            link(dve.tensor_scalar(deg_raw[0:P, :], banks(5)[0:P, 0:T], 0.125, None, ALU.mult))
            link(dve.tensor_scalar(deg[0:P, :], deg_raw[0:P, :], 0.125, None, ALU.max))
            dve.reciprocal(deg[0:P, :], deg[0:P, :]).then_inc(S["deg_ready"], 1)
            dve.wait_ge(S["deg_ready"], 1)
            one_hots(1)
            klink = Links(dve, S["dve_kv"], ROUNDS)
            dve.wait_ge(S["weights_in"], 16 * N_WEIGHTS)
            dve.wait_ge(S["kv_summed"], T)
            dve.wait_ge(S["xt_kept"], R + T)
            for c in range(KC):
                at = slice(128 * c, 128 * c + 128)
                gv, bv = lnrow[:, 0, at], lnrow[:, 1, at]
                if c:
                    dve.wait_ge(S["kvbd_ready"], c)
                klink(dve.tensor_copy(kvs[:, 2, 0:1], banks(1)[:, 129 * c + 128:129 * c + 129]))
                klink(dve.tensor_tensor(kvs[:, 0, :], banks(1)[:, 129 * c:129 * c + 128], gv, ALU.mult))
                klink(dve.scalar_tensor_tensor(kvs[:, 0, :], bv, kvs[:, 2, 0:1], kvs[:, 0, :], ALU.mult, ALU.add))
                klink(dve.tensor_tensor(kvs[:, 1, :], banks(2)[:, 129 * c:129 * c + 128], gv, ALU.mult))
                klink(dve.scalar_tensor_tensor(kvs[:, 1, :], bv, float(N), kvs[:, 1, :], ALU.mult, ALU.add))
                klink(dve.tensor_scalar(kvs[:, 0, :], kvs[:, 0, :], lncol[:, 0:1], None, ALU.mult))
                klink(dve.scalar_tensor_tensor(kvs[:, 0, :], kvs[:, 1, :], lncol[:, 1:2], kvs[:, 0, :], ALU.mult, ALU.add))
                dve.scalar_tensor_tensor(kv_bd[:, c, :], kvs[:, 0, :], 1.0 / N, mask, ALU.mult, ALU.mult).then_inc(S["kvbd_ready"], 1)
            link(dve.memset(orr, 0))
            dve.wait_ge(S["h_kept"], 16)
            for j in range(2, R):
                one_hots(j)
                first_step(j - 2, j - 2)
            with dve.Fori(1, ROUNDS) as i:
                for j in range(R):
                    one_hots(R * i + j)
                    first_step(R * i + j - 2, (j - 2) % R)
            dve.wait_ge(S["matrix_products"], 1)
            for c in range(KC):
                klink(dve.tensor_copy(m1t[:, c, :], banks(5 + 2 * c)[:, 0:D + 1]))
            for c in range(KC):
                at = slice(128 * c, 128 * c + 128)
                dve.tensor_tensor(m1t[:, c, at], m1t[:, c, at], ident, ALU.add).then_inc(S["matrices_ready"], 1)
            for n in (T - 2, T - 1):
                first_step(n, n % R)
            dve.wait_ge(S["matrix_products"], 2)
            for c in range(KC):
                dve.tensor_copy(g_sb[:, c, :], banks(6)[:, D * c:D * c + D]).then_inc(S["matrices_ready"], 1)
            dve.tensor_tensor(bias1[:, :], banks(5)[:, 0:KC], b1c[:, :], ALU.add).then_inc(S["matrices_ready"], 1)
            dve.wait_ge(S["or_done"], T)
            link(dve.tensor_scalar(orr, orr, 0x40404040, None, ALU.bitwise_and))
            link(dve.tensor_reduce(fl[:, 0:1], deg_raw[0:P, :], AX.X, ALU.add))
            dve.tensor_reduce(fl[:, 1:2], orr, AX.X, ALU.max).then_inc(S["flag_part"], 1)

            with dve.Fori(0, ROUNDS) as i:
                for j in range(R):
                    n = R * i + j
                    dve.wait_ge(S["w2_done"], 1 + n + 1)
                    xr = x1[:, bass.ds(n, 1), :].rearrange("p o f -> p (o f)")
                    dve.tensor_tensor(xr, xr, banks(4 + j % 4)[0:P, 0:D], ALU.add).then_inc(S["x1_mixed"], 1)
            dve.wait_ge(S["flag_sum"], 1)
            link(dve.tensor_scalar(small[0:1, 4:5], banks(3)[0:1, 0:1], E / 8.0, None, ALU.not_equal))
            link(dve.tensor_scalar(small[0:1, 5:6], banks(3)[0:1, 1:2], 0.0, None, ALU.is_gt))
            dve.tensor_tensor(small_i[0:1, 0:1], small[0:1, 4:5], small[0:1, 5:6], ALU.max).then_inc(S["flag_ready"], 1)

            with dve.Fori(0, (STEPS - 2) // 2) as it:
                for par in range(2):
                    with dve.Fori(0, ROUNDS) as i:
                        for j in range(R):
                            new_term(T * (1 + par) + 2 * T * it + R * i + j, R * i + j, j, 1 + 2 * it + par, par)
            dve.wait_ge(S["acc_done"], (STEPS - 1) * T)
            dve.wait_ge(S["flag_ready"], 1)
            dve.sem_inc(S["steps_done"], 1)

            bad = dve.value_load(small_i[0:1, 0:1], min_val=0, max_val=1)
            with dve.If(bad == 1):
                dve.wait_ge(S["gen_init"], 64)
                glink = Links(dve, S["gen_add"])
                glink(dve.memset(rows[:, D:D + 1], 1.0))
                glink(dve.tensor_copy(dst_f, dst_all))
                dve.sem_inc(S["gen_dve"], 1)
                with dve.Fori(0, STEPS) as k:
                    glink = Links(dve, S["gen_add"], 2 + 4 * k)
                    glink(dve.memset(sums[:, :, :], 0.0))
                    apart(dve)
                    with dve.Fori(0, EP) as e:
                        n = EP * k + e
                        dve.wait_ge(S["gen_mm"], n + 1)
                        dve.tensor_scalar(oh_g, node_row, dst_f[:, bass.ds(e, 1)], None, ALU.is_equal).then_inc(S["gen_onehot"], 1)
                        for b in range(T // R):
                            dve.wait_ge(S["gen_batch"], R * n + b + 1)
                            for s in range(R):
                                t = R * b + s
                                ins = dve.tensor_tensor(sums[:, t, :], sums[:, t, :], banks(s)[0:P, 0:D + 1], ALU.add)
                            ins.then_inc(S["gen_added"], 1)
                    dve.wait_ge(S["gen_added"], 1 + R * EP * k + R * EP)
                    glink(dve.tensor_scalar(rdeg, sums[:, :, D], 1.0, None, ALU.max))
                    glink(dve.reciprocal(rdeg, rdeg))
                    glink(dve.tensor_tensor(sums[:, :, 0:D], sums[:, :, 0:D],
                                            rdeg.rearrange("p (t o) -> p t o", o=1).to_broadcast([P, T, D]), ALU.mult))
                    dve.scalar_tensor_tensor(acc[:, :, :], sums[:, :, 0:D], invf[0:P, bass.ds(k, 1)], acc[:, :, :],
                                             ALU.mult, ALU.add).then_inc(S["gen_step"], 1)
                    dve.wait_ge(S["gen_step"], k + 1)
                    dve.wait_ge(S["gen_stored"], 16 * k + 16)
                    dve.sem_inc(S["gen_dve"], 1)
                dve.memset(big[0:P, T * D:2 * T * D], 0.0).then_inc(S["gen_end"], 1)
            with dve.Else():
                pass

            def last_step(i, j, main):
                n = R * i + j
                if main:
                    at = (STEPS - 1) * T + n
                    dve.wait_ge(S["low_part"], at + 1)
                    dve.scalar_tensor_tensor(u_sum[:, j, :], banks(j % 3)[0:P, 0:D], deg[0:P, bass.ds(n, 1)],
                                             lo_part[:, j, :], ALU.mult, ALU.add).then_inc(S["sum_ready"], 1)
                    dve.wait_ge(S["sum_ready"], 2 + at + 1)
                    after(dve, S["acc_turned"], n - R + 1)
                    dve.scalar_tensor_tensor(at_in[:, j, :], u_sum[:, j, :], coef[0:P, STEPS - 1:STEPS],
                                             acc[:, bass.ds(n, 1), :].rearrange("p o f -> p (o f)"),
                                             ALU.mult, ALU.add).then_inc(S["acc_in"], 1)
                if some(n - 2) and lies(n - 2):
                    s, m = (j - 2) % R, n - 2
                    dve.wait_ge(S["out_done"], m + 1)
                    xr = x1[:, bass.ds(m, 1), :].rearrange("p o f -> p (o f)")
                    dve.tensor_tensor(xr, xr, banks(6)[0:P, 0:D], ALU.add).then_inc(S["x1_ready"], 1)
                    dve.wait_ge(S["x1_ready"], m + 1)
                    ylink = Links(dve, S["dve_last"], 3 * m)
                    apart(dve)
                    ylink(dve.bn_stats(st[:, s, :], xr))
                    apart(dve)
                    ylink(dve.bn_aggr(mv[:, s, :], st[:, s, :]))
                    dve.tensor_scalar(lnt[:, s:s + 1], mv[:, s, 1:2], EPS, None, ALU.add).then_inc(S["var1_ready"], 1)
                    dve.wait_ge(S["std1_ready"], m + 1)
                    ylink(dve.reciprocal(rstd[:, s:s + 1], lnu[:, s:s + 1]))
                    dve.scalar_tensor_tensor(nmr[:, s:s + 1], mv[:, s, 0:1], -1.0, rstd[:, s:s + 1], ALU.mult, ALU.mult).then_inc(S["norm_ready"], 1)
                if some(n - 3) and lies(n - 3):
                    m = n - 3
                    dve.wait_ge(S["y_turned"], R + m + 1)
                    apart(dve)
                    dve.tensor_reduce(ysum[:, :, bass.ds(m, 1)], banks(7)[:, 0:256].rearrange("p (k m) -> p k m", k=KC)[:, :, 0:P],
                                      AX.X, ALU.add).then_inc(S["y_summed"], 1)
                    yt, at = banks(7)[:, 0:256].rearrange("p (k m) -> p k m", k=KC)[:, :, 0:P], bass.ds(P * m, P)
                    dve.tensor_scalar(y_hi[:, :, at], yt, Y_SCALE, None, ALU.mult).then_inc(S["y_high"], 1)
                    dve.wait_ge(S["y_high"], m + 1)
                    apart(dve)
                    dve.scalar_tensor_tensor(y_lo[:, :, at], yt, Y_SCALE, y_hi[:, :, at],
                                             ALU.mult, ALU.subtract).then_inc(S["yt_ready"], 1)

            for j in range(R):
                last_step(0, j, True)
            with dve.Fori(1, ROUNDS) as i:
                for j in range(R):
                    last_step(i, j, True)
            for j in range(LAG):
                last_step(ROUNDS, j, False)

            dve.wait_ge(S["y_summed"], T)
            link(dve.tensor_reduce(meant[:, :], ysum[:, :, :], AX.X, ALU.add))
            dve.tensor_scalar(meant[:, :], meant[:, :], 1.0 / N, None, ALU.mult).then_inc(S["route_row"], 1)
            dve.wait_ge(S["route_products"], 1)
            prob, low, ex = small[0:1, 8:16], small[0:1, 16:24], small[0:1, 24:32]
            top, rec = small[0:1, 48:56], small[0:1, 40:41]

            def softmax(times):
                link(dve.tensor_reduce(rec, prob, AX.X, ALU.max))
                dve.tensor_scalar(low, prob, rec, None, ALU.subtract).then_inc(S["exp_in"], 1)
                dve.wait_ge(S["exp_out"], times)
                link(dve.tensor_reduce(rec, ex, AX.X, ALU.add))
                link(dve.reciprocal(rec, rec))
                link(dve.tensor_scalar(prob, ex, rec, None, ALU.mult))

            link(dve.tensor_tensor(prob, banks(4)[0:1, 0:NX], br[:, :], ALU.add))
            softmax(1)
            link(dve.tensor_scalar(low, prob, float(N), None, ALU.mult))
            link(dve.reciprocal(low, low))
            link(dve.tensor_scalar(low, low, CAP, 1.0, ALU.mult, ALU.min))
            link(dve.tensor_tensor(prob, prob, low, ALU.mult))
            softmax(2)
            link(dve.max(top, prob))
            link(dve.max_index(idx_u[:, :], top, prob))
            link(dve.tensor_copy(small_i[0:1, 2:4], idx_u[0:1, 0:2]))
            dve.sem_inc(S["route_ready"], 1)
            dve.tensor_scalar(low, top, top[:, 0:1], None, ALU.subtract).then_inc(S["exp_in"], 1)
            dve.wait_ge(S["exp_out"], 3)
            link(dve.tensor_tensor(rec, ex[:, 0:1], ex[:, 1:2], ALU.add))
            link(dve.reciprocal(rec, rec))
            dve.tensor_scalar(small[0:1, 56:58], ex[:, 0:2], rec, None, ALU.mult).then_inc(S["route_row"], 1)
            dve.wait_ge(S["route_products"], 2)
            link(dve.tensor_copy(topw[:, :], banks(4)[:, 16:18]))
            def scales(at, n, to, times):
                top, inv = scale_row[0:n, 0:1], scale_row[0:n, 1:2]
                dve.wait_ge(S["scales_turned"], 2 * times - 1)
                link(dve.tensor_reduce(top, banks(5)[0:n, 0:128], AX.X, ALU.max))
                link(dve.tensor_scalar(top, top, TINY, None, ALU.max))
                link(dve.tensor_scalar(top.bitcast(I32), top.bitcast(I32), 0x7F800000, None, ALU.bitwise_and))
                link(dve.reciprocal(inv, top))
                link(dve.tensor_scalar(scale_row[0:n, 2:2 + n], ident[0:n, 0:n], inv, 2.0 ** 13, ALU.mult, ALU.mult))
                dve.tensor_scalar(scale_row[0:n, 2 + n:2 + 2 * n], ident[0:n, 0:n], top, 2.0 ** -13,
                                  ALU.mult, ALU.mult).then_inc(S["maxima_ready"], 1)
                dve.wait_ge(S["scales_turned"], 2 * times)
                link(dve.tensor_copy(scale3[:, to:to + 2 * n], banks(5)[:, 128:128 + 2 * n]))

            for e in range(2):
                dve.wait_ge(w1_in[e], 32)
                link(dve.tensor_reduce(biggest[:, 4 + e:5 + e], w1e[:, e, :, :], AX.XY, ALU.max, apply_absolute_value=True))
            link(dve.tensor_reduce(biggest[:, 3:4], b1e, AX.XY, ALU.max, apply_absolute_value=True))
            link(dve.tensor_tensor(biggest[:, 0:1], biggest[:, 4:5], biggest[:, 5:6], ALU.max))
            dve.scalar_tensor_tensor(biggest[:, 1:2], biggest[:, 0:1], 256.0, biggest[:, 3:4],
                                     ALU.mult, ALU.add).then_inc(S["maxima_ready"], 1)
            scales(0, 2, 0, 1)
            dve.tensor_scalar(scale3[:, 6:7], scale3[:, 2:3], 1.0 / Y_SCALE, None, ALU.mult).then_inc(S["scale3_ready"], 1)
            for e in range(2):
                dve.wait_ge(S["halves_high"], e + 1)
                dve.scalar_tensor_tensor(w1_lo[:, e, :, :], w1e[:, e, :, :], scale3[:, 0:1], w1_hi[:, e, :, :],
                                         ALU.mult, ALU.subtract).then_inc(S["halves_low"], 1)
            for e in range(2):
                dve.wait_ge(w2_in[e], 32)
                link(dve.tensor_reduce(biggest[:, 6 + e:7 + e], w2e[:, e, :, :], AX.XY, ALU.max, apply_absolute_value=True))
            dve.tensor_tensor(biggest[:, 2:3], biggest[:, 6:7], biggest[:, 7:8], ALU.max).then_inc(S["maxima_ready"], 1)

            def split_hidden(i, at):
                n = 2 * FM * i + at
                e, m = at // FM, at % FM
                dve.wait_ge(S["hid_high"], n + 1)
                apart(dve)
                dve.scalar_tensor_tensor(hid_lo[:, e, m, :], gelu_out[:, at % 2, :], scale3[:, 1:2], hid_hi[:, e, m, :],
                                         ALU.mult, ALU.subtract).then_inc(S["hid_split"], 1)

            split_hidden(0, 0)
            scales(2, 1, 4, 2)
            split_hidden(0, 1)
            link(dve.tensor_tensor(scale3[:, 7:8], scale3[:, 3:4], scale3[:, 5:6], ALU.mult))
            link(dve.tensor_scalar(w2_top, topw, scale3[:, 4:5], None, ALU.mult))
            dve.wait_ge(S["halves_low"], 2)
            for e in range(2):
                dve.tensor_scalar(w2e[:, e, :, :], w2e[:, e, :, :], w2_top[:, e:e + 1], None, ALU.mult).then_inc(S["w2_scaled"], 1)
                split_hidden(0, 2 + 2 * e)
                split_hidden(0, 3 + 2 * e)
            for e in range(2):
                dve.wait_ge(S["halves_high"], 2 + e + 1)
                dve.tensor_tensor(w2_lo[:, e, :, :], w2e[:, e, :, :], w2_hi[:, e, :, :], ALU.subtract).then_inc(S["halves_low"], 1)
                split_hidden(0, 6 + e)
            link(dve.tensor_scalar(b2e[:, 0, :], b2e[:, 0, :], topw[0:P, 0:1], None, ALU.mult))
            dve.scalar_tensor_tensor(b2e[:, 0, :], b2e[:, 1, :], topw[0:P, 1:2], b2e[:, 0, :], ALU.mult, ALU.add).then_inc(S["b2_ready"], 1)

            def result_sum(i, j):
                n = R * i + j
                dve.wait_ge(S["ffn_done"], 1 + n + 1)
                dve.wait_ge(S["yb_ready"], n + 1)
                dve.scalar_tensor_tensor(yb[:, j, :], banks(4 + j % 4)[0:P, 0:D], scale3[0:P, 7:8], yb[:, j, :],
                                         ALU.mult, ALU.add).then_inc(S["r_ready"], 1)
                dve.wait_ge(S["r_ready"], R + n + 1)
                olink = Links(dve, S["dve_out"], 4 * n - 2 * (j > 0))
                olink(dve.bn_stats(st[:, j, :], yb[:, j, :]))
                apart(dve)
                olink(dve.bn_aggr(mv[:, j, :], st[:, j, :]))
                dve.tensor_scalar(lnt[:, j:j + 1], mv[:, j, 1:2], EPS, None, ALU.add).then_inc(S["var2_ready"], 1)

            def result_norm(i, j):
                n = R * i + j
                dve.wait_ge(S["std2_ready"], n + 1)
                olink = Links(dve, S["dve_out"], 4 * n + (4 if j < R - 1 else 2))
                olink(dve.reciprocal(rstd[:, j:j + 1], lnu[:, j:j + 1]))
                dve.wait_ge(out_in[j], 16 * i + 16)
                dve.wait_ge(S["x1b_ready"], n + 1)
                olink(dve.scalar_tensor_tensor(fin[:, j, :], yb[:, j, :], mv[:, j, 0:1], gam[:, 0, :], ALU.subtract, ALU.mult))
                dve.scalar_tensor_tensor(fin[:, j, :], fin[:, j, :], rstd[:, j:j + 1], x1b[:, j, :],
                                         ALU.mult, ALU.add).then_inc(S["out_ready"], 1)

            def result_round(i):
                for j in range(R):
                    result_sum(i, j)
                    if j:
                        result_norm(i, j - 1)
                result_norm(i, R - 1)

            result_round(0)
            with dve.Fori(1, ROUNDS) as i:
                for at in range(2 * FM):
                    split_hidden(i, at)
                result_round(i)

        @block.tensor
        def _(pe):
            mm = pe.matmul

            def clear(b, n):
                for at in range(0, n, 128):
                    m = min(128, n - at)
                    mm(banks(b)[:, at:at + m], zeros[0:1, :], zeros[0:1, 0:m], start=True, stop=True)

            def add(out, lhs, rhs):
                return mm(out, lhs, rhs, start=False, stop=False, skip_group_check=True)

            def turn(to, src):
                for c in range(KC):
                    ins = pe.transpose(to[:, 128 * c:128 * c + P], src[:, 128 * c:128 * c + 128], ident[0:P, 0:P])
                return ins

            for name, c in (("cmp_used", 1), ("batch_done", NB), ("w2_done", 1), ("y_turned", R), ("gen_mm", 1), ("ffn_done", 1)):
                pe.sem_inc(S[name], c)
            pe.wait_ge(S["cst_in"], 16)
            pe.wait_ge(S["ones_set"], 5)
            clear(1, KC * 129)
            clear(2, KC * 129)
            clear(0, 512)
            clear(3, G - 512)

            def turn_token(i, j):
                n = R * i + j
                pe.wait_ge(S["xn_ready"], n + 1)
                pe.wait_ge(S["xt_ready"], n + 1)
                turn(banks(4), xn[:, j, :]).then_inc(S["turned"], 1)

            def token_round(i, samples=False, last=False):
                for j in range(R):
                    n = R * i + j
                    if j < R - 1:
                        turn_token(i, j + 1)
                    elif not last:
                        turn_token(i + 1, 0)
                    pe.wait_ge(S["xt_ready"], 1 + n + 1)
                    pe.wait_ge(S["h_biased"], n + 1)
                    for c in range(KC):
                        ins = mm(banks(5)[0:P, 0:D], xt[:, j, c, :], w_in[:, c, :],
                                 start=(c == 0), stop=(c == KC - 1))
                    ins.then_inc(S["h_done"], 1)
                    pe.wait_ge(S["kc_ready"], n + back(j))
                    for c in range(KC):
                        ins = mm(banks(6 + j % 2)[0:P, :], xt[:, j, c, :], w_kv[:, c, :], start=(c == 0), stop=(c == KC - 1))
                    ins.then_inc(S["kv_done"], 1)
                    if samples:
                        for s in range(SAMPLES[j]):
                            pe.wait_ge(S["cmp_ready"], sum(SAMPLES) * (i - 1) + sum(SAMPLES[:j]) + s + 1)
                            add(banks(0)[0:1, :], ones16[:, :], cmp[:, s, 0:512])
                            add(banks(3)[0:1, 0:G - 512], ones16[:, :], cmp[:, s, 512:G]).then_inc(S["cmp_used"], 1)

            def head_products(i):
                for j in range(R):
                    pe.wait_ge(S["kvn_ready"], R * i + j + 1)
                    for c in range(KC):
                        add(banks(1)[:, 129 * c:129 * c + 129], kvn[:, j, c, 0:128], kvn[:, j, KC + c, :])
                    add(banks(2)[:, 0:KC * 129], ones[0:P, :],
                        kvn[:, j, KC:2 * KC, :].rearrange("p b f -> p (b f)")).then_inc(S["kv_summed"], 1)

            turn_token(0, 0)
            pe.wait_ge(S["token_in"], 16 * 4)
            pe.wait_ge(S["wkv_ready"], 1)
            token_round(0)
            with pe.Fori(1, 3) as i:
                token_round(i, True)
                head_products(i - 1)
            pe.wait_ge(S["below_ready"], 2)
            for t in range(GT):
                ins = mm(banks(0)[0:P, t:t + 1], below[:, P * t:P * t + P], ones[0:1, 0:1], start=True, stop=True)
            ins.then_inc(S["rows_turned"], 1)
            token_round(3)
            head_products(2)
            pe.wait_ge(S["got_in"], 16 * GT)
            pe.wait_ge(S["start_ready"], 1)
            for t in range(GT):
                at = 128 * (t % 4)
                pe.transpose(banks(3 if t < 4 else 0)[:, at:at + P], got[:, t, :], ident[0:P, 0:P]).then_inc(S["code_turned"], 1)
            token_round(4, last=True)
            pe.wait_ge(S["local_ready"], GD)
            pe.wait_ge(S["xt_ready"], 1 + T)
            pe.wait_ge(S["h_biased"], 1 + T)
            pe.wait_ge(S["kc_ready"], 2 + T)
            for d in range(GD):
                mm(banks(3 + d)[0:1, :], ones16[:, :], oh_l[:, d, 0:512], start=True, stop=True).then_inc(S["row_done"], 1)
            pe.wait_ge(S["hmax_ready"], T + 1)
            mm(banks(0)[0:1, 0:P], hmx[:, T:T + 1], ident[0:P, 0:P], start=True, stop=True).then_inc(S["scale_products"], 1)
            head_products(3)
            pe.wait_ge(S["scale_ready"], 1)
            pe.wait_ge(S["row_kept"], 2)
            mm(banks(3)[:, 0:2], ones[0:1, :], small[0:1, 2:4], start=True, stop=True).then_inc(S["scale_products"], 1)
            for d in range(GD - 1):
                mm(banks(0)[0:1, REST * d:REST * d + REST], ones16[:, :], oh_l[:, d, 512:G], start=True, stop=True)
            mm(banks(4)[0:1, 0:REST], ones16[:, :], oh_l[:, GD - 1, 512:G], start=True, stop=True).then_inc(S["row_done"], 1)
            head_products(4)
            pe.wait_ge(S["row_kept"], GD + 2)
            for t in range(T):
                ins = mm(banks(5)[0:P, t:t + 1], deg_row[:, P * t:P * t + P], ones16[0:1, :], start=True, stop=True)
            ins.then_inc(S["rows_turned"], 1)
            pe.wait_ge(S["deg_ready"], 1)

            def products(n):
                for b, size in enumerate(BATCHES):
                    h = 2 * b // NB
                    if b % (NB // 2) == 0:
                        pe.wait_ge(S["oh_ready"], 2 * n + h + 1)
                    pe.wait_ge(S["batch_out"], NB * n + b + 1)
                    g = sum(BATCHES[:b]) - HALVES[0] * h
                    for s in range(size):
                        ins = mm(banks(4 + b % 4)[:, P * s:P * s + P], oh[h][:, 1, :, g + s], oh[h][:, 0, 0:P, g + s],
                                 start=True, stop=True)
                    ins.then_inc(S["batch_done"], 1)

            def first_step(n, j):
                pe.wait_ge(S["batch_out"], 4 + NB * n + NB)
                pe.wait_ge(S["sum_ready"], n + 1)
                apart(pe)
                for c in range(T):
                    if isinstance(n, int) and n == 0:
                        if c % R == R - 1:
                            pe.wait_ge(S["pool_split"], 1 + c // R + 1)
                        else:
                            pe.wait_ge(S["split_ready"], (R - 1) * (c // R) + c % R + 1)
                    ins = mm(banks(j % 3)[:, :], stage[0:P, j, 128 * c:128 * c + 128].bitcast(F8), u[0][:, c, :],
                             start=(c == 0), stop=(c == T - 1))
                ins.then_inc(S["tile_done"], 1)

            for j in range(R):
                products(j)
                if j == 2:
                    pe.wait_ge(S["kvbd_ready"], KC)
                if j:
                    first_step(j - 1, j - 1)
            with pe.Fori(1, ROUNDS) as i:
                for j in range(R):
                    products(R * i + j)
                    first_step(R * i + j - 1, (j - 1) % R)

            pe.wait_ge(S["batch_out"], 4 + NB * T)
            pe.wait_ge(S["weights_in"], 16 * N_WEIGHTS)
            for c in range(KC):
                ins = mm(banks(5 + 2 * c)[:, 0:D + 1], kv_bd[:, c, :], wq_t[:, c, :], start=True, stop=True)
            ins.then_inc(S["matrix_products"], 1)
            first_step(T - 1, R - 1)
            pe.wait_ge(S["matrices_ready"], KC)
            for m in range(KC):
                for c in range(KC):
                    mm(banks(6)[:, D * m:D * m + D], m1t[:, c, 128 * m:128 * m + 128], w1[:, c, :],
                       start=(c == 0), stop=(c == KC - 1))
            for m in range(KC):
                for c in range(KC):
                    ins = mm(banks(5)[:, m:m + 1], w1[:, c, 128 * m:128 * m + 128], m1t[:, c, D:D + 1],
                             start=(c == 0), stop=(c == KC - 1))
            ins.then_inc(S["matrix_products"], 1)
            pe.wait_ge(S["matrices_ready"], 2 * KC + 1)
            pe.wait_ge(S["sum_ready"], 2 + T)
            pe.wait_ge(S["xt_kept"], R + T)

            def wide(b, lhs, i, c, k):
                for at, n in ((0, 512), (512, R * P - 512)):
                    ins = mm(banks(b, 2)[:, at:at + n], lhs, xt_all[:, c, bass.ds(R * P * i + at, n)],
                             start=(c == 0), stop=(c == k - 1))
                return ins

            def tile_bank(sem, i, j):
                last = 1 if j == 0 else 4 if j == 4 else 5
                pe.wait_ge(sem, R + R * i + j - last + 1)

            with pe.Fori(0, ROUNDS) as i:
                for m in range(KC):
                    pe.wait_ge(S["gelu_done"], KC * i + m + 1)
                    for c in range(KC):
                        ins = wide(2 * m, g_sb[:, c, 128 * m:128 * m + 128], i, c, KC)
                    ins.then_inc(S["mix_done"], 1)
                pe.wait_ge(S["gelu_done"], KC + KC * i + KC)
                for j in range(R):
                    tile_bank(S["x1_mixed"], i, j)
                    for c in range(KC):
                        ins = mm(banks(4 + j % 4)[0:P, 0:D], hb[:, c, P * j:P * j + P], w2[:, c, :],
                                 start=(c == 0), stop=(c == KC - 1))
                    ins.then_inc(S["w2_done"], 1)

            pe.wait_ge(S["flag_part"], 1)
            mm(banks(3)[0:1, 0:2], ones[0:P, 0:1], fl[:, :], start=True, stop=True).then_inc(S["flag_sum"], 1)

            def diffuse(k, loads, i, j, src):
                n = T * k + R * i + j
                pe.wait_ge(slot_in[j], 16 * (loads + i + 1))
                pe.wait_ge(S["sum_ready"], n + 1)
                for c in range(T):
                    if j == 0 and c in (0, T - 2, T - 1):
                        pe.wait_ge(S["split_ready"], T * k - ROUNDS + (T - 2 if c == 0 else c + 1))
                    if c in (0, T - 2, T - 1):
                        apart(pe)
                    ins = mm(banks(j % 3)[:, :], stage[0:P, j, 128 * c:128 * c + 128].bitcast(F8), u[src][:, c, :],
                             start=(c == 0), stop=(c == T - 1))
                ins.then_inc(S["tile_done"], 1)

            with pe.Fori(0, (STEPS - 2) // 2) as it:
                for par in range(2):
                    with pe.Fori(0, ROUNDS) as i:
                        for j in range(R):
                            diffuse(1 + par + 2 * it, ROUNDS * (2 * it + par), i, j, 1 - par)

            pe.wait_ge(S["flag_ready"], 1)
            bad = pe.value_load(small_i[0:1, 0:1], min_val=0, max_val=1)
            with pe.If(bad == 1):
                with pe.Fori(0, STEPS) as k:
                    with pe.Fori(0, EP) as e:
                        n = EP * k + e
                        pe.wait_ge(S["gen_rows"], 16 * n + 16)
                        pe.wait_ge(S["gen_onehot"], n + 1)
                        for b in range(T // R):
                            pe.wait_ge(S["gen_added"], R * n + b + 1)
                            for s in range(R):
                                t = R * b + s
                                ins = mm(banks(s)[0:P, 0:D + 1], oh_g[:, P * t:P * t + P], rows, start=True, stop=True)
                            ins.then_inc(S["gen_batch"], 1)
                        pe.wait_ge(S["gen_batch"], R * n + R)
                        pe.sem_inc(S["gen_mm"], 1)
                pe.wait_ge(S["gen_end"], 1)
            with pe.Else():
                pass

            def last_step(i, j, main):
                n = R * i + j
                if main:
                    diffuse(STEPS - 1, (STEPS - 2) * ROUNDS, i, j, 1)
                if some(n - 1) and lies(n - 1):
                    pe.wait_ge(S["acc_in"], n)
                    after(pe, S["at_ready"], n - 1)
                    turn(banks(5), at_in[:, (j - 1) % R, :]).then_inc(S["acc_turned"], 1)
                if some(n - 2) and lies(n - 2):
                    pe.wait_ge(S["at_ready"], n - 1)
                    after(pe, S["x1_ready"], n - 2)
                    for c in range(KC):
                        ins = mm(banks(6)[0:P, 0:D], at_t[:, (j - 2) % R, c, :], w_out[:, c, :], start=(c == 0), stop=(c == KC - 1))
                    ins.then_inc(S["out_done"], 1)
                if some(n - 3) and lies(n - 3):
                    pe.wait_ge(S["y_ready"], n - 2)
                    after(pe, S["yt_ready"], n - 3)
                    turn(banks(7), y_in[:, (j - 3) % R, :]).then_inc(S["y_turned"], 1)

            pe.wait_ge(S["x1_mixed"], R + T)
            for j in range(R):
                last_step(0, j, True)
            with pe.Fori(1, ROUNDS) as i:
                for j in range(R):
                    last_step(i, j, True)
            for j in range(LAG):
                last_step(ROUNDS, j, False)

            pe.wait_ge(S["route_row"], 1)
            for c in range(KC):
                ins = mm(banks(4)[0:1, 0:NX], meant[:, c:c + 1], wr[:, c, :], start=(c == 0), stop=(c == KC - 1))
            ins.then_inc(S["route_products"], 1)
            pe.wait_ge(S["route_row"], 2)
            mm(banks(4)[:, 16:18], ones[0:1, :], small[0:1, 56:58], start=True, stop=True).then_inc(S["route_products"], 1)

            def spread_scales(at, n, times):
                pe.wait_ge(S["maxima_ready"], 2 * times - 1)
                pe.transpose(banks(5)[0:n, 0:128], biggest[:, at:at + n], ident).then_inc(S["scales_turned"], 1)
                pe.wait_ge(S["maxima_ready"], 2 * times)
                mm(banks(5)[:, 128:128 + 2 * n], ones[0:n, :], scale_row[0:n, 2:2 + 2 * n],
                   start=True, stop=True).then_inc(S["scales_turned"], 1)

            spread_scales(0, 2, 1)

            pe.wait_ge(S["yt_ready"], T)
            pe.wait_ge(S["sum_ready"], 2 + STEPS * T)

            def expert_round(i, first=False):
                for e in range(2):
                    if first:
                        pe.wait_ge(S["halves_high"], e + 1)
                    for m in range(FM):
                        at = FM * e + m
                        pe.wait_ge(S["hid_ready"], 2 * FM * i + at + 1)
                        b, to = 2 * (at % 2), slice(128 * m, 128 * m + 128)
                        terms = [(w, y, c) for w, y in ((w1_hi, y_hi), (w1_hi, y_lo), (w1_lo, y_hi)) for c in range(KC)]
                        for k, (w, y, c) in enumerate(terms):
                            if first and m == 0 and k == 2 * KC:
                                pe.wait_ge(S["halves_low"], e + 1)
                            for col, size in ((0, 512), (512, R * P - 512)):
                                ins = mm(banks(b, 2)[:, col:col + size], w[:, e, c, to], y[:, c, bass.ds(R * P * i + col, size)],
                                         start=(k == 0), stop=(k == 3 * KC - 1))
                        ins.then_inc(S["hid_done"], 1)
                        if first and at == 2:
                            spread_scales(2, 1, 2)
                for j in range(R):
                    tile_bank(S["r_ready"], i, j)
                    to = slice(P * j, P * j + P)
                    terms = [(h, w, e, m) for h, ws in ((hid_hi, (w2_hi, w2_lo)), (hid_lo, (w2_hi,)))
                             for e in range(2) for m in range(FM) for w in ws]
                    for k, (h, w, e, m) in enumerate(terms):
                        if j == 0 and h is hid_hi and w is w2_hi:
                            if first and m == 0:
                                pe.wait_ge(S["halves_low"], 2 + e + 1)
                            pe.wait_ge(S["hid_high"], 2 * FM * i + FM * e + m + 1)
                        if j == 0 and h is hid_lo:
                            pe.wait_ge(S["hid_split"], 2 + 2 * FM * i + FM * e + m + 1)
                        ins = mm(banks(4 + j % 4)[0:P, 0:D], h[:, e, m, to], w[:, e, m, :],
                                 start=(k == 0), stop=(k == len(terms) - 1))
                    ins.then_inc(S["ffn_done"], 1)

            expert_round(0, True)
            with pe.Fori(1, ROUNDS) as i:
                expert_round(i)


def kernel(**inputs):
    import concourse.bacc as _bacc
    from concourse.bass_utils import run_bass_kernel_spmd as _run

    x = {k: np.ascontiguousarray(v) for k, v in inputs.items()}
    m = "L0_mix_"
    heads = x[m + "w_qkv"].reshape(D, HEADS, 3, HD)
    bias = x[m + "b_qkv"].reshape(HEADS, 3, HD)
    laid = {
        "x": x["x"], "src": x["src"], "dst": x["dst"], "const": constants(),
        "w_in_t": x["L0_gnn_W_in"].T, "b_in": x["L0_gnn_b_in"],
        "w_out_t": x["L0_gnn_W_out"].T, "b_out": x["L0_gnn_b_out"],
        "w_q_t": np.concatenate([heads[:, :, 0].reshape(D, D).T, bias[:, 0].reshape(D, 1)], axis=1),
        "w_kv": heads[:, :, 1:].transpose(0, 2, 1, 3).reshape(D, 2 * D),
        "b_kv": bias[:, 1:].transpose(1, 0, 2).reshape(2 * D),
        "kln": np.stack([np.tile(x[m + "kln_g"], 4), np.tile(x[m + "kln_b"], 4)], axis=1),
        "vln_g": np.tile(x[m + "vln_g"], HEADS), "vln_b": np.tile(x[m + "vln_b"], HEADS),
        "w1": x[m + "w1"], "b1": x[m + "b1"].reshape(KC, 128).T, "w2": x[m + "w2"], "b2": x[m + "b2"],
        "wr": x["L0_ffn_Wr"], "br": x["L0_ffn_br"],
        "e_w1": x["L0_ffn_W1"].reshape(NX, KC, 128, FF),
        "e_b1": x["L0_ffn_b1"].reshape(NX, FM, 128).transpose(0, 2, 1),
        "e_w2": x["L0_ffn_W2"].reshape(NX, FM, 128, D), "e_b2": x["L0_ffn_b2"],
        "gamma": x["L0_ffn_gamma"], "beta": x["L0_ffn_beta"],
    }
    nc = _bacc.Bacc("TRN2", target_bir_lowering=False, num_devices=1)
    arrays, a = {}, {}
    for name, v in laid.items():
        arrays["in_" + name] = np.ascontiguousarray(v)
        a[name] = nc.dram_tensor("in_" + name, v.shape, mybir.dt.from_np(v.dtype), kind="ExternalInput").ap()
    out = nc.dram_tensor("out_0", (N, D), F32, kind="ExternalOutput").ap()
    gps_kernel(nc, a, out)
    return _run(nc, [arrays], core_ids=[0]).results[0]["out_0"]
```
